# Optimizing a Trainium2 kernel written in Bass

```python
import numpy as np
import jax
import jax.numpy as jnp

def _softmax(x, axis=-1):
    return jax.nn.softmax(x, axis=axis)

def _gelu(x):
    return jax.nn.gelu(x, approximate=True)

def _silu(x):
    return jax.nn.silu(x)

def _sigmoid(x):
    return jax.nn.sigmoid(x)

def _layernorm(x, axis=-1, eps=1e-05):
    m = jnp.mean(x, axis=axis, keepdims=True)
    v = jnp.var(x, axis=axis, keepdims=True)
    return (x - m) / jnp.sqrt(v + eps)

def _scatter_add(tgt, idx, src, axis=0):
    return tgt.at[idx].add(src)

def _segment_sum(src, seg, n):
    return jax.ops.segment_sum(src, seg, n)
kernel_name = 'mk_cond_resid_d2_seqx_r2_f8fc12'

def setup_inputs(seed: int=0):
    np.random.seed(seed)
    _w = jnp.asarray

    def _rec_inputs():
        import jax
        import jax.numpy as jnp
        _rk = jax.random.key(seed)
        x = -0.0003929 + 0.9999 * jax.random.normal(jax.random.fold_in(_rk, 1), (4, 1024, 512), jnp.float32)
        _lenS = 1024 - jax.random.randint(jax.random.fold_in(_rk, 7), (4,), 0, max(1, 1024 // 4) + 1, jnp.int32)
        _lenS2 = 1024 - jax.random.randint(jax.random.fold_in(_rk, 8), (4,), 0, max(1, 1024 // 4) + 1, jnp.int32)
        cond_2048 = 0.00782532 + 1.00527 * jax.random.normal(jax.random.fold_in(_rk, 11), (4, 1024), jnp.float32)
        return (x, cond_2048)
    x, cond_2048 = _rec_inputs()

    def _L0_cond_setup():
        import jax, jax.numpy as jnp
        import numpy as np
        B, S, D_MODEL, D_INNER, D_STATE = (4, 2048, 512, 1024, 16)
        key = jax.random.key(seed)
        ks = jax.random.split(key, 12)
        inp = {'x': jax.random.normal(ks[0], (B, S, D_MODEL), jnp.float32), 't_emb': jax.random.normal(ks[1], (B, D_INNER), jnp.float32), 'W_in': jax.random.normal(ks[2], (2 * D_INNER, D_MODEL), jnp.float32) * 0.02, 'W_conv': jax.random.normal(ks[3], (D_INNER, 1, 4), jnp.float32) * 0.1, 'b_conv': jnp.zeros((D_INNER,), jnp.float32), 'ln_g': jnp.ones((D_INNER,), jnp.float32), 'ln_b': jnp.zeros((D_INNER,), jnp.float32), 'W_xproj': jax.random.normal(ks[4], (3 * D_STATE, D_INNER), jnp.float32) * 0.02, 'W_dt': jax.random.normal(ks[5], (D_STATE, D_STATE), jnp.float32) * 0.01, 'b_dt': jax.random.uniform(ks[6], (D_STATE,), jnp.float32) * 0.1, 'A_log': jax.random.normal(ks[7], (D_STATE,), jnp.float32) * 0.1, 'D': jnp.ones((D_INNER,), jnp.float32) * 0.1, 'W_out': jax.random.normal(ks[8], (D_MODEL, D_INNER), jnp.float32) * 0.02}
        return inp
    _L0_cond_all = _L0_cond_setup()
    _L0_cond_in = {k: v for k, v in _L0_cond_all.items() if k in ('W_in', 'W_conv', 'b_conv', 'ln_g', 'ln_b', 'W_xproj', 'W_dt', 'b_dt', 'A_log', 'D', 'W_out')}
    del _L0_cond_all

    def _L1_cond_setup():
        import jax, jax.numpy as jnp
        import numpy as np
        EPS_IN = 1e-05
        EPS_DM = 1e-08

        def _dcoef(weight, style):
            return jax.lax.rsqrt(jnp.einsum('oi,bi->bo', jnp.square(weight), jnp.square(style)) + EPS_DM)
        key = jax.random.key(seed)
        ks = jax.random.split(key, 7)
        B, S, H = (8, 512, 512)
        lim = 1.0 / np.sqrt(H)
        u = lambda k, shp: jax.random.uniform(k, shp, jnp.float32, -lim, lim)
        return {'x': jax.random.normal(ks[0], (B, S, H), jnp.float32), 'q_weight': u(ks[1], (H, H)), 'k_weight': u(ks[2], (H, H)), 'v_weight': u(ks[3], (H, H)), 'w_weight': u(ks[4], (H, H)), 'u_weight': u(ks[5], (H, H)), 'styles': jax.random.normal(ks[6], (B, 2 * H), jnp.float32) * 0.5 + 1.0, 'num_heads': 16}
    _L1_cond_all = _L1_cond_setup()
    _L1_cond_in = {k: v for k, v in _L1_cond_all.items() if k in ('q_weight', 'k_weight', 'v_weight', 'w_weight', 'u_weight')}
    del _L1_cond_all
    return {'x': x, 'cond_2048': cond_2048, 'L0_cond_W_in': _L0_cond_in['W_in'], 'L0_cond_W_conv': _L0_cond_in['W_conv'], 'L0_cond_b_conv': _L0_cond_in['b_conv'], 'L0_cond_ln_g': _L0_cond_in['ln_g'], 'L0_cond_ln_b': _L0_cond_in['ln_b'], 'L0_cond_W_xproj': _L0_cond_in['W_xproj'], 'L0_cond_W_dt': _L0_cond_in['W_dt'], 'L0_cond_b_dt': _L0_cond_in['b_dt'], 'L0_cond_A_log': _L0_cond_in['A_log'], 'L0_cond_D': _L0_cond_in['D'], 'L0_cond_W_out': _L0_cond_in['W_out'], 'L1_cond_q_weight': _L1_cond_in['q_weight'], 'L1_cond_k_weight': _L1_cond_in['k_weight'], 'L1_cond_v_weight': _L1_cond_in['v_weight'], 'L1_cond_w_weight': _L1_cond_in['w_weight'], 'L1_cond_u_weight': _L1_cond_in['u_weight']}

def reference(x, cond_2048, L0_cond_W_in, L0_cond_W_conv, L0_cond_b_conv, L0_cond_ln_g, L0_cond_ln_b, L0_cond_W_xproj, L0_cond_W_dt, L0_cond_b_dt, L0_cond_A_log, L0_cond_D, L0_cond_W_out, L1_cond_q_weight, L1_cond_k_weight, L1_cond_v_weight, L1_cond_w_weight, L1_cond_u_weight):
    import jax
    import jax.numpy as jnp

    def _L0_cond_ref(x, t_emb, W_in, W_conv, b_conv, ln_g, ln_b, W_xproj, W_dt, b_dt, A_log, D, W_out):
        import jax, jax.numpy as jnp
        import numpy as np
        B, S, D_MODEL, D_INNER, D_STATE = (4, 2048, 512, 1024, 16)
        d_inner = W_conv.shape[0]
        d_state = A_log.shape[0]
        xr, gate = jnp.split(x @ W_in.T, 2, axis=-1)
        xr = xr + t_emb[:, None, :]
        xc = jax.lax.conv_general_dilated(xr.transpose(0, 2, 1), W_conv, (1,), [(3, 0)], feature_group_count=d_inner, dimension_numbers=('NCH', 'OIH', 'NCH')) + b_conv[None, :, None]
        xc = jax.nn.silu(xc).transpose(0, 2, 1)
        mu = xc.mean(-1, keepdims=True)
        var = xc.var(-1, keepdims=True)
        xn = (xc - mu) / jnp.sqrt(var + 1e-05) * ln_g + ln_b
        Bm, Cm, dt = jnp.split(xn @ W_xproj.T, 3, axis=-1)
        dt = jnp.tanh(dt @ W_dt.T + b_dt) * 0.01
        A = -jnp.tanh(A_log)
        Ad = 1.0 + dt * A
        Bd = Bm * jnp.minimum(jnp.linalg.norm(xn, axis=-1, keepdims=True), 1.0)
        h0 = jnp.zeros((xn.shape[0], d_state, d_inner), xn.dtype)

        def step(h, inputs):
            ad, bd, xt, ct = inputs
            h = jnp.clip(h * ad[:, :, None] + bd[:, :, None] * xt[:, None, :], -10.0, 10.0)
            yt = jnp.einsum('bd,bdh->bh', ct, h)
            return (h, yt)
        _, ys = jax.lax.scan(step, h0, (Ad.transpose(1, 0, 2), Bd.transpose(1, 0, 2), xn.transpose(1, 0, 2), Cm.transpose(1, 0, 2)))
        y = ys.transpose(1, 0, 2) + D * xn
        return y * jax.nn.silu(gate) @ W_out.T

    def _L1_cond_ref(x, q_weight, k_weight, v_weight, w_weight, u_weight, styles, num_heads):
        import jax, jax.numpy as jnp
        import numpy as np
        EPS_IN = 1e-05
        EPS_DM = 1e-08

        def _dcoef(weight, style):
            return jax.lax.rsqrt(jnp.einsum('oi,bi->bo', jnp.square(weight), jnp.square(style)) + EPS_DM)
        B, S, H = x.shape
        nh = num_heads
        d = H // nh
        scale = jnp.asarray(d, x.dtype) ** (-0.5)
        s1 = styles[:, :H]
        s2 = styles[:, H:]
        x = x * s1[:, None, :]
        mu = jnp.mean(x, axis=-1, keepdims=True)
        var = jnp.mean(jnp.square(x - mu), axis=-1, keepdims=True)
        x = (x - mu) * jax.lax.rsqrt(var + EPS_IN)
        q_dc = _dcoef(q_weight, s1)
        k_dc = _dcoef(k_weight, s1)
        v_dc = _dcoef(v_weight, s1)
        w_dc = _dcoef(w_weight, s2)
        u_dc = _dcoef(u_weight, s2)

        def heads(t):
            return t.reshape(B, S, nh, d).transpose(0, 2, 1, 3)
        q = heads(jnp.einsum('bsh,oh->bso', x, q_weight) * q_dc[:, None, :])
        k = heads(jnp.einsum('bsh,oh->bso', x, k_weight) * k_dc[:, None, :])
        v_flat = jnp.einsum('bsh,oh->bso', x, v_weight) * v_dc[:, None, :] * s2[:, None, :]
        skip = v_flat
        v = heads(v_flat)
        attn = jnp.einsum('bhqd,bhkd->bhqk', q, k) * scale
        attn = jax.nn.softmax(attn, axis=-1)
        out = jnp.einsum('bhqk,bhkd->bhqd', attn, v).transpose(0, 2, 1, 3).reshape(B, S, H)
        out = jnp.einsum('bsh,oh->bso', out, w_weight) * w_dc[:, None, :]
        skip = jnp.einsum('bsh,oh->bso', skip, u_weight) * u_dc[:, None, :]
        return out + skip
    x = x + _L0_cond_ref(x, cond_2048, L0_cond_W_in, L0_cond_W_conv, L0_cond_b_conv, L0_cond_ln_g, L0_cond_ln_b, L0_cond_W_xproj, L0_cond_W_dt, L0_cond_b_dt, L0_cond_A_log, L0_cond_D, L0_cond_W_out)
    x = x + _L1_cond_ref(x, L1_cond_q_weight, L1_cond_k_weight, L1_cond_v_weight, L1_cond_w_weight, L1_cond_u_weight, cond_2048, 16)
    return x

_drawn_inputs = setup_inputs


def setup_inputs(seed=0):
    import zlib

    import numpy as np

    out = dict(_drawn_inputs(seed))
    spreads = {'L0_cond_b_conv': (0.0, 0.1),
     'L0_cond_ln_g': (1.0, 0.2),
     'L0_cond_ln_b': (0.0, 0.1),
     'L0_cond_D': (0.10000000149011612, 0.6)}
    factors = {'L0_cond_W_dt': 8.0, 'L0_cond_b_dt': 8.0, 'L0_cond_A_log': 8.0}
    for name, (base, spread) in spreads.items():
        noise = np.random.default_rng([zlib.crc32(name.encode()), seed]).standard_normal(out[name].shape)
        drawn = base * np.exp(spread * noise) if base else spread * noise
        out[name] = jnp.asarray(drawn.astype(out[name].dtype))
    for name, factor in factors.items():
        out[name] = (out[name] * factor).astype(out[name].dtype)
    return out
```

```python
from contextlib import ExitStack

import numpy as np

import concourse.bass as bass
from concourse import mybir

f32 = mybir.dt.float32
f32r = mybir.dt.float32r
bf16 = mybir.dt.bfloat16
ALU = mybir.AluOpType
ACT = mybir.ActivationFunctionType

P = 128
BATCH, SEQ, MODEL, INNER, STATES, TAPS = 4, 1024, 512, 1024, 16, 4
HEADS = 16
HD = MODEL // HEADS
NM, NQ, NK, NH = INNER // P, SEQ // P, MODEL // P, SEQ // 512
HALF = INNER // 2

START = 1


def start_counts(engine, semaphores):
    for s in semaphores:
        engine.sem_inc(s, START)


def pre_phase(nc, I, Xp, Xn, Bp, Ad, Cm):
    with ExitStack() as ctx:
        sb = lambda n, s, d=f32: ctx.enter_context(nc.sbuf_tensor("a_" + n, s, d))
        pb = lambda n, s, d=f32: ctx.enter_context(nc.psum_tensor("a_" + n, s, d))
        sems = []
        def sem(n):
            sems.append(ctx.enter_context(nc.semaphore("a_" + n)))
            return sems[-1]
        w_in = sb("w_in", [P, NK, INNER]); x_t = sb("x_t", [P, NK, SEQ])
        temb = sb("temb", [P, NM]); w_conv = sb("w_conv", [P, NM, TAPS]); b_conv = sb("b_conv", [P, NM])
        ln_g = sb("ln_g", [P, INNER]); ln_b = sb("ln_b", [P, INNER])
        w_xp = sb("w_xp", [P, NM, 3 * STATES]); w_dt = sb("w_dt", [STATES, 64])
        b_dt = sb("b_dt", [STATES, 1]); a_log = sb("a_log", [STATES, 1]); neg_a = sb("neg_a", [STATES, 1])
        ident = sb("ident", [P, P]); idle = sb("idle", [P, 1])
        padded = sb("padded", [P, 2, TAPS - 1 + SEQ]); acc = sb("acc", [P, 2, SEQ]); xc_t = sb("xc_t", [P, NM, SEQ])
        stats = sb("stats", [P, 2, 6]); mv = sb("mv", [P, 2]); var_eps = sb("var_eps", [P, 1]); std = sb("std", [P, 1])
        rstd = sb("rstd", [P, 2]); nmr = sb("nmr", [P, 2])
        xn0 = sb("xn0", [P, 2, INNER]); xg = sb("xg", [P, 2, INNER]); xn = sb("xn", [P, 4, INNER])
        x1 = sb("x1", [P, 4, INNER], bf16); r1 = sb("r1", [P, 2, INNER]); x2 = sb("x2", [P, 2, INNER], bf16); x3 = sb("x3", [P, 2, INNER], bf16)
        square = sb("square", [P, INNER]); sumsq = sb("sumsq", [P, NQ])
        xn_t = sb("xn_t", [P, 2, NM, P]); xproj = sb("xproj", [P, NQ, 3 * STATES])
        ssm = sb("ssm", [P, NQ]); root = sb("root", [P, NQ]); geq = sb("geq", [P, NQ]); nrm = sb("nrm", [P, NQ])
        bd = sb("bd", [P, NQ, STATES]); b1 = sb("b1", [P, NQ, STATES], bf16); br1 = sb("br1", [P, NQ, STATES]); b2 = sb("b2", [P, NQ, STATES], bf16); b3 = sb("b3", [P, NQ, STATES], bf16)
        c_t = sb("c_t", [STATES, SEQ]); dt_t = sb("dt_t", [STATES, SEQ]); th = sb("th", [STATES, SEQ]); ad = sb("ad", [STATES, SEQ])
        pa = [pb(f"pa{i}", [P, 1024]) for i in range(2)]
        pt = pb("pt", [P, 1024]); px = pb("px", [P, 512])
        consts = sem("consts"); const_c = sem("const_c"); x_in = sem("x_in"); s_xr = sem("s_xr"); s_ev = sem("s_ev"); s_tap = sem("s_tap"); s_conv = sem("s_conv"); s_xc = sem("s_xc")
        s_tp = sem("s_tp"); s_dv = sem("s_dv"); s_sd = sem("s_sd"); s_nmr = sem("s_nmr"); s_xn0 = sem("s_xn0"); s_xg = sem("s_xg"); s_xn = sem("s_xn")
        s_x1 = sem("s_x1"); s_ss = sem("s_ss"); s_r1 = sem("s_r1"); s_x2 = sem("s_x2"); s_x3 = sem("s_x3"); s_tb = sem("s_tb"); s_xnt = sem("s_xnt"); s_xp = sem("s_xp"); s_xe = sem("s_xe")
        o_x1 = [sem(f"o_x1{i}") for i in range(4)]; o_xn = [sem(f"o_xn{i}") for i in range(4)]
        o_x2 = [sem(f"o_x2{i}") for i in range(2)]; o_x3 = [sem(f"o_x3{i}") for i in range(2)]
        s_t3 = sem("s_t3"); s_c3 = sem("s_c3"); s_mm3 = sem("s_mm3"); s_th = sem("s_th"); s_ad = sem("s_ad"); s_rt = sem("s_rt"); s_v3 = sem("s_v3"); s_b1 = sem("s_b1"); o_3 = sem("o_3")

        with nc.Block() as block:
            @block.sync
            def _(sp):
                start_counts(sp, sems)
                for dst, src in ((w_in[:], I["w_in_t"][:, 0:INNER].rearrange("(k p) n -> p k n", p=P)),
                                 (w_conv[:], I["w_conv"].rearrange("(m p) o j -> p m (o j)", p=P)),
                                 (b_conv[:], I["b_conv"].rearrange("(m p) -> p m", p=P)),
                                 (ln_g[:], I["ln_g"].rearrange("(o n) -> o n", o=1).to_broadcast([P, INNER])),
                                 (ln_b[:], I["ln_b"].rearrange("(o n) -> o n", o=1).to_broadcast([P, INNER])),
                                 (w_xp[:], I["w_xproj_t"].rearrange("(m p) n -> p m n", p=P)),
                                 (w_dt[:], I["w_dt_t"]), (b_dt[:], I["b_dt"].rearrange("(p o) -> p o", o=1)), (a_log[:], I["a_log"].rearrange("(p o) -> p o", o=1)),
                                 (ident[:], I["ident"])):
                    sp.dma_start(dst, src, allow_slow_non_contiguous=True).then_inc(consts, 16)
                sp.wait_ge(consts, START + 160)
            @block.vector
            def _(dve):
                nc.vector.memset(padded[:, :, 0:TAPS - 1], 0.0)
                dve.wait_ge(s_th, START + 1)
                nc.vector.tensor_scalar(out=neg_a[:], in0=neg_a[:], scalar1=-0.01, scalar2=None, op0=ALU.mult).then_inc(const_c, 1)
            @block.scalar
            def _(act):
                act.wait_ge(consts, START + 160)
                nc.scalar.activation(neg_a[:], a_log[:], ACT.Tanh).then_inc(s_th, 1)

        with nc.Block() as block:
            @block.sync
            def _(sp):
                with sp.Fori(0, BATCH) as b:
                    sp.wait_ge(s_xr, START + b * NM)
                    sp.wait_ge(s_ev, START + b * NM)
                    sp.dma_start(x_t[:], I["x_t"][bass.ds(b, 1)].rearrange("o (k p) t -> p (o k) t", p=P)).then_inc(x_in, 16)
                    sp.dma_start(temb[:], I["t_emb"][bass.ds(b, 1)].rearrange("o (m p) -> p (o m)", p=P), allow_slow_non_contiguous=True).then_inc(x_in, 16)
                    xp_b = Xp.rearrange("(i h b) (t c) -> b i t h c", i=3, h=2, c=HALF)[bass.ds(b, 1)].rearrange("o i t h c -> i (o t) h c")
                    def parts(s):
                        q = s - 1
                        if 0 <= q < NQ:
                            sp.wait_ge(s_xn, START + b * NQ + q + 1)
                            sp.wait_ge(s_x1, START + b * NQ + q + 1)
                            sp.dma_start(Xn[bass.ds(b, 1)].rearrange("o t c -> (o t) c")[q * P:(q + 1) * P, :], xn[:, q % 4, :]).then_inc(o_xn[q % 4], 16)
                            sp.dma_start(xp_b[0][q * P:(q + 1) * P], x1[:, q % 4, :].rearrange("p (h c) -> p h c", h=2)).then_inc(o_x1[q % 4], 16)
                        q = s - 2
                        if 0 <= q < NQ:
                            sp.wait_ge(s_x2, START + b * NQ + q + 1)
                            sp.dma_start(xp_b[1][q * P:(q + 1) * P], x2[:, q % 2, :].rearrange("p (h c) -> p h c", h=2)).then_inc(o_x2[q % 2], 16)
                            sp.wait_ge(s_x3, START + b * NQ + q + 1)
                            sp.dma_start(xp_b[2][q * P:(q + 1) * P], x3[:, q % 2, :].rearrange("p (h c) -> p h c", h=2)).then_inc(o_x3[q % 2], 16)
                    for s in range(NQ + 2):
                        parts(s)
                    bp = Bp[:, bass.ds(b, 1)].rearrange("i o (q p) d -> i p (o q) d", p=P)
                    sp.wait_ge(s_b1, START + b * 3 + 3)
                    for j, t in enumerate((b1, b2, b3)):
                        sp.dma_start(bp[j], t[:]).then_inc(o_3, 16)
                    sp.wait_ge(s_c3, START + b * 2 + 2)
                    sp.dma_start(Cm[bass.ds(b * STATES, STATES), :], c_t[:]).then_inc(o_3, 16)
                    sp.wait_ge(s_ad, START + b + 1)
                    sp.dma_start(Ad[bass.ds(b * STATES, STATES), :], ad[:]).then_inc(o_3, 16)
                sp.wait_ge(o_3, START + 80 * BATCH)
                for t in o_x1 + o_xn:
                    sp.wait_ge(t, START + 32 * BATCH)
                for t in o_x2 + o_x3:
                    sp.wait_ge(t, START + 64 * BATCH)
            @block.tensor
            def _(pe):
                with pe.Fori(0, BATCH) as b:
                    pe.wait_ge(x_in, START + b * 32 + 32)
                    for m in range(NM):
                        if m < 2:
                            pe.wait_ge(s_c3, START + b * 2)
                            pe.wait_ge(s_th, START + b * 2 + 1)
                        else:
                            pe.wait_ge(s_ev, START + b * NM + m - 1)
                        for h in range(NH):
                            for k in range(NK):
                                mm = nc.tensor.matmul(pa[m % 2][:, h * 512:h * 512 + 512], w_in[:, k, m * P:(m + 1) * P], x_t[:, k, h * 512:h * 512 + 512], start=(k == 0), stop=(k == NK - 1))
                        mm.then_inc(s_xr, 1)
                    pe.wait_ge(s_xc, START + b * NM + NM)
                    for s in range(NQ + 3):
                        if s < NQ:
                            if s >= 2:
                                pe.wait_ge(s_xn0, START + b * NQ + s - 1)
                            for m in range(NM):
                                mm = nc.tensor.transpose(pa[s % 2][:, m * P:(m + 1) * P], xc_t[:, m, s * P:(s + 1) * P], ident[:])
                            mm.then_inc(s_tp, 1)
                        q = s - 2
                        if 0 <= q < NQ:
                            pe.wait_ge(s_xn, START + b * NQ + q + 1)
                            if q >= 1:
                                pe.wait_ge(s_xnt, START + b * NQ + q)
                            for m in range(NM):
                                mm = nc.tensor.transpose(pt[:, m * P:(m + 1) * P], xn[:, q % 4, m * P:(m + 1) * P], ident[:])
                            mm.then_inc(s_tb, 1)
                        q = s - 3
                        if 0 <= q < NQ:
                            pe.wait_ge(s_xnt, START + b * NQ + q + 1)
                            if q >= 1:
                                pe.wait_ge(s_xe, START + b * NQ + q)
                            for m in range(NM):
                                mm = nc.tensor.matmul(px[:, 0:3 * STATES], xn_t[:, q % 2, m, :], w_xp[:, m, :], start=(m == 0), stop=(m == NM - 1))
                            mm.then_inc(s_xp, 1)
                    pe.wait_ge(s_xe, START + b * NQ + NQ)
                    for j in range(2):
                        for q in range(NQ):
                            mm = nc.tensor.transpose(pa[j][0:STATES, q * P:(q + 1) * P], xproj[:, q, (j + 1) * STATES:(j + 2) * STATES], ident[:])
                        mm.then_inc(s_t3, 1)
                    pe.wait_ge(s_c3, START + b * 2 + 2)
                    for h in range(NH):
                        mm = nc.tensor.matmul(pt[0:64, h * 512:h * 512 + 512], w_dt[:], dt_t[:, h * 512:h * 512 + 512], start=True, stop=True)
                    mm.then_inc(s_mm3, 1)
            @block.scalar
            def _(act):
                with act.Fori(0, BATCH) as b:
                    act.wait_ge(x_in, START + b * 32 + 32)
                    for m in range(NM + 1):
                        if m < NM:
                            act.wait_ge(s_xr, START + b * NM + m + 1)
                            act.wait_ge(s_conv, START + b * (3 * NM) + (3 * (m - 1) if m >= 2 else 0))
                            nc.scalar.activation(padded[:, m % 2, TAPS - 1:], pa[m % 2][:], ACT.Identity, bias=temb[:, m:m + 1]).then_inc(s_ev, 1)
                            act.wait_ge(s_ev, START + b * NM + m + 1)
                            if m >= 2:
                                act.wait_ge(s_xc, START + b * NM + m - 1)
                            nc.scalar.activation(acc[:, m % 2, :], padded[:, m % 2, TAPS - 1:], ACT.Identity, bias=b_conv[:, m:m + 1], scale=w_conv[:, m, TAPS - 1:TAPS]).then_inc(s_tap, 1)
                        if m >= 1:
                            act.wait_ge(s_conv, START + b * (3 * NM) + 3 * m)
                            nc.scalar.activation(xc_t[:, m - 1, :], acc[:, (m - 1) % 2, :], ACT.Silu).then_inc(s_xc, 1)
                    for s in range(NQ + 4):
                        if s < NQ:
                            act.wait_ge(s_dv, START + b * (4 * NQ) + 4 * s + 4)
                            if s >= 1:
                                act.wait_ge(s_nmr, START + b * (2 * NQ) + 2 * s)
                            nc.scalar.activation(std[:], var_eps[:], ACT.Sqrt).then_inc(s_sd, 1)
                            act.wait_ge(s_nmr, START + b * (2 * NQ) + 2 * s + 2)
                            if s >= 2:
                                act.wait_ge(s_xg, START + b * NQ + s - 1)
                            nc.scalar.activation(xn0[:, s % 2, :], pa[s % 2][:], ACT.Identity, bias=nmr[:, s % 2:s % 2 + 1], scale=rstd[:, s % 2:s % 2 + 1]).then_inc(s_xn0, 1)
                        q = s - 1
                        if 0 <= q < NQ:
                            act.wait_ge(s_xn, START + b * NQ + q + 1)
                            act.wait_ge(o_x1[q % 4], START + b * 32 + 16 * (q // 4))
                            nc.scalar.copy(x1[:, q % 4, :], xn[:, q % 4, :]).then_inc(s_x1, 1)
                            act.wait_ge(s_ss, START + b * NQ + q)
                            nc.scalar.activation(square[:], xn[:, q % 4, :], ACT.Square, accum_out=sumsq[:, q:q + 1]).then_inc(s_ss, 1)
                        q = s - 2
                        if 0 <= q < NQ:
                            act.wait_ge(s_r1, START + b * NQ + q + 1)
                            act.wait_ge(o_x2[q % 2], START + b * 64 + 16 * (q // 2))
                            act.wait_ge(s_x3, START + b * NQ + max(q - 1, 0))
                            nc.scalar.copy(x2[:, q % 2, :], r1[:, q % 2, :]).then_inc(s_x2, 1)
                        q = s - 4
                        if 0 <= q < NQ:
                            act.wait_ge(s_xp, START + b * NQ + q + 1)
                            nc.scalar.copy(xproj[:, q, :], px[:, 0:3 * STATES]).then_inc(s_xe, 1)
                    act.wait_ge(s_v3, START + b * 5 + 1)
                    nc.scalar.activation(root[:], ssm[:], ACT.Sqrt).then_inc(s_rt, 1)
                    for j, t in enumerate((c_t, dt_t)):
                        act.wait_ge(s_t3, START + b * 2 + j + 1)
                        if j == 0:
                            act.wait_ge(o_3, START + b * 80)
                        nc.scalar.copy(t[:], pa[j][0:STATES, :]).then_inc(s_c3, 1)
                    act.wait_ge(s_mm3, START + b + 1)
                    act.wait_ge(s_ad, START + b)
                    nc.scalar.activation(th[:], pt[0:STATES, :], ACT.Tanh, bias=b_dt[:]).then_inc(s_th, 2)
            @block.gpsimd
            def _(pool):
                with pool.Fori(0, BATCH) as b:
                    for s in range(NQ + 2):
                        if s < NQ:
                            pool.wait_ge(s_xn0, START + b * NQ + s + 1)
                            if s >= 2:
                                pool.wait_ge(s_xn, START + b * NQ + s - 1)
                            nc.gpsimd.tensor_tensor(out=xg[:, s % 2, :], in0=xn0[:, s % 2, :], in1=ln_g[:], op=ALU.mult).then_inc(s_xg, 1)
                        q = s - 2
                        if 0 <= q < NQ:
                            pool.wait_ge(s_x2, START + b * NQ + q + 1)
                            pool.wait_ge(o_x3[q % 2], START + b * 64 + 16 * (q // 2))
                            nc.gpsimd.tensor_tensor(out=x3[:, q % 2, :], in0=r1[:, q % 2, :], in1=x2[:, q % 2, :], op=ALU.subtract).then_inc(s_x3, 1)
            @block.vector
            def _(dve):
                with dve.Fori(0, BATCH) as b:
                    for m in range(NM):
                        dve.wait_ge(s_tap, START + b * NM + m + 1)
                        for j in range(TAPS - 1):
                            if j:
                                dve.wait_ge(s_conv, START + b * (3 * NM) + 3 * m + j)
                            nc.vector.scalar_tensor_tensor(out=acc[:, m % 2, :], in0=padded[:, m % 2, j:j + SEQ], scalar=w_conv[:, m, j:j + 1], in1=acc[:, m % 2, :],
                                                           op0=ALU.mult, op1=ALU.add).then_inc(s_conv, 1)
                    for s in range(NQ + 3):
                        if s < NQ:
                            dve.wait_ge(s_tp, START + b * NQ + s + 1)
                            base = 4 * s
                            if s >= 1:
                                dve.wait_ge(s_sd, START + b * NQ + s)
                            for h in range(2):
                                nc.vector.bn_stats(out=stats[:, h, :], in_=pa[s % 2][:, h * 512:h * 512 + 512]).then_inc(s_dv, 1)
                            dve.wait_ge(s_dv, START + b * (4 * NQ) + base + 2)
                            nc.vector.memset(idle[:], 0.0)
                            nc.vector.bn_aggr(out=mv[:], in_=stats[:]).then_inc(s_dv, 1)
                            dve.wait_ge(s_dv, START + b * (4 * NQ) + base + 3)
                            nc.vector.tensor_scalar(out=var_eps[:], in0=mv[:, 1:2], scalar1=1e-5, scalar2=None, op0=ALU.add).then_inc(s_dv, 1)
                        q = s - 1
                        if 0 <= q < NQ:
                            dve.wait_ge(s_xg, START + b * NQ + q + 1)
                            dve.wait_ge(o_xn[q % 4], START + b * 32 + 16 * (q // 4))
                            if q >= 4:
                                dve.wait_ge(s_ss, START + b * NQ + q - 3)
                                dve.wait_ge(s_tb, START + b * NQ + q - 3)
                            nc.vector.tensor_tensor(out=xn[:, q % 4, :], in0=xg[:, q % 2, :], in1=ln_b[:], op=ALU.add).then_inc(s_xn, 1)
                        if s < NQ:
                            dve.wait_ge(s_sd, START + b * NQ + s + 1)
                            if s >= 2:
                                dve.wait_ge(s_xn0, START + b * NQ + s - 1)
                            nc.vector.reciprocal(out=rstd[:, s % 2:s % 2 + 1], in_=std[:]).then_inc(s_nmr, 1)
                            dve.wait_ge(s_nmr, START + b * (2 * NQ) + 2 * s + 1)
                            nc.vector.scalar_tensor_tensor(out=nmr[:, s % 2:s % 2 + 1], in0=mv[:, 0:1], scalar=-1.0, in1=rstd[:, s % 2:s % 2 + 1], op0=ALU.mult, op1=ALU.mult).then_inc(s_nmr, 1)
                        q = s - 2
                        if 0 <= q < NQ:
                            dve.wait_ge(s_x1, START + b * NQ + q + 1)
                            dve.wait_ge(s_x3, START + b * NQ + max(q - 1, 0))
                            nc.vector.tensor_tensor(out=r1[:, q % 2, :], in0=xn[:, q % 4, :], in1=x1[:, q % 4, :], op=ALU.subtract).then_inc(s_r1, 1)
                            dve.wait_ge(s_tb, START + b * NQ + q + 1)
                            dve.wait_ge(s_xp, START + b * NQ + max(q - 1, 0))
                            nc.vector.tensor_copy(out=xn_t[:, q % 2], in_=pt[:].rearrange("p (m t) -> p m t", m=NM)).then_inc(s_xnt, 1)
                    dve.wait_ge(s_ss, START + b * NQ + NQ)
                    dve.wait_ge(s_rt, START + b)
                    nc.vector.tensor_scalar(out=ssm[:], in0=sumsq[:], scalar1=1.0, scalar2=None, op0=ALU.min).then_inc(s_v3, 1)
                    nc.vector.tensor_scalar(out=geq[:], in0=sumsq[:], scalar1=1.0, scalar2=None, op0=ALU.is_ge).then_inc(s_v3, 1)
                    dve.wait_ge(s_v3, START + b * 5 + 2)
                    dve.wait_ge(s_rt, START + b + 1)
                    nc.vector.tensor_tensor(out=nrm[:], in0=root[:], in1=geq[:], op=ALU.max).then_inc(s_v3, 1)
                    dve.wait_ge(s_v3, START + b * 5 + 3)
                    nc.vector.tensor_scalar(out=nrm[:], in0=nrm[:], scalar1=1.0, scalar2=None, op0=ALU.min).then_inc(s_v3, 1)
                    dve.wait_ge(s_v3, START + b * 5 + 4)
                    dve.wait_ge(s_xe, START + b * NQ + NQ)
                    dve.wait_ge(o_3, START + b * 80)
                    nc.vector.tensor_tensor(out=bd[:], in0=xproj[:, :, 0:STATES], in1=nrm[:].rearrange("p (q o) -> p q o", o=1).to_broadcast([P, NQ, STATES]), op=ALU.mult).then_inc(s_v3, 1)
                    dve.wait_ge(s_v3, START + b * 5 + 5)
                    nc.vector.tensor_copy(out=b1[:], in_=bd[:]).then_inc(s_b1, 1)
                    dve.wait_ge(s_b1, START + b * 3 + 1)
                    nc.vector.tensor_tensor(out=br1[:], in0=bd[:], in1=b1[:], op=ALU.subtract).then_inc(const_c, 1)
                    dve.wait_ge(const_c, START + b + 2)
                    nc.vector.tensor_copy(out=b2[:], in_=br1[:]).then_inc(s_b1, 1)
                    dve.wait_ge(s_b1, START + b * 3 + 2)
                    nc.vector.tensor_tensor(out=b3[:], in0=br1[:], in1=b2[:], op=ALU.subtract).then_inc(s_b1, 1)
                    dve.wait_ge(s_th, START + b * 2 + 3)
                    nc.vector.tensor_scalar(out=ad[:], in0=th[:], scalar1=neg_a[:], scalar2=1.0, op0=ALU.mult, op1=ALU.add).then_inc(s_ad, 1)


def scan_phase(nc, Xp, Bp, Ad, Cm, Y, maskB_d, maskC_d):
    T = 16
    STEPS = 2 * T
    LOOPS = SEQ // STEPS
    ROWS = 2 * BATCH
    K = 6 * ROWS
    RING = 4
    AHEAD = STEPS
    with ExitStack() as ctx:
        sb = lambda n, s, d: ctx.enter_context(nc.sbuf_tensor("b_" + n, s, d))
        pb = lambda n, s, d: ctx.enter_context(nc.psum_tensor("b_" + n, s, d))
        sems = []
        def sem(n):
            sems.append(ctx.enter_context(nc.semaphore("b_" + n)))
            return sems[-1]
        bd_all = sb("bd_all", [K, SEQ * STATES], bf16)
        decay_all = sb("decay_all", [128, SEQ], f32)
        c_all = sb("c_all", [128, SEQ], f32)
        mask_b = sb("mask_b", [K, 128], f32)
        mask_c = sb("mask_c", [128, T, 32], f32)
        x_moving = sb("x_moving", [K, 2, T * HALF], bf16)
        b_weights = sb("b_weights", [K, 2, T, 128], bf16)
        c_weights = sb("c_weights", [128, 2, T, 32], f32)
        decay = sb("decay", [128, 2, T], f32)
        z = sb("z", [128, HALF], f32)
        h = sb("h", [128, RING, HALF], f32)
        y_stage = sb("y_stage", [128, 2, T // 4, 128], f32)
        zeros = sb("zeros", [K, HALF], bf16)
        bx = [pb(f"bx{i}", [128, HALF], f32) for i in range(2)]
        y_psum = [pb(f"y_psum{i}", [128, 512], f32) for i in range(2)]
        consts_in = sem("consts_in"); zeros_ready = sem("zeros_ready")
        x_in = [sem(f"x_in{i}") for i in range(2)]
        w_ready = [sem(f"w_ready{i}") for i in range(2)]
        bx_ready = sem("bx_ready")
        z_ready = sem("z_ready")
        h_ready = sem("h_ready")
        read = sem("read")
        y_free = sem("y_free")
        y_out = [sem(f"y_out{i}") for i in range(2)]

        with nc.Block() as block:
            @block.sync
            def _(sp):
                start_counts(sp, sems)
                sp.dma_start(mask_b[:], maskB_d).then_inc(consts_in, 16)
                sp.dma_start(mask_c[:], maskC_d).then_inc(consts_in, 16)
                for half in range(2):
                    sp.dma_start(c_all[64 * half:64 * half + 64, :], Cm).then_inc(consts_in, 16)
                    sp.dma_start(decay_all[64 * half:64 * half + 64, :], Ad).then_inc(consts_in, 16)
                row = 0
                for part, copies in ((0, 3), (1, 2), (2, 1)):
                    for _ in range(2 * copies):
                        sp.dma_start(bd_all[row:row + BATCH, :], Bp[part].rearrange("b t d -> b (t d)")).then_inc(consts_in, 16)
                        row += BATCH
                sp.wait_ge(consts_in, START + 18 * 16)
            @block.vector
            def _(dve):
                nc.vector.memset(zeros[:], 0.0).then_inc(zeros_ready, 1)
                nc.vector.memset(h[:, RING - 1, :], 0.0).then_inc(zeros_ready, 1)
                nc.vector.memset(c_weights[:, 1, T - 1, :], 0.0).then_inc(zeros_ready, 1)
            @block.tensor
            def _(pe):
                pe.wait_ge(zeros_ready, START + 3)
                nc.tensor.matmul(y_psum[0][:], zeros[:, 0:128], zeros[:], start=True, stop=True).then_inc(read, AHEAD)
                nc.tensor.matmul(y_psum[1][:], zeros[:, 0:128], zeros[:], start=True, stop=True).then_inc(y_free, 1)

        with nc.Block() as block:
            @block.sync
            def _(sp):
                with sp.Fori(0, LOOPS) as it:
                    for i in range(2):
                        sp.wait_ge(read, START + it * STEPS + (AHEAD - 15 if i == 0 else AHEAD + 1))
                        t0 = it * STEPS + i * T
                        for row, parts in ((0, 3), (24, 2), (40, 1)):
                            src = Xp[0:parts * ROWS, bass.ds(t0 * HALF, T * HALF)]
                            sp.dma_start(x_moving[row:row + parts * ROWS, i, :], src).then_inc(x_in[i], 16)
            @block.gpsimd
            def _(pool):
                with pool.Fori(0, LOOPS) as it:
                    for i in range(2):
                        t0 = it * STEPS + i * T
                        pool.wait_ge(read, START + it * STEPS + (AHEAD - 15 if i == 0 else AHEAD + 1))
                        bd = bd_all[:, bass.ds(t0 * STATES, T * STATES)].rearrange("k (t o d) -> k t o d", o=1, d=STATES).to_broadcast([K, T, 8, STATES])
                        mb = mask_b[:].rearrange("k (o r d) -> k o r d", o=1, d=STATES).to_broadcast([K, T, 8, STATES])
                        nc.gpsimd.tensor_tensor(out=b_weights[:, i].rearrange("k t (r d) -> k t r d", d=STATES), in0=bd, in1=mb, op=ALU.mult).then_inc(w_ready[i], 1)
                        cc = c_all[:, bass.ds(t0, T)].rearrange("p (t o) -> p t o", o=1).to_broadcast([128, T, 32])
                        nc.gpsimd.tensor_tensor(out=c_weights[:, i], in0=cc, in1=mask_c[:], op=ALU.mult).then_inc(w_ready[i], 1)
                        nc.gpsimd.tensor_copy(out=decay[:, i], in_=decay_all[:, bass.ds(t0, T)]).then_inc(w_ready[i], 1)
            @block.tensor
            def _(pe):
                def readout(it, u):
                    i, tt = (u // T) % 2, u % T
                    pe.wait_ge(h_ready, START + it * (2 * STEPS) + 2 * (u + 1))
                    if u % 4 == 0:
                        pe.wait_ge(y_free, START + it * (STEPS // 4) + u // 4)
                    for j in range(4):
                        m = nc.tensor.matmul(y_psum[(u // 4) % 2][32 * j:32 * j + 32, 0:128], c_weights[:, i, tt, :],
                                             h[:, u % RING, 128 * j:128 * j + 128], start=(u % 4 == 0), stop=(u % 4 == 3), skip_group_check=True)
                    m.then_inc(read, 1)
                with pe.Fori(0, LOOPS) as it:
                    for u in range(STEPS):
                        i, tt = u // T, u % T
                        if tt == 0:
                            pe.wait_ge(x_in[i], START + it * 48 + 48)
                            pe.wait_ge(w_ready[i], START + it * 3 + 3)
                        if u == 0 or u == 1:
                            pe.wait_ge(h_ready, START + it * (2 * STEPS) + 2 * max(u - 1, 0))
                        else:
                            pe.wait_ge(z_ready, START + it * (2 * STEPS) + 2 * (u - 1))
                        nc.tensor.matmul(bx[u % 2][:], b_weights[:, i, tt, :], x_moving[:, i, tt * HALF:(tt + 1) * HALF],
                                         start=True, stop=True).then_inc(bx_ready, 1)
                        readout(it, u - 1)
                pe.wait_ge(h_ready, START + LOOPS * 2 * STEPS)
                u = STEPS - 1
                for j in range(4):
                    m = nc.tensor.matmul(y_psum[1][32 * j:32 * j + 32, 0:128], c_weights[:, 1, T - 1, :],
                                         h[:, RING - 1, 128 * j:128 * j + 128], start=False, stop=True, skip_group_check=True)
                m.then_inc(read, 1)
            @block.vector
            def _(dve):
                HW = HALF // 2
                with dve.Fori(0, LOOPS) as it:
                    for u in range(STEPS):
                        i, tt = u // T, u % T
                        if tt == 0:
                            dve.wait_ge(w_ready[i], START + it * 3 + 3)
                        dve.wait_ge(bx_ready, START + it * STEPS + (u + 1))
                        for g in range(2):
                            c = slice(g * HW, (g + 1) * HW)
                            dve.wait_ge(h_ready, START + it * (2 * STEPS) + (2 * u - 1 + g if 2 * u - 1 + g > 0 else g * 0))
                            nc.vector.scalar_tensor_tensor(out=z[:, c], in0=h[:, (u - 1) % RING, c], scalar=decay[:, i, tt:tt + 1], in1=bx[u % 2][:, c],
                                                           op0=ALU.mult, op1=ALU.add).then_inc(z_ready, 1)
                        dve.wait_ge(read, START + it * STEPS + (AHEAD + u - 2))
                        for g in range(2):
                            c = slice(g * HW, (g + 1) * HW)
                            dve.wait_ge(z_ready, START + it * (2 * STEPS) + (2 * u + 1 + g))
                            nc.vector.tensor_scalar(out=h[:, u % RING, c], in0=z[:, c], scalar1=-10.0, scalar2=10.0,
                                                    op0=ALU.max, op1=ALU.min).then_inc(h_ready, 1)
            @block.scalar
            def _(act):
                with act.Fori(0, LOOPS) as it:
                    for q in range(STEPS // 4):
                        i = (4 * q) // T
                        act.wait_ge(read, START + it * STEPS + (AHEAD + 4 * q + 5))
                        if (4 * q) % T == 0:
                            act.wait_ge(y_out[i], START + it * 64)
                        nc.scalar.copy(y_stage[:, i, q % (T // 4), :], y_psum[q % 2][:, 0:128]).then_inc(y_free, 1)
                        if (4 * q + 4) % T == 0:
                            act.wait_ge(y_free, START + it * (STEPS // 4) + (q + 2))
                            dst = Y[bass.ds(it * STEPS + i * T, T)].rearrange("(q s) r (j c) -> j (s r) q c", s=4, j=4)
                            for j in range(4):
                                act.dma_start(dst[j], y_stage[32 * j:32 * j + 32, i]).then_inc(y_out[i], 16)
                for i in range(2):
                    act.wait_ge(y_out[i], START + LOOPS * 64)


def gate_phase(nc, I, Xn, Y, X1):
    with ExitStack() as ctx:
        sb = lambda n, s, d=f32: ctx.enter_context(nc.sbuf_tensor("c_" + n, s, d))
        pb = lambda n, s, d=f32: ctx.enter_context(nc.psum_tensor("c_" + n, s, d))
        sems = []
        def sem(n):
            sems.append(ctx.enter_context(nc.semaphore("c_" + n)))
            return sems[-1]
        w_gate = sb("w_gate", [P, NK, INNER]); w_out = sb("w_out", [P, NM, MODEL]); ident = sb("ident", [P, P]); d_row = sb("d_row", [P, INNER])
        x_t = sb("x_t", [P, NK, SEQ])
        y = sb("y", [P, 2, INNER]); xn = sb("xn", [P, 2, INNER]); x = sb("x", [P, 4, MODEL])
        sg = sb("sg", [P, 2, INNER]); t2 = sb("t2", [P, INNER]); yg = sb("yg", [P, 2, INNER]); yg_t = sb("yg_t", [P, 2, NM, P]); x1 = sb("x1", [P, 2, MODEL])
        pg = [pb(f"pg{i}", [P, INNER]) for i in range(2)]; pt = pb("pt", [P, INNER]); po = [pb(f"po{i}", [P, MODEL]) for i in range(2)]
        consts = sem("consts"); xt_in = sem("xt_in")
        y_in = [sem(f"y_in{i}") for i in range(2)]; x_in = [sem(f"x_in{i}") for i in range(4)]; o_x1 = [sem(f"o_x1{i}") for i in range(2)]
        s_g = sem("s_g"); s_sg = sem("s_sg"); s_dx = sem("s_dx"); s_t2 = sem("s_t2"); s_yg = sem("s_yg"); s_tp = sem("s_tp"); s_cp = sem("s_cp"); s_o = sem("s_o"); s_x1 = sem("s_x1")
        with nc.Block() as block:
            @block.sync
            def _(sp):
                start_counts(sp, sems)
                for dst, src in ((w_gate[:], I["w_in_t"][:, INNER:2 * INNER].rearrange("(k p) n -> p k n", p=P)),
                                 (w_out[:], I["w_out_t"].rearrange("(m p) n -> p m n", p=P)),
                                 (d_row[:], I["D"].rearrange("(o n) -> o n", o=1).to_broadcast([P, INNER])), (ident[:], I["ident"])):
                    sp.dma_start(dst, src).then_inc(consts, 16)
                sp.wait_ge(consts, START + 64)
        with nc.Block() as block:
            @block.sync
            def _(sp):
                with sp.Fori(0, BATCH) as b:
                    sp.wait_ge(s_g, START + b * NQ)
                    sp.dma_start(x_t[:], I["x_t"][bass.ds(b, 1)].rearrange("o (k p) t -> p (o k) t", p=P)).then_inc(xt_in, 16)
                    for s in range(NQ + 3):
                        q = s
                        if q < NQ:
                            sp.wait_ge(s_t2, START + b * NQ + max(q - 1, 0))
                            if q >= 4:
                                sp.wait_ge(s_x1, START + b * NQ + q - 3)
                            sp.dma_start(y[:, q % 2, :], Y[q * P:(q + 1) * P].rearrange("t (h b) c -> b t h c", h=2)[bass.ds(b, 1)].rearrange("o t h c -> (o t) h c")).then_inc(y_in[q % 2], 16)
                            sp.dma_start(xn[:, q % 2, :], Xn[bass.ds(b, 1)].rearrange("o t c -> (o t) c")[q * P:(q + 1) * P, :]).then_inc(y_in[q % 2], 16)
                            sp.dma_start(x[:, q % 4, :], I["x"][bass.ds(b, 1)].rearrange("o t c -> (o t) c")[q * P:(q + 1) * P, :]).then_inc(x_in[q % 4], 16)
                        q = s - 3
                        if q >= 0:
                            sp.wait_ge(s_x1, START + b * NQ + q + 1)
                            sp.dma_start(X1[bass.ds(b, 1)].rearrange("o t c -> (o t) c")[q * P:(q + 1) * P, :], x1[:, q % 2, :]).then_inc(o_x1[q % 2], 16)
                for i in range(2):
                    sp.wait_ge(o_x1[i], START + 64 * BATCH)
            @block.tensor
            def _(pe):
                with pe.Fori(0, BATCH) as b:
                    pe.wait_ge(xt_in, START + b * 16 + 16)
                    for s in range(NQ + 2):
                        q = s
                        if q < NQ:
                            pe.wait_ge(s_sg, START + b * NQ + max(q - 1, 0))
                            for h in range(2):
                                for k in range(NK):
                                    mm = nc.tensor.matmul(pg[q % 2][:, h * 512:h * 512 + 512], x_t[:, k, q * P:(q + 1) * P], w_gate[:, k, h * 512:h * 512 + 512], start=(k == 0), stop=(k == NK - 1))
                            mm.then_inc(s_g, 1)
                        q = s - 1
                        if 0 <= q < NQ:
                            pe.wait_ge(s_yg, START + b * NQ + q + 1)
                            pe.wait_ge(s_cp, START + b * NQ + q)
                            for m in range(NM):
                                mm = nc.tensor.transpose(pt[:, m * P:(m + 1) * P], yg[:, q % 2, m * P:(m + 1) * P], ident[:])
                            mm.then_inc(s_tp, 1)
                        q = s - 2
                        if 0 <= q < NQ:
                            pe.wait_ge(s_cp, START + b * NQ + q + 1)
                            pe.wait_ge(s_x1, START + b * NQ + max(q - 1, 0))
                            for m in range(NM):
                                mm = nc.tensor.matmul(po[q % 2][:], yg_t[:, q % 2, m, :], w_out[:, m, :], start=(m == 0), stop=(m == NM - 1))
                            mm.then_inc(s_o, 1)
            @block.scalar
            def _(act):
                with act.Fori(0, BATCH) as b:
                    for s in range(NQ + 1):
                        q = s
                        if q < NQ:
                            act.wait_ge(s_g, START + b * NQ + q + 1)
                            act.wait_ge(s_yg, START + b * NQ + max(q - 1, 0))
                            nc.scalar.activation(sg[:, q % 2, :], pg[q % 2][:], ACT.Silu).then_inc(s_sg, 1)
                        q = s - 1
                        if q >= 0:
                            act.wait_ge(s_tp, START + b * NQ + q + 1)
                            act.wait_ge(s_o, START + b * NQ + max(q - 1, 0))
                            nc.scalar.copy(yg_t[:, q % 2], pt[:].rearrange("p (m t) -> p m t", m=NM)).then_inc(s_cp, 1)
            @block.gpsimd
            def _(pool):
                with pool.Fori(0, BATCH) as b:
                    for q in range(NQ):
                        pool.wait_ge(y_in[q % 2], START + b * (16 * NQ) + 32 * (q // 2 + 1))
                        nc.gpsimd.tensor_tensor(out=xn[:, q % 2, :], in0=xn[:, q % 2, :], in1=d_row[:], op=ALU.mult).then_inc(s_dx, 1)
            @block.vector
            def _(dve):
                with dve.Fori(0, BATCH) as b:
                    for s in range(NQ + 2):
                        q = s
                        if q < NQ:
                            dve.wait_ge(s_dx, START + b * NQ + q + 1)
                            dve.wait_ge(s_yg, START + b * NQ + q)
                            nc.vector.tensor_tensor(out=t2[:], in0=xn[:, q % 2, :], in1=y[:, q % 2, :], op=ALU.add).then_inc(s_t2, 1)
                            dve.wait_ge(s_t2, START + b * NQ + q + 1)
                            dve.wait_ge(s_sg, START + b * NQ + q + 1)
                            dve.wait_ge(s_tp, START + b * NQ + max(q - 1, 0))
                            nc.vector.tensor_tensor(out=yg[:, q % 2, :], in0=t2[:], in1=sg[:, q % 2, :], op=ALU.mult).then_inc(s_yg, 1)
                        q = s - 2
                        if q >= 0:
                            dve.wait_ge(s_o, START + b * NQ + q + 1)
                            dve.wait_ge(x_in[q % 4], START + b * 32 + 16 * (q // 4 + 1))
                            dve.wait_ge(o_x1[q % 2], START + b * 64 + 16 * (q // 2))
                            nc.vector.tensor_tensor(out=x1[:, q % 2, :], in0=x[:, q % 4, :], in1=po[q % 2][:], op=ALU.add).then_inc(s_x1, 1)


def proj_phase(nc, I, X1, QK, V, X2, WDC):
    with ExitStack() as ctx:
        sb = lambda n, s, d=f32: ctx.enter_context(nc.sbuf_tensor("d_" + n, s, d))
        pb = lambda n, s, d=f32: ctx.enter_context(nc.psum_tensor("d_" + n, s, d))
        sems = []
        def sem(n):
            sems.append(ctx.enter_context(nc.semaphore("d_" + n)))
            return sems[-1]
        mats = "qkvwu"
        w = {j: sb("w_" + j, [P, NK, MODEL]) for j in mats}
        w2 = sb("w2", [P, 2, NK, MODEL]); ident = sb("ident", [P, P])
        s_col = sb("s_col", [P, 2 * NK, BATCH]); ssq = sb("ssq", [P, 2 * NK, BATCH])
        s2_row = sb("s2_row", [P, BATCH, MODEL]); rows = sb("rows", [P, 3 * BATCH, MODEL]); idle = sb("idle", [P, 1])
        qk = sb("qk", [P, 2 * NK * BATCH]); qk_col = sb("qk_col", [P, NK * BATCH])
        s1_row = sb("s1_row", [P, MODEL]); wu_b = sb("wu_b", [P, NK, MODEL])
        x1 = sb("x1", [P, 4, MODEL]); xs = sb("xs", [P, 2, MODEL]); xl = sb("xl", [P, 2, MODEL]); xl_t = sb("xl_t", [P, NK, SEQ])
        stats = sb("stats", [P, 6]); mv = sb("mv", [P, 2]); var_eps = sb("var_eps", [P, 1]); std = sb("std", [P, 1]); rstd = sb("rstd", [P, 2]); nmr = sb("nmr", [P, 2])
        v = sb("v", [P, 2, MODEL]); v_t = sb("v_t", [P, NK, P]); x2 = sb("x2", [P, 2, MODEL])
        qf = sb("qf", [P, 2, SEQ]); hi = sb("hi", [P, 2, SEQ], f32r); lo = sb("lo", [P, 2, SEQ], f32r)
        pt = pb("pt", [P, MODEL]); pv = pb("pv", [P, MODEL]); pvt = pb("pvt", [P, MODEL]); psk = pb("psk", [P, MODEL])
        pqk = [pb(f"pqk{i}", [P, SEQ]) for i in range(2)]
        consts = sem("consts"); s_w2 = sem("s_w2"); s_cf = sem("s_cf"); s_rw = sem("s_rw"); s_sq = sem("s_sq"); s_rc = sem("s_rc"); o_w = sem("o_w")
        b_in = sem("b_in"); x_in = [sem(f"x_in{i}") for i in range(4)]
        s_xs = sem("s_xs"); s_dv = sem("s_dv"); s_sd = sem("s_sd"); s_nm = sem("s_nm"); s_xl = sem("s_xl"); s_tp = sem("s_tp"); s_xt = sem("s_xt")
        s_pv = sem("s_pv"); s_v = sem("s_v"); s_vt = sem("s_vt"); s_vc = sem("s_vc"); s_sk = sem("s_sk"); s_x2 = sem("s_x2"); s_wu = sem("s_wu")
        s_qk = sem("s_qk"); s_qf = sem("s_qf"); s_hi = sem("s_hi"); s_lo = sem("s_lo")
        o_v = [sem(f"o_v{i}") for i in range(2)]; o_x2 = [sem(f"o_x2{i}") for i in range(2)]; o_qk = [sem(f"o_qk{i}") for i in range(2)]
        with nc.Block() as block:
            @block.sync
            def _(sp):
                start_counts(sp, sems)
                for j in mats:
                    sp.dma_start(w[j][:], I[j + "_t"].rearrange("(k p) n -> p k n", p=P)).then_inc(consts, 16)
                sp.dma_start(ident[:], I["ident"]).then_inc(consts, 16)
                for b in range(BATCH):
                    sp.dma_start(s_col[:, :, b], I["t_emb"][b].rearrange("(m p) -> p m", p=P), allow_slow_non_contiguous=True).then_inc(consts, 16)
                    sp.dma_start(s2_row[:, b, :], I["t_emb"][b:b + 1, MODEL:2 * MODEL].to_broadcast([P, MODEL])).then_inc(consts, 16)
                sp.wait_ge(s_rc, START + 2)
                for b in range(BATCH):
                    sp.dma_start(WDC[b], rows[:, BATCH + b, :]).then_inc(o_w, 16)
                sp.wait_ge(o_w, START + 16 * BATCH)
            @block.scalar
            def _(act):
                act.wait_ge(consts, START + 16 * (6 + 2 * BATCH))
                nc.scalar.activation(ssq[:], s_col[:], ACT.Square).then_inc(s_w2, 1)
                for n, j in enumerate(mats):
                    if n >= 2:
                        act.wait_ge(s_cf, START + (1, 2, 6)[n - 2])
                    nc.scalar.activation(w2[:, n % 2], w[j][:], ACT.Square).then_inc(s_w2, 1)
                act.wait_ge(s_rw, START + 1 + 3 * BATCH)
                nc.scalar.activation(rows[:], rows[:], ACT.Sqrt).then_inc(s_sq, 1)
                nc.scalar.activation(qk[:], qk[:], ACT.Sqrt).then_inc(s_sq, 1)
            @block.tensor
            def _(pe):
                for n, j in enumerate(mats):
                    pe.wait_ge(s_w2, START + n + 2)
                    if n < 2:
                        for ot in range(NK):
                            for k in range(NK):
                                c = (n * NK + ot) * BATCH
                                mm = nc.tensor.matmul(pt[:, c:c + BATCH], w2[:, n % 2, k, ot * P:(ot + 1) * P], ssq[:, k, :], start=(k == 0), stop=(k == NK - 1))
                        mm.then_inc(s_cf, 1)
                    else:
                        for b in range(BATCH):
                            e = (n - 2) * BATCH + b
                            if e >= 2:
                                pe.wait_ge(s_rw, START + e)
                            for k in range(NK):
                                style = ssq[:, (0 if n == 2 else NK) + k, b:b + 1].to_broadcast([P, P])
                                mm = nc.tensor.matmul((pv, pvt)[e % 2][:], style, w2[:, n % 2, k, :], start=(k == 0), stop=(k == NK - 1))
                            mm.then_inc(s_cf, 1)
            @block.vector
            def _(dve):
                dve.wait_ge(s_cf, START + 2)
                nc.vector.tensor_scalar(out=qk[:], in0=pt[:, 0:2 * NK * BATCH], scalar1=1e-8, scalar2=None, op0=ALU.add).then_inc(s_rw, 1)
                for e in range(3 * BATCH):
                    dve.wait_ge(s_cf, START + 3 + e)
                    nc.vector.tensor_scalar(out=rows[:, e, :], in0=(pv, pvt)[e % 2][:], scalar1=1e-8, scalar2=None, op0=ALU.add).then_inc(s_rw, 1)
                dve.wait_ge(s_sq, START + 2)
                nc.vector.reciprocal(out=qk[:], in_=qk[:]).then_inc(s_rc, 1)
                nc.vector.reciprocal(out=rows[:], in_=rows[:]).then_inc(s_rc, 1)
                dve.wait_ge(s_rc, START + 2)
                nc.vector.scalar_tensor_tensor(out=qk_col[:], in0=qk[:, 0:NK * BATCH], scalar=float(np.float32(HD) ** np.float32(-0.5)), in1=qk[:, NK * BATCH:], op0=ALU.mult, op1=ALU.mult).then_inc(s_rc, 1)
                nc.vector.tensor_tensor(out=rows[:, 0:BATCH, :], in0=rows[:, 0:BATCH, :], in1=s2_row[:], op=ALU.mult).then_inc(s_rc, 1)

        NP = 2 * NK
        with nc.Block() as block:
            @block.sync
            def _(sp):
                with sp.Fori(0, BATCH) as b:
                    sp.wait_ge(s_xs, START + b * NQ)
                    sp.dma_start(s1_row[:], I["t_emb"][bass.ds(b, 1), 0:MODEL].to_broadcast([P, MODEL])).then_inc(b_in, 16)
                    for s in range(NQ + 4):
                        q = s - 2
                        if 0 <= q < NQ:
                            sp.wait_ge(s_v, START + b * NQ + q + 1)
                            sp.dma_start(V.rearrange("(b g) t c -> b t g c", b=BATCH)[bass.ds(b, 1)].rearrange("o t g c -> (o t) g c")[q * P:(q + 1) * P], v[:, q % 2, :].rearrange("p (g c) -> p g c", c=P)).then_inc(o_v[q % 2], 16)
                        q = s
                        if q < NQ:
                            sp.wait_ge(s_x2, START + b * NQ + max(q - 3, 0))
                            sp.dma_start(x1[:, q % 4, :], X1[bass.ds(b, 1)].rearrange("o t c -> (o t) c")[q * P:(q + 1) * P, :]).then_inc(x_in[q % 4], 16)
                        q = s - 4
                        if 0 <= q < NQ:
                            sp.wait_ge(s_x2, START + b * NQ + q + 1)
                            sp.dma_start(X2[bass.ds(b, 1)].rearrange("o t c -> (o t) c")[q * P:(q + 1) * P, :], x2[:, q % 2, :]).then_inc(o_x2[q % 2], 16)
                    for e in range(NP):
                        ot, j = e // 2, e % 2
                        for part, t, s_t in ((0, hi, s_hi), (1, lo, s_lo)):
                            sp.wait_ge(s_t, START + b * NP + e + 1)
                            dst = QK[2 * j + part].rearrange("b (t p) s -> b t p s", p=P)[bass.ds(b, 1)].rearrange("o t p s -> (o t) p s")[ot]
                            sp.dma_start(dst, t[:, e % 2, :].bitcast(f32)).then_inc(o_qk[e % 2], 16)
                for i in range(2):
                    sp.wait_ge(o_v[i], START + 64 * BATCH)
                    sp.wait_ge(o_x2[i], START + 64 * BATCH)
                    sp.wait_ge(o_qk[i], START + 128 * BATCH)
            @block.gpsimd
            def _(pool):
                with pool.Fori(0, BATCH) as b:
                    pool.wait_ge(s_sk, START + b * NQ)
                    nc.gpsimd.tensor_tensor(out=wu_b[:], in0=w["u"][:], in1=rows[:, 2 * BATCH:3 * BATCH, :][:, bass.ds(b, 1), :].to_broadcast([P, NK, MODEL]), op=ALU.mult).then_inc(s_wu, 1)
            @block.tensor
            def _(pe):
                with pe.Fori(0, BATCH) as b:
                    for s in range(NQ + 3):
                        q = s
                        if q < NQ:
                            pe.wait_ge(s_xl, START + b * NQ + q + 1)
                            pe.wait_ge(s_xt, START + b * NQ + q)
                            for k in range(NK):
                                mm = nc.tensor.transpose(pt[:, k * P:(k + 1) * P], xl[:, q % 2, k * P:(k + 1) * P], ident[:])
                            mm.then_inc(s_tp, 1)
                        q = s - 1
                        if 0 <= q < NQ:
                            pe.wait_ge(s_xt, START + b * NQ + q + 1)
                            pe.wait_ge(s_v, START + b * NQ + q)
                            for k in range(NK):
                                mm = nc.tensor.matmul(pv[:], xl_t[:, k, q * P:(q + 1) * P], w["v"][:, k, :], start=(k == 0), stop=(k == NK - 1))
                            mm.then_inc(s_pv, 1)
                        q = s - 2
                        if 0 <= q < NQ:
                            pe.wait_ge(s_v, START + b * NQ + q + 1)
                            pe.wait_ge(s_vc, START + b * NQ + q)
                            for k in range(NK):
                                mm = nc.tensor.transpose(pvt[:, k * P:(k + 1) * P], v[:, q % 2, k * P:(k + 1) * P], ident[:])
                            mm.then_inc(s_vt, 1)
                        q = s - 3
                        if 0 <= q < NQ:
                            pe.wait_ge(s_vc, START + b * NQ + q + 1)
                            pe.wait_ge(s_x2, START + b * NQ + q)
                            if q == 0:
                                pe.wait_ge(s_wu, START + b + 1)
                            for k in range(NK):
                                mm = nc.tensor.matmul(psk[:], v_t[:, k, :], wu_b[:, k, :], start=(k == 0), stop=(k == NK - 1))
                            mm.then_inc(s_sk, 1)
                    for e in range(NP):
                        ot, j = e // 2, e % 2
                        pe.wait_ge(s_qf, START + b * NP + max(e - 1, 0))
                        for h in range(NH):
                            for k in range(NK):
                                mm = nc.tensor.matmul(pqk[e % 2][:, h * 512:h * 512 + 512], w["qk"[j]][:, k, ot * P:(ot + 1) * P], xl_t[:, k, h * 512:h * 512 + 512], start=(k == 0), stop=(k == NK - 1))
                        mm.then_inc(s_qk, 1)
            @block.scalar
            def _(act):
                with act.Fori(0, BATCH) as b:
                    for s in range(NQ + 3):
                        q = s
                        if q < NQ:
                            act.wait_ge(s_dv, START + b * (3 * NQ) + 3 * q + 3)
                            act.wait_ge(s_nm, START + b * (2 * NQ) + 2 * q)
                            nc.scalar.activation(std[:], var_eps[:], ACT.Sqrt).then_inc(s_sd, 1)
                            act.wait_ge(s_nm, START + b * (2 * NQ) + 2 * q + 2)
                            act.wait_ge(s_tp, START + b * NQ + max(q - 1, 0))
                            nc.scalar.activation(xl[:, q % 2, :], xs[:, q % 2, :], ACT.Identity, bias=nmr[:, q % 2:q % 2 + 1], scale=rstd[:, q % 2:q % 2 + 1]).then_inc(s_xl, 1)
                            act.wait_ge(s_tp, START + b * NQ + q + 1)
                            if q == 0:
                                act.wait_ge(s_qk, START + b * NP)
                            nc.scalar.copy(xl_t[:, :, q * P:(q + 1) * P], pt[:].rearrange("p (k t) -> p k t", k=NK)).then_inc(s_xt, 1)
                        q = s - 2
                        if 0 <= q < NQ:
                            act.wait_ge(s_vt, START + b * NQ + q + 1)
                            act.wait_ge(s_sk, START + b * NQ + q)
                            nc.scalar.copy(v_t[:], pvt[:].rearrange("p (k t) -> p k t", k=NK)).then_inc(s_vc, 1)
                    for e in range(NP):
                        ot, j = e // 2, e % 2
                        act.wait_ge(s_qk, START + b * NP + e + 1)
                        act.wait_ge(s_lo, START + b * NP + max(e - 1, 0))
                        if j == 0:
                            scale = qk_col[:].rearrange("p (t b) -> p t b", b=BATCH)[:, ot, bass.ds(b, 1)]
                            nc.scalar.activation(qf[:, e % 2, :], pqk[e % 2][:], ACT.Identity, scale=scale, bias=0.0).then_inc(s_qf, 1)
                        else:
                            nc.scalar.copy(qf[:, e % 2, :], pqk[e % 2][:]).then_inc(s_qf, 1)
            @block.vector
            def _(dve):
                with dve.Fori(0, BATCH) as b:
                    dve.wait_ge(b_in, START + b * 16 + 16)
                    for s in range(NQ + 4):
                        q = s
                        if q < NQ:
                            dve.wait_ge(x_in[q % 4], START + b * 32 + 16 * (q // 4 + 1))
                            dve.wait_ge(s_xl, START + b * NQ + max(q - 1, 0))
                            nc.vector.tensor_tensor(out=xs[:, q % 2, :], in0=x1[:, q % 4, :], in1=s1_row[:], op=ALU.mult).then_inc(s_xs, 1)
                            dve.wait_ge(s_xs, START + b * NQ + q + 1)
                            nc.vector.bn_stats(out=stats[:], in_=xs[:, q % 2, :]).then_inc(s_dv, 1)
                            dve.wait_ge(s_dv, START + b * (3 * NQ) + 3 * q + 1)
                            nc.vector.memset(idle[:], 0.0)
                            nc.vector.bn_aggr(out=mv[:], in_=stats[:]).then_inc(s_dv, 1)
                            dve.wait_ge(s_dv, START + b * (3 * NQ) + 3 * q + 2)
                            dve.wait_ge(s_sd, START + b * NQ + q)
                            nc.vector.tensor_scalar(out=var_eps[:], in0=mv[:, 1:2], scalar1=1e-5, scalar2=None, op0=ALU.add).then_inc(s_dv, 1)
                        if s < NQ:
                            dve.wait_ge(s_sd, START + b * NQ + s + 1)
                            nc.vector.reciprocal(out=rstd[:, s % 2:s % 2 + 1], in_=std[:]).then_inc(s_nm, 1)
                            dve.wait_ge(s_nm, START + b * (2 * NQ) + 2 * s + 1)
                            nc.vector.scalar_tensor_tensor(out=nmr[:, s % 2:s % 2 + 1], in0=mv[:, 0:1], scalar=-1.0, in1=rstd[:, s % 2:s % 2 + 1], op0=ALU.mult, op1=ALU.mult).then_inc(s_nm, 1)
                        q = s - 1
                        if 0 <= q < NQ:
                            dve.wait_ge(s_pv, START + b * NQ + q + 1)
                            dve.wait_ge(o_v[q % 2], START + b * 64 + 16 * (q // 2))
                            dve.wait_ge(s_vt, START + b * NQ + max(q - 1, 0))
                            nc.vector.tensor_tensor(out=v[:, q % 2, :], in0=rows[:, 0:BATCH, :].rearrange("p b n -> p (b n)")[:, bass.ds(b * MODEL, MODEL)], in1=pv[:], op=ALU.mult).then_inc(s_v, 1)
                        q = s - 3
                        if 0 <= q < NQ:
                            dve.wait_ge(s_sk, START + b * NQ + q + 1)
                            dve.wait_ge(o_x2[q % 2], START + b * 64 + 16 * (q // 2))
                            nc.vector.tensor_tensor(out=x2[:, q % 2, :], in0=x1[:, q % 4, :], in1=psk[:], op=ALU.add).then_inc(s_x2, 1)
                    for e in range(NP):
                        dve.wait_ge(s_qf, START + b * NP + e + 1)
                        dve.wait_ge(o_qk[e % 2], START + b * 128 + 32 * (e // 2))
                        nc.vector.tensor_copy(out=hi[:, e % 2, :], in_=qf[:, e % 2, :]).then_inc(s_hi, 1)
                        dve.wait_ge(s_hi, START + b * NP + e + 1)
                        nc.vector.tensor_tensor(out=lo[:, e % 2, :], in0=qf[:, e % 2, :], in1=hi[:, e % 2, :].bitcast(f32), op=ALU.subtract).then_inc(s_lo, 1)


def attention_phase(nc, I, QK, V, OT):
    GROUP = P // HD
    NGROUPS = BATCH * HEADS // GROUP
    KROWS = 3 * HD
    STACK = KROWS + 1
    UNITS = GROUP * NQ
    STEPS = NH * NQ
    PER_STEP = 3
    HALFQ = SEQ // NH
    with ExitStack() as ctx:
        sb = lambda n, s, d=f32: ctx.enter_context(nc.sbuf_tensor("e_" + n, s, d))
        pb = lambda n, s, d=f32: ctx.enter_context(nc.psum_tensor("e_" + n, s, d))
        sems = []
        def sem(n):
            sems.append(ctx.enter_context(nc.semaphore("e_" + n)))
            return sems[-1]
        qs = [sb(f"qs{i}", [STACK, GROUP, SEQ], f32r) for i in range(2)]
        ks = [sb(f"ks{i}", [STACK, GROUP, SEQ], f32r) for i in range(2)]
        v = [sb(f"v{i}", [P, NQ, P]) for i in range(2)]
        ident = sb("ident", [P, P]); ones = sb("ones", [P, HD]); ones_row = sb("ones_row", [STACK, GROUP * SEQ])
        row_max = [sb(f"row_max{i}", [P, UNITS]) for i in range(2)]
        neg_row = [sb(f"neg_row{i}", [UNITS, P], f32r) for i in range(2)]
        probs = sb("probs", [P, 2, GROUP, HALFQ])
        den = sb("den", [P, HALFQ]); rden = sb("rden", [P, HALFQ]); raw = sb("raw", [P, HALFQ]); o = sb("o", [P, 2, HALFQ])
        p_max = pb("p_max", [P, SEQ]); p_exp = [pb(f"p_exp{i}", [P, 2, HALFQ]) for i in range(2)]
        p_o = pb("p_o", [P, HALFQ]); p_d = pb("p_d", [P, HALFQ])
        consts = sem("consts"); c_ones = sem("c_ones")
        stacks_in = [sem(f"stacks_in{i}") for i in range(2)]; max_in = [sem(f"max_in{i}") for i in range(2)]
        unit_scores = sem("unit_scores"); unit_max = sem("unit_max"); max_turned = sem("max_turned"); max_row = sem("max_row")
        scores = sem("scores"); exps = sem("exps"); products = sem("products")
        den_taken = sem("den_taken"); raw_taken = sem("raw_taken"); rden_ready = sem("rden_ready"); o_ready = sem("o_ready")
        o_out = [sem(f"o_out{i}") for i in range(2)]

        def load(sp, n, i):
            for stack, order in ((qs[i], (0, 0, 1)), (ks[i], (2, 3, 2))):
                for row, part in enumerate(order):
                    src = QK[part].rearrange("b (g h p) s -> (b g) p h s", h=GROUP, p=HD)[bass.ds(n, 1)].rearrange("o p h s -> (o p) h s")
                    sp.dma_start(stack[row * HD:(row + 1) * HD].bitcast(f32), src).then_inc(stacks_in[i], 16)
            sp.dma_start(v[i][:], V[bass.ds(n, 1)].rearrange("o (q p) c -> p (o q) c", p=P)).then_inc(stacks_in[i], 16)
        LOADS = 7 * 16

        def send_max(sp, n, i, turn):
            sp.wait_ge(max_row, START + n + 1)
            sp.dma_start(qs[i][KROWS:STACK].rearrange("o h t -> o (h t)").rearrange("o (u c) -> (o u) c", c=P).bitcast(f32) if False else
                         qs[i][KROWS:STACK].rearrange("o h (q c) -> o (h q) c", c=P).bitcast(f32),
                         neg_row[i][:].bitcast(f32)).then_inc(max_in[i], 16)

        def send_out(sp, n):
            for half in range(NH):
                sp.wait_ge(o_ready, START + n * NH + half + 1)
                sp.dma_start(OT[bass.ds(n, 1)].rearrange("o p s -> (o p) s")[:, half * HALFQ:(half + 1) * HALFQ], o[:, half, :]).then_inc(o_out[half], 16)

        def max_unit(pe, n, i, u):
            h, q = divmod(u, NQ)
            pe.wait_ge(unit_max, START + n * UNITS + u)
            for half in range(NH):
                mm = nc.tensor.matmul(p_max[:, half * 512:(half + 1) * 512], qs[i][0:KROWS, h, q * P:(q + 1) * P], ks[i][0:KROWS, h, half * 512:(half + 1) * 512], start=True, stop=True)
            mm.then_inc(unit_scores, 1)

        def turn_max(pe, n, i):
            pe.wait_ge(unit_max, START + n * UNITS + UNITS)
            pe.wait_ge(max_row, START + n)
            nc.tensor.transpose(p_max[0:UNITS, 0:P], row_max[i][:], ident[:]).then_inc(max_turned, 1)

        def products_step(pe, n, i, s):
            half, kt = divmod(s, NQ)
            pe.wait_ge(exps, START + n * (2 * STEPS) + 2 * s + 2)
            if kt == 0:
                pe.wait_ge(den_taken, START + n * NH + half)
                pe.wait_ge(raw_taken, START + n * NH + half)
            for h in range(GROUP):
                nc.tensor.matmul(p_o[HD * h:HD * (h + 1), :], v[i][:, kt, HD * h:HD * (h + 1)], probs[:, s % 2, h, :], start=(kt == 0), stop=(kt == NQ - 1), skip_group_check=True)
            for h in range(GROUP):
                mm = nc.tensor.matmul(p_d[HD * h:HD * (h + 1), :], ones[:], probs[:, s % 2, h, :], start=(kt == 0), stop=(kt == NQ - 1), skip_group_check=True)
            mm.then_inc(products, 1)

        def scores_pair(pe, n, i, s, pair):
            half, kt = divmod(s, NQ)
            pe.wait_ge(exps, START + n * (2 * STEPS) + max(2 * s - 1 + pair, 0))
            for j in range(2):
                h = 2 * pair + j
                mm = nc.tensor.matmul(p_exp[pair][:, j, :], ks[i][:, h, kt * P:(kt + 1) * P], qs[i][:, h, half * HALFQ:(half + 1) * HALFQ], start=True, stop=True)
            mm.then_inc(scores, 1)

        def pe_group(pe, n, i, turn, ahead):
            pe.wait_ge(max_in[i], START + turn * 16 + 16)
            if ahead:
                nturn = turn + 1 if i else turn
                pe.wait_ge(stacks_in[1 - i], START + nturn * LOADS + LOADS)
            u = 0
            for s in range(STEPS):
                for part in range(PER_STEP):
                    if part < 2:
                        scores_pair(pe, n, i, s, part)
                    elif s:
                        products_step(pe, n, i, s - 1)
                    if ahead and u < UNITS:
                        max_unit(pe, n + 1, 1 - i, u)
                        u += 1
                        if u == UNITS:
                            last = s
                if ahead and s == last_step:
                    turn_max(pe, n + 1, 1 - i)
            products_step(pe, n, i, STEPS - 1)
        last_step = -(-UNITS // PER_STEP)

        def act_group(act, n, i, turn):
            for s in range(STEPS):
                for pair in range(2):
                    act.wait_ge(scores, START + n * (2 * STEPS) + 2 * s + pair + 1)
                    if pair == 0:
                        act.wait_ge(products, START + n * STEPS + max(s - 1, 0))
                    nc.scalar.activation(probs[:, s % 2, 2 * pair:2 * pair + 2, :], p_exp[pair][:], ACT.Exp).then_inc(exps, 1)
                if s == NQ:
                    take_raw(act, n, 0)
            take_raw(act, n, 1)

        def take_raw(act, n, half):
            act.wait_ge(products, START + n * STEPS + (half + 1) * NQ)
            act.wait_ge(o_ready, START + n * NH + half)
            nc.scalar.copy(raw[:], p_o[:]).then_inc(raw_taken, 1)

        def dve_unit(dve, n, i, u):
            dve.wait_ge(unit_scores, START + n * UNITS + u + 1)
            if u == 0:
                dve.wait_ge(max_turned, START + n)
            nc.vector.tensor_reduce(out=row_max[i][:, u:u + 1], in_=p_max[:], axis=mybir.AxisListType.X, op=ALU.max).then_inc(unit_max, 1)

        def dve_row(dve, n, i, turn):
            dve.wait_ge(max_turned, START + n + 1)
            dve.wait_ge(max_in[i], START + turn * 16)
            nc.vector.tensor_scalar(out=neg_row[i][:], in0=p_max[0:UNITS, 0:P], scalar1=-1.0, scalar2=None, op0=ALU.mult).then_inc(max_row, 1)

        def take_den(dve, n, half):
            dve.wait_ge(products, START + n * STEPS + (half + 1) * NQ)
            dve.wait_ge(rden_ready, START + n * NH + half)
            nc.vector.tensor_copy(out=den[:], in_=p_d[:]).then_inc(den_taken, 1)
            dve.wait_ge(den_taken, START + n * NH + half + 1)
            dve.wait_ge(o_ready, START + n * NH + half)
            nc.vector.reciprocal(out=rden[:], in_=den[:]).then_inc(rden_ready, 1)

        def dve_group(dve, n, i, turn, ahead):
            nturn = turn + 1 if i else turn
            u = 0
            for s in range(STEPS):
                if s == NQ + 1:
                    take_den(dve, n, 0)
                for part in range(PER_STEP):
                    if ahead and u < UNITS:
                        dve_unit(dve, n + 1, 1 - i, u)
                        u += 1
                if ahead and s == last_step:
                    dve_row(dve, n + 1, 1 - i, nturn)
            take_den(dve, n, 1)

        def pool_group(pool, n):
            for half in range(NH):
                pool.wait_ge(rden_ready, START + n * NH + half + 1)
                pool.wait_ge(raw_taken, START + n * NH + half + 1)
                pool.wait_ge(o_out[half], START + n * 16)
                nc.gpsimd.tensor_tensor(out=o[:, half, :], in0=raw[:], in1=rden[:], op=ALU.mult).then_inc(o_ready, 1)

        with nc.Block() as block:
            @block.sync
            def _(sp):
                start_counts(sp, sems)
                sp.dma_start(ident[:], I["ident"]).then_inc(consts, 16)
                for i in range(2):
                    load(sp, i, i)
                send_max(sp, 0, 0, 0)
                sp.wait_ge(max_in[0], START + 16)
            @block.vector
            def _(dve):
                nc.vector.memset(ones[:], 1.0)
                nc.vector.memset(ones_row[:], 1.0).then_inc(c_ones, 1)
                dve.wait_ge(c_ones, START + 1)
                for i in range(2):
                    nc.vector.tensor_copy(out=ks[i][KROWS:STACK].rearrange("p g t -> p (g t)"), in_=ones_row[KROWS:STACK, :])
                for u in range(UNITS):
                    dve_unit(dve, 0, 0, u)
                dve_row(dve, 0, 0, 0)
            @block.tensor
            def _(pe):
                pe.wait_ge(consts, START + 16)
                pe.wait_ge(stacks_in[0], START + LOADS)
                for u in range(UNITS):
                    max_unit(pe, 0, 0, u)
                turn_max(pe, 0, 0)

        PAIRS = NGROUPS // 2 - 1
        with nc.Block() as block:
            @block.sync
            def _(sp):
                with sp.Fori(0, PAIRS) as it:
                    for i in range(2):
                        n = it * 2 + i
                        send_max(sp, n + 1, 1 - i, None)
                        sp.wait_ge(products, START + it * (2 * STEPS) + (i + 1) * STEPS)
                        load(sp, n + 2, i)
                        send_out(sp, n)
                send_max(sp, NGROUPS - 1, 1, None)
                for n in (NGROUPS - 2, NGROUPS - 1):
                    send_out(sp, n)
                for half in range(NH):
                    sp.wait_ge(o_out[half], START + 16 * NGROUPS)
            @block.tensor
            def _(pe):
                with pe.Fori(0, PAIRS) as it:
                    for i in range(2):
                        pe_group(pe, it * 2 + i, i, it, True)
                pe_group(pe, NGROUPS - 2, 0, PAIRS, True)
                pe_group(pe, NGROUPS - 1, 1, PAIRS, False)
            @block.scalar
            def _(act):
                with act.Fori(0, PAIRS) as it:
                    for i in range(2):
                        act_group(act, it * 2 + i, i, it)
                act_group(act, NGROUPS - 2, 0, PAIRS)
                act_group(act, NGROUPS - 1, 1, PAIRS)
            @block.vector
            def _(dve):
                with dve.Fori(0, PAIRS) as it:
                    for i in range(2):
                        dve_group(dve, it * 2 + i, i, it, True)
                dve_group(dve, NGROUPS - 2, 0, PAIRS, True)
                dve_group(dve, NGROUPS - 1, 1, PAIRS, False)
            @block.gpsimd
            def _(pool):
                with pool.Fori(0, NGROUPS) as n:
                    pool_group(pool, n)

def out_phase(nc, I, OT, X2, WDC, out):
    with ExitStack() as ctx:
        sb = lambda n, s, d=f32: ctx.enter_context(nc.sbuf_tensor("f_" + n, s, d))
        sems = []
        def sem(n):
            sems.append(ctx.enter_context(nc.semaphore("f_" + n)))
            return sems[-1]
        w = sb("w", [P, NK, MODEL]); wdc = [sb(f"wdc{i}", [P, MODEL]) for i in range(2)]; wb = [sb(f"wb{i}", [P, NK, MODEL]) for i in range(2)]
        ot = [sb(f"ot{i}", [P, NK, SEQ]) for i in range(2)]; x2 = sb("x2", [P, 4, MODEL]); o = sb("o", [P, 4, MODEL])
        po = [ctx.enter_context(nc.psum_tensor(f"f_po{i}", [P, MODEL], f32)) for i in range(4)]
        consts = sem("consts"); b_in = [sem(f"b_in{i}") for i in range(2)]; x_in = [sem(f"x_in{i}") for i in range(4)]; s_wb = sem("s_wb"); s_o = sem("s_o"); s_x = sem("s_x"); o_out = [sem(f"o_out{i}") for i in range(4)]
        with nc.Block() as block:
            @block.sync
            def _(sp):
                start_counts(sp, sems)
                sp.dma_start(w[:], I["w_t"].rearrange("(k p) n -> p k n", p=P)).then_inc(consts, 16)
                with sp.Fori(0, BATCH // 2) as it:
                    for i in range(2):
                        b = it * 2 + i
                        sp.wait_ge(s_o, START + it * (2 * NQ))
                        sp.dma_start(ot[i][:], OT.rearrange("(b g) p s -> b p g s", b=BATCH)[bass.ds(b, 1)].rearrange("o p g s -> (o p) g s")).then_inc(b_in[i], 16)
                        sp.dma_start(wdc[i][:], WDC[bass.ds(b, 1)].rearrange("o p n -> (o p) n")).then_inc(b_in[i], 16)
                        for s in range(NQ + 3):
                            q = s
                            if q < NQ:
                                sp.wait_ge(s_x, START + it * (2 * NQ) + i * NQ + max(q - 3, 0))
                                sp.dma_start(x2[:, q % 4, :], X2[bass.ds(b, 1)].rearrange("o t c -> (o t) c")[q * P:(q + 1) * P, :]).then_inc(x_in[q % 4], 16)
                            q = s - 3
                            if q >= 0:
                                sp.wait_ge(s_x, START + it * (2 * NQ) + i * NQ + q + 1)
                                sp.dma_start(out[bass.ds(b, 1)].rearrange("o t c -> (o t) c")[q * P:(q + 1) * P, :], o[:, q % 4, :]).then_inc(o_out[q % 4], 16)
                for i in range(4):
                    sp.wait_ge(o_out[i], START + 32 * BATCH)
            @block.gpsimd
            def _(pool):
                pool.wait_ge(consts, START + 16)
                with pool.Fori(0, BATCH // 2) as it:
                    for i in range(2):
                        pool.wait_ge(b_in[i], START + it * 32 + 32)
                        nc.gpsimd.tensor_tensor(out=wb[i][:], in0=w[:], in1=wdc[i][:].rearrange("p (o n) -> p o n", o=1).to_broadcast([P, NK, MODEL]), op=ALU.mult).then_inc(s_wb, 1)
            @block.tensor
            def _(pe):
                with pe.Fori(0, BATCH // 2) as it:
                    for i in range(2):
                        pe.wait_ge(s_wb, START + it * 2 + i + 1)
                        pe.wait_ge(b_in[i], START + it * 32 + 32)
                        for q in range(NQ):
                            pe.wait_ge(s_x, START + it * (2 * NQ) + (i * NQ + q - 3 if i * NQ + q > 3 else 0))
                            for k in range(NK):
                                mm = nc.tensor.matmul(po[q % 4][:], ot[i][:, k, q * P:(q + 1) * P], wb[i][:, k, :], start=(k == 0), stop=(k == NK - 1))
                            mm.then_inc(s_o, 1)
            @block.vector
            def _(dve):
                with dve.Fori(0, BATCH // 2) as it:
                    for i in range(2):
                        for q in range(NQ):
                            dve.wait_ge(s_o, START + it * (2 * NQ) + i * NQ + q + 1)
                            dve.wait_ge(x_in[q % 4], START + it * 64 + i * 32 + 16 * (q // 4 + 1))
                            dve.wait_ge(o_out[q % 4], START + it * 64 + i * 32 + 16 * (q // 4))
                            nc.vector.tensor_tensor(out=o[:, q % 4, :], in0=x2[:, q % 4, :], in1=po[q % 4][:], op=ALU.add).then_inc(s_x, 1)


def build(nc, I, out):
    def scratch(name, shape, dtype=f32):
        return nc.dram_tensor(name, shape, dtype, kind="Internal").ap()

    Xp = scratch("xn_parts", [3 * 2 * BATCH, SEQ * HALF], bf16)
    Xn = scratch("xn_full", [BATCH, SEQ, INNER])
    Bp = scratch("b_parts", [3, BATCH, SEQ, STATES], bf16)
    Ad = scratch("decays", [BATCH * STATES, SEQ])
    Cm = scratch("c_rows", [BATCH * STATES, SEQ])
    Y = scratch("scan_out", [SEQ, 2 * BATCH, HALF])
    X1 = scratch("x1_full", [BATCH, SEQ, MODEL])
    QK = scratch("qk_parts", [4, BATCH, MODEL, SEQ])
    V = scratch("v_groups", [BATCH * HEADS * HD // P, SEQ, P])
    X2 = scratch("x2_full", [BATCH, SEQ, MODEL])
    WDC = scratch("w_coefs", [BATCH, P, MODEL])
    OT = scratch("attended", [BATCH * HEADS * HD // P, P, SEQ])
    pre_phase(nc, I, Xp, Xn, Bp, Ad, Cm)
    scan_phase(nc, Xp, Bp, Ad, Cm, Y, I["mask_b"], I["mask_c"])
    gate_phase(nc, I, Xn, Y, X1)
    proj_phase(nc, I, X1, QK, V, X2, WDC)
    attention_phase(nc, I, QK, V, OT)
    out_phase(nc, I, OT, X2, WDC, out)


def kernel(**inputs):
    import concourse.bacc as bacc
    from concourse.bass_utils import run_bass_kernel_spmd

    turned = lambda name: np.ascontiguousarray(np.asarray(inputs[name]).T)
    plain = lambda name: np.ascontiguousarray(inputs[name])
    mask_b = np.zeros((6 * 2 * BATCH, P), np.float32)
    for k in range(mask_b.shape[0]):
        r = k % (2 * BATCH)
        mask_b[k, r * STATES:(r + 1) * STATES] = 1
    mask_c = np.zeros((P, 16, 32), np.float32)
    for p in range(P):
        for t in range(16):
            mask_c[p, t, (t % 4) * 8 + p // STATES] = 1
    arrays = {
        "x": plain("x"), "x_t": np.ascontiguousarray(np.asarray(inputs["x"]).transpose(0, 2, 1)), "t_emb": plain("cond_2048"),
        "w_in_t": turned("L0_cond_W_in"), "w_conv": plain("L0_cond_W_conv"), "b_conv": plain("L0_cond_b_conv"),
        "ln_g": plain("L0_cond_ln_g"), "ln_b": plain("L0_cond_ln_b"), "w_xproj_t": turned("L0_cond_W_xproj"),
        "w_dt_t": np.ascontiguousarray(np.pad(turned("L0_cond_W_dt"), ((0, 0), (0, 64 - STATES)))),
        "b_dt": plain("L0_cond_b_dt"), "a_log": plain("L0_cond_A_log"), "D": plain("L0_cond_D"), "w_out_t": turned("L0_cond_W_out"),
        "ident": np.eye(P, dtype=np.float32), "mask_b": mask_b, "mask_c": mask_c,
    }
    for j in "qkvwu":
        arrays[j + "_t"] = turned(f"L1_cond_{j}_weight")
    nc = bacc.Bacc("TRN2", target_bir_lowering=False, num_devices=1)
    I = {n: nc.dram_tensor(f"in_{n}_dram", a.shape, mybir.dt.from_np(a.dtype), kind="ExternalInput").ap() for n, a in arrays.items()}
    out = nc.dram_tensor("out_dram", (BATCH, SEQ, MODEL), f32, kind="ExternalOutput").ap()
    build(nc, I, out)
    r = run_bass_kernel_spmd(nc, [{f"in_{n}_dram": a for n, a in arrays.items()}], core_ids=[0])
    return r.results[0]["out_dram"]
```

```python
from contextlib import ExitStack

import numpy as np

import concourse.bass as bass
from concourse import mybir

f32 = mybir.dt.float32
f32r = mybir.dt.float32r
bf16 = mybir.dt.bfloat16
ALU = mybir.AluOpType
ACT = mybir.ActivationFunctionType

P = 128
BATCH, SEQ, MODEL, INNER, STATES, TAPS = 4, 1024, 512, 1024, 16, 4
HEADS = 16
HD = MODEL // HEADS
NM, NQ, NK, NH = INNER // P, SEQ // P, MODEL // P, SEQ // 512
HALF = INNER // 2

START = 2


def start_counts(engine, semaphores):
    for s in semaphores:
        engine.sem_inc(s, START)


def pre_phase(nc, I, Xp, Xn, Bp, Ad, Cm):
    ALL = 3 * STATES
    with ExitStack() as ctx:
        sb = lambda n, s, d=f32: ctx.enter_context(nc.sbuf_tensor("a_" + n, s, d))
        pb = lambda n, s, d=f32: ctx.enter_context(nc.psum_tensor("a_" + n, s, d))
        sems = []
        def sem(n):
            sems.append(nc.alloc_semaphore(name="a_" + n))
            return sems[-1]
        w_in = sb("w_in", [P, NK, INNER]); x_t = sb("x_t", [P, NK, SEQ])
        temb = sb("temb", [P, NM]); w_conv = sb("w_conv", [P, NM, TAPS]); b_conv = sb("b_conv", [P, NM])
        ln_g = sb("ln_g", [P, INNER]); ln_b = sb("ln_b", [P, INNER])
        w_xp = sb("w_xp", [P, NM, ALL]); w_dt = sb("w_dt", [ALL, 64])
        b_dt = sb("b_dt", [STATES, 1]); a_log = sb("a_log", [STATES, 1]); neg_a = sb("neg_a", [STATES, 1])
        ident = sb("ident", [P, P]); idle = sb("idle", [P, NQ])
        padded = sb("padded", [P, 2, TAPS - 1 + SEQ]); acc = sb("acc", [P, 2, SEQ]); xc_t = sb("xc_t", [P, NM, SEQ])
        stats = sb("stats", [P, NQ, 2, 6]); mv = sb("mv", [P, NQ, 2]); var_eps = sb("var_eps", [P, NQ]); std = sb("std", [P, NQ])
        rstd = sb("rstd", [P, NQ]); nmr = sb("nmr", [P, NQ])
        xn = sb("xn", [P, NQ, INNER])
        x1 = sb("x1", [P, 2, INNER], bf16); r1 = sb("r1", [P, 2, INNER]); x2 = sb("x2", [P, 2, INNER], bf16); x3 = sb("x3", [P, 2, INNER], bf16)
        square = sb("square", [P, INNER]); sumsq = sb("sumsq", [P, NQ])
        xn_t = sb("xn_t", [P, 2, NM, P]); xproj = sb("xproj", [P, NQ, P])
        ssm = sb("ssm", [P, NQ]); root = sb("root", [P, NQ]); geq = sb("geq", [P, NQ]); nrm = sb("nrm", [P, NQ])
        bd = sb("bd", [P, NQ, STATES]); b1 = sb("b1", [P, NQ, STATES], bf16); br1 = sb("br1", [P, NQ, STATES]); b2 = sb("b2", [P, NQ, STATES], bf16); b3 = sb("b3", [P, NQ, STATES], bf16)
        proj_t = sb("proj_t", [ALL, SEQ]); th = sb("th", [STATES, SEQ]); ad = sb("ad", [STATES, SEQ])
        pa = [pb(f"pa{i}", [P, 1024]) for i in range(2)]
        pt = pb("pt", [P, 1024]); px = pb("px", [P, 512])
        consts = sem("consts"); a_ready = sem("a_ready"); x_in = sem("x_in"); s_xr = sem("s_xr"); s_ev = sem("s_ev"); s_tap = sem("s_tap"); s_conv = sem("s_conv"); s_xc = sem("s_xc")
        s_ta = sem("s_ta"); s_cx = sem("s_cx"); s_st = sem("s_st"); s_mv = sem("s_mv"); s_ve = sem("s_ve"); s_sd = sem("s_sd"); s_nm = sem("s_nm"); s_n0 = sem("s_n0"); s_xg = sem("s_xg"); s_xn = sem("s_xn")
        s_x1 = sem("s_x1"); s_ss = sem("s_ss"); s_r1 = sem("s_r1"); s_x2 = sem("s_x2"); s_x3 = sem("s_x3"); s_tb = sem("s_tb"); s_xnt = sem("s_xnt"); s_xp = sem("s_xp"); s_xe = sem("s_xe")
        o_xn = [sem(f"o_xn{i}") for i in range(2)]; o_x1 = [sem(f"o_x1{i}") for i in range(2)]
        o_x2 = [sem(f"o_x2{i}") for i in range(2)]; o_x3 = [sem(f"o_x3{i}") for i in range(2)]
        s_t3 = sem("s_t3"); s_c3 = sem("s_c3"); s_mm3 = sem("s_mm3"); s_th = sem("s_th"); s_ad = sem("s_ad"); s_rt = sem("s_rt"); s_v3 = sem("s_v3"); s_b1 = sem("s_b1"); o_3 = sem("o_3")

        def load_batch(sp, n):
            sp.dma_start(x_t[:], I["x_t"][bass.ds(n, 1)].rearrange("o (k p) t -> p (o k) t", p=P)).then_inc(x_in, 16)
            sp.dma_start(temb[:], I["t_emb"][bass.ds(n, 1)].rearrange("o (m p) -> p (o m)", p=P), allow_slow_non_contiguous=True).then_inc(x_in, 16)

        with nc.Block() as block:
            @block.sync
            def _(sp):
                start_counts(sp, sems)
                load_batch(sp, 0)
                for dst, src in ((w_in[:], I["w_in_t"][:, 0:INNER].rearrange("(k p) n -> p k n", p=P)),
                                 (w_conv[:], I["w_conv"].rearrange("(m p) o j -> p m (o j)", p=P)),
                                 (b_conv[:], I["b_conv"].rearrange("(m p) -> p m", p=P)),
                                 (ln_g[:], I["ln_g"].rearrange("(o n) -> o n", o=1).to_broadcast([P, INNER])),
                                 (ln_b[:], I["ln_b"].rearrange("(o n) -> o n", o=1).to_broadcast([P, INNER])),
                                 (w_xp[:], I["w_xproj_t"].rearrange("(m p) n -> p m n", p=P)),
                                 (w_dt[2 * STATES:ALL, :], I["w_dt_t"]), (b_dt[:], I["b_dt"].rearrange("(p o) -> p o", o=1)), (a_log[:], I["a_log"].rearrange("(p o) -> p o", o=1)),
                                 (ident[:], I["ident"])):
                    sp.dma_start(dst, src, allow_slow_non_contiguous=True).then_inc(consts, 16)
                sp.wait_ge(consts, START + 160)
            @block.vector
            def _(dve):
                nc.vector.memset(padded[:, :, 0:TAPS - 1], 0.0)
                nc.vector.memset(xproj[:, :, ALL:P], 0.0)
                dve.wait_ge(s_th, START + 1)
                nc.vector.tensor_scalar(out=neg_a[:], in0=neg_a[:], scalar1=-0.01, scalar2=None, op0=ALU.mult).then_inc(a_ready, 1)
            @block.scalar
            def _(act):
                act.wait_ge(consts, START + 160)
                nc.scalar.activation(neg_a[:], a_log[:], ACT.Tanh).then_inc(s_th, 1)

        def sp_part(sp, n, p, more):
            if p is not None:
                xp_b = Xp.rearrange("(i h b) (t c) -> b i t h c", i=3, h=2, c=HALF)[bass.ds(p, 1)].rearrange("o i t h c -> i (o t) h c")
            for s in range(NQ + 1):
                q = s
                if p is not None and q < NQ:
                    sp.wait_ge(s_xn, START + p * NQ + q + 1)
                    sp.dma_start(Xn[bass.ds(p, 1)].rearrange("o t c -> (o t) c")[q * P:(q + 1) * P, :], xn[:, q, :]).then_inc(o_xn[q % 2], 16)
                    sp.wait_ge(s_x1, START + p * NQ + q + 1)
                    sp.dma_start(xp_b[0][q * P:(q + 1) * P], x1[:, q % 2, :].rearrange("p (h c) -> p h c", h=2)).then_inc(o_x1[q % 2], 16)
                if s == NQ and more:
                    sp.wait_ge(s_xr, START + n * NM + NM)
                    sp.wait_ge(s_ev, START + n * NM + NM)
                    load_batch(sp, n + 1)
                q = s - 1
                if p is not None and q >= 0:
                    sp.wait_ge(s_x2, START + p * NQ + q + 1)
                    sp.dma_start(xp_b[1][q * P:(q + 1) * P], x2[:, q % 2, :].rearrange("p (h c) -> p h c", h=2)).then_inc(o_x2[q % 2], 16)
                    sp.wait_ge(s_x3, START + p * NQ + q + 1)
                    sp.dma_start(xp_b[2][q * P:(q + 1) * P], x3[:, q % 2, :].rearrange("p (h c) -> p h c", h=2)).then_inc(o_x3[q % 2], 16)
            if p is not None:
                sp.wait_ge(s_c3, START + p + 1)
                sp.dma_start(Cm[bass.ds(p * STATES, STATES), :], proj_t[STATES:2 * STATES, :]).then_inc(o_3, 16)
                bp = Bp[:, bass.ds(p, 1)].rearrange("i o (q t) d -> i t (o q) d", t=P)
                sp.wait_ge(s_b1, START + p * 3 + 3)
                for j, t in enumerate((b1, b2, b3)):
                    sp.dma_start(bp[j], t[:]).then_inc(o_3, 16)
                sp.wait_ge(s_ad, START + p + 1)
                sp.dma_start(Ad[bass.ds(p * STATES, STATES), :], ad[:]).then_inc(o_3, 16)

        def pe_part(pe, n, p):
            for s in range(NQ + 1):
                if n is not None and s < NM:
                    m = s
                    if m == 0:
                        pe.wait_ge(x_in, START + n * 32 + 32)
                    if m < 2:
                        pe.wait_ge(s_cx, START + n * NQ)
                    else:
                        pe.wait_ge(s_ev, START + n * NM + m - 1)
                    for h in range(NH):
                        for k in range(NK):
                            mm = nc.tensor.matmul(pa[m % 2][:, h * 512:h * 512 + 512], w_in[:, k, m * P:(m + 1) * P], x_t[:, k, h * 512:h * 512 + 512], start=(k == 0), stop=(k == NK - 1))
                    mm.then_inc(s_xr, 1)
                q = s
                if p is not None and q < NQ:
                    pe.wait_ge(s_xn, START + p * NQ + q + 1)
                    if q == 0:
                        pe.wait_ge(s_th, START + p + 1)
                    else:
                        pe.wait_ge(s_xnt, START + p * NQ + q)
                    for m in range(NM):
                        mm = nc.tensor.transpose(pt[:, m * P:(m + 1) * P], xn[:, q, m * P:(m + 1) * P], ident[:])
                    mm.then_inc(s_tb, 1)
                q = s - 1
                if p is not None and q >= 0:
                    pe.wait_ge(s_xnt, START + p * NQ + q + 1)
                    pe.wait_ge(s_xe, START + p * NQ + q)
                    for m in range(NM):
                        mm = nc.tensor.matmul(px[:, 0:ALL], xn_t[:, q % 2, m, :], w_xp[:, m, :], start=(m == 0), stop=(m == NM - 1))
                    mm.then_inc(s_xp, 1)
            if p is not None:
                pe.wait_ge(s_xe, START + p * NQ + NQ)
                for q in range(NQ):
                    mm = nc.tensor.transpose(pt[:, q * P:(q + 1) * P], xproj[:, q, :], ident[:])
                mm.then_inc(s_t3, 1)
            if n is not None:
                pe.wait_ge(s_xc, START + n * NM + NM)
                for q in range(NQ):
                    if q >= 2:
                        pe.wait_ge(s_cx, START + n * NQ + q - 1)
                    for m in range(NM):
                        mm = nc.tensor.transpose(pa[q % 2][:, m * P:(m + 1) * P], xc_t[:, m, q * P:(q + 1) * P], ident[:])
                    mm.then_inc(s_ta, 1)
            if p is not None:
                pe.wait_ge(s_c3, START + p + 1)
                for h in range(NH):
                    mm = nc.tensor.matmul(pt[0:64, h * 512:h * 512 + 512], w_dt[2 * STATES:ALL, :], proj_t[2 * STATES:ALL, h * 512:h * 512 + 512], start=True, stop=True)
                mm.then_inc(s_mm3, 1)

        def act_part(act, n, p):
            for s in range(NQ + 2):
                q = s
                if p is not None and q < NQ:
                    act.wait_ge(s_nm, START + p * 2 + 2)
                    nc.scalar.activation(xn[:, q, :], xn[:, q, :], ACT.Identity, bias=nmr[:, q:q + 1], scale=rstd[:, q:q + 1]).then_inc(s_n0, 1)
                q = s - 1
                if p is not None and 0 <= q < NQ:
                    act.wait_ge(s_r1, START + p * NQ + q + 1)
                    act.wait_ge(o_x2[q % 2], START + p * 64 + 16 * (q // 2))
                    act.wait_ge(s_x3, START + p * NQ + max(q - 1, 0))
                    nc.scalar.copy(x2[:, q % 2, :], r1[:, q % 2, :]).then_inc(s_x2, 1)
                m = s - 1
                if n is not None and 0 <= m < NM:
                    act.wait_ge(s_conv, START + n * (3 * NM) + 3 * m + 3)
                    nc.scalar.activation(xc_t[:, m, :], acc[:, m % 2, :], ACT.Silu).then_inc(s_xc, 1)
                q = s - 2
                if p is not None and q >= 0:
                    act.wait_ge(s_xp, START + p * NQ + q + 1)
                    nc.scalar.copy(xproj[:, q, 0:ALL], px[:, 0:ALL]).then_inc(s_xe, 1)
                m = s
                if n is not None and m < NM:
                    act.wait_ge(s_xr, START + n * NM + m + 1)
                    if m >= 2:
                        act.wait_ge(s_conv, START + n * (3 * NM) + 3 * (m - 1))
                    nc.scalar.activation(padded[:, m % 2, TAPS - 1:], pa[m % 2][:], ACT.Identity, bias=temb[:, m:m + 1]).then_inc(s_ev, 1)
                    act.wait_ge(s_ev, START + n * NM + m + 1)
                    nc.scalar.activation(acc[:, m % 2, :], padded[:, m % 2, TAPS - 1:], ACT.Identity, bias=b_conv[:, m:m + 1], scale=w_conv[:, m, TAPS - 1:TAPS]).then_inc(s_tap, 1)
                q = s
                if p is not None and q < NQ:
                    act.wait_ge(s_xn, START + p * NQ + q + 1)
                    act.wait_ge(o_x1[q % 2], START + p * 64 + 16 * (q // 2))
                    nc.scalar.copy(x1[:, q % 2, :], xn[:, q, :]).then_inc(s_x1, 1)
                    act.wait_ge(s_ss, START + p * NQ + q)
                    nc.scalar.activation(square[:], xn[:, q, :], ACT.Square, accum_out=sumsq[:, q:q + 1]).then_inc(s_ss, 1)
            if p is not None:
                act.wait_ge(s_t3, START + p + 1)
                act.wait_ge(o_3, START + p * 80)
                nc.scalar.copy(proj_t[:], pt[0:ALL, :]).then_inc(s_c3, 1)
            if n is not None:
                for q in range(NQ):
                    act.wait_ge(s_ta, START + n * NQ + q + 1)
                    if p is not None:
                        act.wait_ge(o_xn[q % 2], START + n * 64)
                        act.wait_ge(s_r1, START + n * NQ)
                    nc.scalar.copy(xn[:, q, :], pa[q % 2][:]).then_inc(s_cx, 1)
                act.wait_ge(s_ve, START + n + 1)
                nc.scalar.activation(std[:], var_eps[:], ACT.Sqrt).then_inc(s_sd, 1)
            if p is not None:
                act.wait_ge(s_v3, START + p * 6 + 2)
                nc.scalar.activation(root[:], ssm[:], ACT.Sqrt).then_inc(s_rt, 1)
                act.wait_ge(s_mm3, START + p + 1)
                act.wait_ge(s_ad, START + p)
                nc.scalar.activation(th[:], pt[0:STATES, :], ACT.Tanh, bias=b_dt[:]).then_inc(s_th, 1)

        def pool_part(pool, p):
            for s in range(NQ + 1):
                q = s
                if q < NQ:
                    pool.wait_ge(s_n0, START + p * NQ + q + 1)
                    nc.gpsimd.tensor_tensor(out=xn[:, q, :], in0=xn[:, q, :], in1=ln_g[:], op=ALU.mult).then_inc(s_xg, 1)
                q = s - 1
                if q >= 0:
                    pool.wait_ge(s_x2, START + p * NQ + q + 1)
                    pool.wait_ge(o_x3[q % 2], START + p * 64 + 16 * (q // 2))
                    nc.gpsimd.tensor_tensor(out=x3[:, q % 2, :], in0=r1[:, q % 2, :], in1=x2[:, q % 2, :], op=ALU.subtract).then_inc(s_x3, 1)

        def dve_part(dve, n, p):
            for s in range(NQ):
                q = m = s
                if p is not None:
                    dve.wait_ge(s_xg, START + p * NQ + q + 1)
                    nc.vector.tensor_tensor(out=xn[:, q, :], in0=xn[:, q, :], in1=ln_b[:], op=ALU.add).then_inc(s_xn, 1)
                if n is not None:
                    dve.wait_ge(s_tap, START + n * NM + m + 1)
                    for j in range(TAPS - 1):
                        if j:
                            dve.wait_ge(s_conv, START + n * (3 * NM) + 3 * m + j)
                        nc.vector.scalar_tensor_tensor(out=acc[:, m % 2, :], in0=padded[:, m % 2, j:j + SEQ], scalar=w_conv[:, m, j:j + 1], in1=acc[:, m % 2, :],
                                                       op0=ALU.mult, op1=ALU.add).then_inc(s_conv, 1)
                if p is not None:
                    dve.wait_ge(s_x1, START + p * NQ + q + 1)
                    dve.wait_ge(s_x3, START + p * NQ + max(q - 1, 0))
                    nc.vector.tensor_tensor(out=r1[:, q % 2, :], in0=xn[:, q, :], in1=x1[:, q % 2, :], op=ALU.subtract).then_inc(s_r1, 1)
                    dve.wait_ge(s_tb, START + p * NQ + q + 1)
                    dve.wait_ge(s_xp, START + p * NQ + max(q - 1, 0))
                    nc.vector.tensor_copy(out=xn_t[:, q % 2], in_=pt[:].rearrange("p (m t) -> p m t", m=NM)).then_inc(s_xnt, 1)
            if p is not None:
                dve.wait_ge(s_ss, START + p * NQ + NQ)
                nc.vector.tensor_scalar(out=ssm[:], in0=sumsq[:], scalar1=1.0, scalar2=None, op0=ALU.min).then_inc(s_v3, 1)
                nc.vector.tensor_scalar(out=geq[:], in0=sumsq[:], scalar1=1.0, scalar2=None, op0=ALU.is_ge).then_inc(s_v3, 1)
            if n is not None:
                for s in range(NQ + 1):
                    q = s
                    if q < NQ:
                        dve.wait_ge(s_cx, START + n * NQ + q + 1)
                        for h in range(2):
                            nc.vector.bn_stats(out=stats[:, q, h, :], in_=xn[:, q, h * 512:h * 512 + 512]).then_inc(s_st, 1)
                    q = s - 1
                    if q >= 0:
                        dve.wait_ge(s_st, START + n * (2 * NQ) + 2 * q + 2)
                        nc.vector.memset(idle[:, q:q + 1], 0.0)
                        nc.vector.bn_aggr(out=mv[:, q, :], in_=stats[:, q]).then_inc(s_mv, 1)
                dve.wait_ge(s_mv, START + n * NQ + NQ)
                nc.vector.tensor_scalar(out=var_eps[:], in0=mv[:, :, 1], scalar1=1e-5, scalar2=None, op0=ALU.add).then_inc(s_ve, 1)
                dve.wait_ge(s_sd, START + n + 1)
                nc.vector.reciprocal(out=rstd[:], in_=std[:]).then_inc(s_nm, 1)
                dve.wait_ge(s_nm, START + n * 2 + 1)
                nc.vector.scalar_tensor_tensor(out=nmr[:], in0=mv[:, :, 0], scalar=-1.0, in1=rstd[:], op0=ALU.mult, op1=ALU.mult).then_inc(s_nm, 1)
            if p is not None:
                dve.wait_ge(s_rt, START + p + 1)
                nc.vector.tensor_tensor(out=nrm[:], in0=root[:], in1=geq[:], op=ALU.max).then_inc(s_v3, 1)
                dve.wait_ge(s_v3, START + p * 6 + 3)
                nc.vector.tensor_scalar(out=nrm[:], in0=nrm[:], scalar1=1.0, scalar2=None, op0=ALU.min).then_inc(s_v3, 1)
                dve.wait_ge(s_v3, START + p * 6 + 4)
                dve.wait_ge(s_xe, START + p * NQ + NQ)
                dve.wait_ge(o_3, START + p * 80)
                nc.vector.tensor_tensor(out=bd[:], in0=xproj[:, :, 0:STATES], in1=nrm[:].rearrange("p (q o) -> p q o", o=1).to_broadcast([P, NQ, STATES]), op=ALU.mult).then_inc(s_v3, 1)
                dve.wait_ge(s_v3, START + p * 6 + 5)
                nc.vector.tensor_copy(out=b1[:], in_=bd[:]).then_inc(s_b1, 1)
                dve.wait_ge(s_b1, START + p * 3 + 1)
                nc.vector.tensor_tensor(out=br1[:], in0=bd[:], in1=b1[:], op=ALU.subtract).then_inc(s_v3, 1)
                dve.wait_ge(s_v3, START + p * 6 + 6)
                nc.vector.tensor_copy(out=b2[:], in_=br1[:]).then_inc(s_b1, 1)
                dve.wait_ge(s_b1, START + p * 3 + 2)
                nc.vector.tensor_tensor(out=b3[:], in0=br1[:], in1=b2[:], op=ALU.subtract).then_inc(s_b1, 1)
                dve.wait_ge(s_th, START + p + 2)
                nc.vector.tensor_scalar(out=ad[:], in0=th[:], scalar1=neg_a[:], scalar2=1.0, op0=ALU.mult, op1=ALU.add).then_inc(s_ad, 1)

        def batches(e, part):
            part(e, 0, None)
            with e.Fori(1, BATCH) as n:
                part(e, n, n - 1)
            part(e, None, BATCH - 1)

        with nc.Block() as block:
            @block.sync
            def _(sp):
                sp_part(sp, 0, None, True)
                with sp.Fori(1, BATCH - 1) as n:
                    sp_part(sp, n, n - 1, True)
                sp_part(sp, BATCH - 1, BATCH - 2, False)
                sp_part(sp, None, BATCH - 1, False)
                sp.wait_ge(o_3, START + 80 * BATCH)
                for t in o_xn + o_x1 + o_x2 + o_x3:
                    sp.wait_ge(t, START + 64 * BATCH)
            @block.tensor
            def _(pe):
                batches(pe, pe_part)
            @block.scalar
            def _(act):
                batches(act, act_part)
            @block.gpsimd
            def _(pool):
                with pool.Fori(0, BATCH) as p:
                    pool_part(pool, p)
            @block.vector
            def _(dve):
                batches(dve, dve_part)
        return sems


def scan_phase(nc, I, Xp, Xn, Bp, Ad, Cm, Y, SG, X1, used_before):
    T = 16
    STEPS = 2 * T
    LOOPS = SEQ // STEPS
    ROWS = 2 * BATCH
    K = 6 * ROWS
    RING = 4
    LAG = P // STEPS
    assert LOOPS == BATCH * NQ and LAG == BATCH
    GC = 256
    gate_pieces = [("gate", h, n, k) for h in range(2) for n in range(HALF // GC) for k in range(NK)]
    turn_pieces = [("turn", g, i) for g in range(2) for i in range(2)]
    out_pieces = [("out", n, m) for n in range(MODEL // GC) for m in range(NM)]
    PIECES = gate_pieces[:-2] + turn_pieces[:2] + gate_pieces[-2:] + turn_pieces[2:] + out_pieces
    AT = [[p for c, p in enumerate(PIECES) if c * STEPS // len(PIECES) == u] for u in range(STEPS)]
    AHEAD = STEPS
    with ExitStack() as ctx:
        sb = lambda n, s, d: ctx.enter_context(nc.sbuf_tensor("b_" + n, s, d))
        pb = lambda n, s, d: ctx.enter_context(nc.psum_tensor("b_" + n, s, d))
        sems = []
        def sem(n):
            sems.append(ctx.enter_context(nc.semaphore("b_" + n)))
            return sems[-1]
        bd_all = sb("bd_all", [K, SEQ * STATES], bf16)
        decay_all = sb("decay_all", [128, SEQ], f32)
        c_all = sb("c_all", [128, SEQ], f32)
        mask_b = sb("mask_b", [K, 128], f32)
        mask_c = sb("mask_c", [128, T, 32], f32)
        x_moving = sb("x_moving", [K, 2, T * HALF], bf16)
        b_weights = sb("b_weights", [K, 2, T, 128], bf16)
        c_weights = sb("c_weights", [128, 2, T, 32], f32)
        decay = sb("decay", [128, 2, T], f32)
        z = sb("z", [128, HALF], f32)
        h = sb("h", [128, RING, HALF], f32)
        y_stage = sb("y_stage", [128, 2, T // 4, 128], f32)
        zeros = sb("zeros", [K, HALF], bf16)
        w_gate = sb("w_gate", [128, NK, INNER], f32); x_tile = sb("x_tile", [128, NK, 128], f32); sg = sb("sg", [128, 2, HALF], f32)
        w_out = sb("w_out", [P, NM, MODEL], f32); d_row = sb("d_row", [P, INNER], f32); ident = sb("ident", [P, P], f32)
        xn = sb("xn", [P, INNER], f32); y = sb("y", [P, INNER], f32); sg_in = sb("sg_in", [P, INNER], f32); yg = sb("yg", [P, INNER], f32)
        yg_t = sb("yg_t", [P, NM, P], f32); x = sb("x", [P, MODEL], f32); o = sb("o", [P, MODEL], f32); x1 = sb("x1", [P, MODEL], f32)
        p_turn = pb("p_turn", [P, HALF], f32); p_out = pb("p_out", [P, MODEL], f32)
        gate = [pb(f"gate{i}", [128, HALF], f32) for i in range(2)]
        bx = [pb(f"bx{i}", [128, HALF], f32) for i in range(2)]
        y_psum = [pb(f"y_psum{i}", [128, 512], f32) for i in range(2)]
        tile_in = sem("tile_in"); gate_ready = sem("gate_ready"); gate_taken = sem("gate_taken"); sg_out = [sem(f"sg_out{i}") for i in range(2)]
        xn_in = sem("xn_in"); y_in = sem("y_in"); res_in = sem("res_in"); mixed = sem("mixed"); gated = sem("gated"); turned = sem("turned"); turned_taken = sem("turned_taken")
        out_ready = sem("out_ready"); out_taken = sem("out_taken"); x1_ready = sem("x1_ready"); x1_out = sem("x1_out")
        consts_in = sem("consts_in"); zeros_ready = sem("zeros_ready")
        x_in = [sem(f"x_in{i}") for i in range(2)]
        w_ready = [sem(f"w_ready{i}") for i in range(2)]
        bx_ready = sem("bx_ready")
        z_ready = sem("z_ready")
        h_ready = sem("h_ready")
        read = sem("read")
        y_free = sem("y_free")
        y_out = [sem(f"y_out{i}") for i in range(2)]

        with nc.Block() as block:
            @block.sync
            def _(sp):
                start_counts(sp, sems)
                sp.dma_start(mask_b[:], I["mask_b"]).then_inc(consts_in, 16)
                sp.dma_start(mask_c[:], I["mask_c"]).then_inc(consts_in, 16)
                for half in range(2):
                    sp.dma_start(c_all[64 * half:64 * half + 64, :], Cm).then_inc(consts_in, 16)
                    sp.dma_start(decay_all[64 * half:64 * half + 64, :], Ad).then_inc(consts_in, 16)
                row = 0
                for part, copies in ((0, 3), (1, 2), (2, 1)):
                    for _ in range(2 * copies):
                        sp.dma_start(bd_all[row:row + BATCH, :], Bp[part].rearrange("b t d -> b (t d)")).then_inc(consts_in, 16)
                        row += BATCH
                sp.dma_start(w_gate[:], I["w_in_t"][:, INNER:2 * INNER].rearrange("(k p) n -> p k n", p=128)).then_inc(consts_in, 16)
                sp.dma_start(w_out[:], I["w_out_t"].rearrange("(m p) n -> p m n", p=P)).then_inc(consts_in, 16)
                sp.dma_start(d_row[:], I["D"].rearrange("(o n) -> o n", o=1).to_broadcast([P, INNER])).then_inc(consts_in, 16)
                sp.dma_start(ident[:], I["ident"]).then_inc(consts_in, 16)
                sp.wait_ge(consts_in, START + 22 * 16)
            @block.vector
            def _(dve):
                nc.vector.memset(zeros[:], 0.0).then_inc(zeros_ready, 1)
                nc.vector.memset(h[:, RING - 1, :], 0.0).then_inc(zeros_ready, 1)
                nc.vector.memset(c_weights[:, 1, T - 1, :], 0.0).then_inc(zeros_ready, 1)
            @block.tensor
            def _(pe):
                pe.wait_ge(zeros_ready, START + 3)
                nc.tensor.matmul(y_psum[0][:], zeros[:, 0:128], zeros[:], start=True, stop=True).then_inc(read, AHEAD)
                nc.tensor.matmul(y_psum[1][:], zeros[:, 0:128], zeros[:], start=True, stop=True).then_inc(y_free, 1)

        nc.clear_and_free_semaphores(used_before)
        def load_mixed(sp, j, tq, b):
            sp.wait_ge(gated, START + j)
            sp.dma_start(xn[:], Xn[b, bass.ds(tq * P, P), :]).then_inc(xn_in, 16)
            for half in range(2):
                sp.wait_ge(sg_out[half], START + j * 16 + 16)
            sp.dma_start(sg_in[:], SG[bass.ds(j, 1)].rearrange("o p c -> (o p) c")).then_inc(xn_in, 16)
        def load_y(sp, j, tq, b, it):
            for i in range(2):
                sp.wait_ge(y_out[i], START + it * 64)
            sp.dma_start(y[:], Y[bass.ds(tq * P, P)].rearrange("t (h b) c -> b t h c", h=2)[b]).then_inc(y_in, 16)
        def load_x(sp, j, tq, b):
            sp.wait_ge(x1_ready, START + j)
            sp.dma_start(x[:], I["x"][b, bass.ds(tq * P, P), :]).then_inc(res_in, 16)
        def store_x1(sp, j):
            sp.wait_ge(x1_ready, START + j + 1)
            sp.dma_start(X1[bass.ds(j, 1)].rearrange("o p c -> (o p) c"), x1[:]).then_inc(x1_out, 16)

        def mix(e, engine, j):
            e.wait_ge(xn_in, START + j * 32 + 32)
            engine.tensor_tensor(out=xn[:], in0=xn[:], in1=d_row[:], op=ALU.mult).then_inc(mixed, 1)
            e.wait_ge(mixed, START + j * 2 + 1)
            e.wait_ge(y_in, START + j * 16 + 16)
            engine.tensor_tensor(out=xn[:], in0=xn[:], in1=y[:], op=ALU.add).then_inc(mixed, 1)
            e.wait_ge(mixed, START + j * 2 + 2)
            e.wait_ge(turned, START + j * 2)
            engine.tensor_tensor(out=yg[:], in0=xn[:], in1=sg_in[:], op=ALU.mult).then_inc(gated, 1)
        def add_x(e, engine, j):
            e.wait_ge(out_taken, START + j + 1)
            e.wait_ge(res_in, START + j * 16 + 16)
            e.wait_ge(x1_out, START + j * 16)
            engine.tensor_tensor(out=x1[:], in0=x[:], in1=o[:], op=ALU.add).then_inc(x1_ready, 1)

        def piece_of(pe, it, j, piece):
            if piece[0] == "gate":
                _, half, n, k = piece
                if piece == gate_pieces[0]:
                    pe.wait_ge(tile_in, START + it * 16 + 16)
                    pe.wait_ge(gate_taken, START + it * 2)
                c = half * HALF + n * GC
                mm = nc.tensor.matmul(gate[half][:, n * GC:(n + 1) * GC], x_tile[:, k, :], w_gate[:, k, c:c + GC], start=(k == 0), stop=(k == NK - 1))
                if n == HALF // GC - 1 and k == NK - 1:
                    mm.then_inc(gate_ready, 1)
            elif j is None:
                return
            elif piece[0] == "turn":
                _, g, i = piece
                if (g, i) == (0, 0):
                    pe.wait_ge(gated, START + j + 1)
                if (g, i) == (1, 0):
                    pe.wait_ge(turned_taken, START + j * 2 + 1)
                for m in (2 * i, 2 * i + 1):
                    mm = nc.tensor.transpose(p_turn[:, m * P:(m + 1) * P], yg[:, (4 * g + m) * P:(4 * g + m + 1) * P], ident[:])
                if i == 1:
                    mm.then_inc(turned, 1)
            else:
                _, n, m = piece
                if n == 0 and m % 4 == 0:
                    pe.wait_ge(turned_taken, START + j * 2 + m // 4 + 1)
                if (n, m) == (0, 0):
                    pe.wait_ge(out_taken, START + j)
                mm = nc.tensor.matmul(p_out[:, n * GC:(n + 1) * GC], yg_t[:, m, :], w_out[:, m, n * GC:(n + 1) * GC], start=(m == 0), stop=(m == NM - 1))
                if piece == out_pieces[-1]:
                    mm.then_inc(out_ready, 1)

        def take_gate(act, it, half):
            act.wait_ge(gate_ready, START + it * 2 + half + 1)
            act.wait_ge(sg_out[half], START + it * 16)
            nc.scalar.activation(sg[:, half, :], gate[half][:], ACT.Silu).then_inc(gate_taken, 1)
            act.wait_ge(gate_taken, START + it * 2 + half + 1)
            act.dma_start(SG[bass.ds(it, 1)].rearrange("o p c -> (o p) c")[:, half * HALF:(half + 1) * HALF], sg[:, half, :]).then_inc(sg_out[half], 16)
        def take_turned(act, j, g):
            act.wait_ge(turned, START + j * 2 + g + 1)
            act.wait_ge(out_ready, START + j)
            nc.scalar.copy(yg_t[:, 4 * g:4 * g + 4, :], p_turn[:].rearrange("p (m t) -> p m t", m=4)).then_inc(turned_taken, 1)
        def take_out(act, j):
            act.wait_ge(out_ready, START + j + 1)
            act.wait_ge(x1_ready, START + j)
            nc.scalar.copy(o[:], p_out[:]).then_inc(out_taken, 1)

        def sp_loop(sp, it, j, tq=None, b=None, out=False):
            for i in range(2):
                sp.wait_ge(read, START + it * STEPS + (AHEAD - 15 if i == 0 else AHEAD + 1))
                t0 = it * STEPS + i * T
                for row, parts in ((0, 3), (24, 2), (40, 1)):
                    src = Xp[0:parts * ROWS, bass.ds(t0 * HALF, T * HALF)]
                    sp.dma_start(x_moving[row:row + parts * ROWS, i, :], src).then_inc(x_in[i], 16)
                if i == 0:
                    sp.wait_ge(gate_ready, START + it * 2)
                    sp.dma_start(x_tile[:], I["x_tiles"][bass.ds(it, 1)].rearrange("o p k t -> (o p) k t")).then_inc(tile_in, 16)
                    if j is not None:
                        load_mixed(sp, j, tq, b)
            if j is not None:
                load_y(sp, j, tq, b, it)
                if out:
                    store_x1(sp, j + (-1))
                load_x(sp, j, tq, b)

        def pool_loop(pool, it, j, out=False):
            for i in range(2):
                t0 = it * STEPS + i * T
                pool.wait_ge(read, START + it * STEPS + (AHEAD - 15 if i == 0 else AHEAD + 1))
                bd = bd_all[:, bass.ds(t0 * STATES, T * STATES)].rearrange("k (t o d) -> k t o d", o=1, d=STATES).to_broadcast([K, T, 8, STATES])
                mb = mask_b[:].rearrange("k (o r d) -> k o r d", o=1, d=STATES).to_broadcast([K, T, 8, STATES])
                nc.gpsimd.tensor_tensor(out=b_weights[:, i].rearrange("k t (r d) -> k t r d", d=STATES), in0=bd, in1=mb, op=ALU.mult).then_inc(w_ready[i], 1)
                cc = c_all[:, bass.ds(t0, T)].rearrange("p (t o) -> p t o", o=1).to_broadcast([128, T, 32])
                nc.gpsimd.tensor_tensor(out=c_weights[:, i], in0=cc, in1=mask_c[:], op=ALU.mult).then_inc(w_ready[i], 1)
                nc.gpsimd.tensor_copy(out=decay[:, i], in_=decay_all[:, bass.ds(t0, T)]).then_inc(w_ready[i], 1)
            if out:
                add_x(pool, nc.gpsimd, j + (-1))
            if j is not None:
                mix(pool, nc.gpsimd, j)

        def readout(pe, it, u):
            i, tt = (u // T) % 2, u % T
            pe.wait_ge(h_ready, START + it * (2 * STEPS) + 2 * (u + 1))
            if u % 4 == 0:
                pe.wait_ge(y_free, START + it * (STEPS // 4) + u // 4)
            for j in range(4):
                m = nc.tensor.matmul(y_psum[(u // 4) % 2][32 * j:32 * j + 32, 0:128], c_weights[:, i, tt, :],
                                     h[:, u % RING, 128 * j:128 * j + 128], start=(u % 4 == 0), stop=(u % 4 == 3), skip_group_check=True)
            m.then_inc(read, 1)

        def pe_loop(pe, it, j):
            for u in range(STEPS):
                i, tt = u // T, u % T
                if tt == 0:
                    pe.wait_ge(x_in[i], START + it * 48 + 48)
                    pe.wait_ge(w_ready[i], START + it * 3 + 3)
                if u == 0 or u == 1:
                    pe.wait_ge(h_ready, START + it * (2 * STEPS) + 2 * max(u - 1, 0))
                else:
                    pe.wait_ge(z_ready, START + it * (2 * STEPS) + 2 * (u - 1))
                nc.tensor.matmul(bx[u % 2][:], b_weights[:, i, tt, :], x_moving[:, i, tt * HALF:(tt + 1) * HALF],
                                 start=True, stop=True).then_inc(bx_ready, 1)
                for piece in AT[u]:
                    piece_of(pe, it, j, piece)
                readout(pe, it, u - 1)

        def dve_loop(dve, it):
            HW = HALF // 2
            for u in range(STEPS):
                i, tt = u // T, u % T
                if tt == 0:
                    dve.wait_ge(w_ready[i], START + it * 3 + 3)
                dve.wait_ge(bx_ready, START + it * STEPS + (u + 1))
                for g in range(2):
                    c = slice(g * HW, (g + 1) * HW)
                    dve.wait_ge(h_ready, START + it * (2 * STEPS) + max(2 * u - 1 + g, 0))
                    nc.vector.scalar_tensor_tensor(out=z[:, c], in0=h[:, (u - 1) % RING, c], scalar=decay[:, i, tt:tt + 1], in1=bx[u % 2][:, c],
                                                   op0=ALU.mult, op1=ALU.add).then_inc(z_ready, 1)
                dve.wait_ge(read, START + it * STEPS + (AHEAD + u - 2))
                for g in range(2):
                    c = slice(g * HW, (g + 1) * HW)
                    dve.wait_ge(z_ready, START + it * (2 * STEPS) + (2 * u + 1 + g))
                    nc.vector.tensor_scalar(out=h[:, u % RING, c], in0=z[:, c], scalar1=-10.0, scalar2=10.0,
                                            op0=ALU.max, op1=ALU.min).then_inc(h_ready, 1)

        def act_loop(act, it, j):
            for q in range(STEPS // 4):
                i = (4 * q) // T
                act.wait_ge(read, START + it * STEPS + (AHEAD + 4 * q + 5))
                if (4 * q) % T == 0:
                    act.wait_ge(y_out[i], START + it * 64)
                nc.scalar.copy(y_stage[:, i, q % (T // 4), :], y_psum[q % 2][:, 0:128]).then_inc(y_free, 1)
                if (4 * q + 4) % T == 0:
                    act.wait_ge(y_free, START + it * (STEPS // 4) + (q + 2))
                    dst = Y[bass.ds(it * STEPS + i * T, T)].rearrange("(q s) r (j c) -> j (s r) q c", s=4, j=4)
                    for part in range(4):
                        act.dma_start(dst[part], y_stage[32 * part:32 * part + 32, i]).then_inc(y_out[i], 16)
                if q == 1:
                    take_gate(act, it, 0)
                if q == 2 and j is not None:
                    take_turned(act, j, 0)
                if q == 3 and j is not None:
                    take_turned(act, j, 1)
                if q == 4:
                    take_gate(act, it, 1)
                if q == 7 and j is not None:
                    take_out(act, j)

        TILES = BATCH * NQ
        with nc.Block() as block:
            @block.sync
            def _(sp):
                with sp.Fori(0, LAG) as it:
                    sp_loop(sp, it, None)
                for b in range(BATCH):
                    sp_loop(sp, LAG + b, b, 0, b, b > 0)
                with sp.Fori(1, NQ - 1) as tq:
                    for b in range(BATCH):
                        j = tq * BATCH + b
                        sp_loop(sp, j + LAG, j, tq, b, True)
                for b in range(BATCH):
                    j = TILES - LAG + b
                    load_mixed(sp, j, NQ - 1, b)
                    load_y(sp, j, NQ - 1, b, LOOPS)
                    store_x1(sp, j - 1)
                    load_x(sp, j, NQ - 1, b)
                store_x1(sp, TILES - 1)
                sp.wait_ge(x1_out, START + TILES * 16)
            @block.gpsimd
            def _(pool):
                with pool.Fori(0, LAG) as it:
                    pool_loop(pool, it, None)
                pool_loop(pool, LAG, 0)
                with pool.Fori(1, TILES - LAG) as j:
                    pool_loop(pool, j + LAG, j, True)
            @block.tensor
            def _(pe):
                with pe.Fori(0, LAG) as it:
                    pe_loop(pe, it, None)
                with pe.Fori(0, TILES - LAG) as j:
                    pe_loop(pe, j + LAG, j)
                readout(pe, LOOPS, -1)
                with pe.Fori(TILES - LAG, TILES) as j:
                    for piece in turn_pieces + out_pieces:
                        piece_of(pe, None, j, piece)
            @block.vector
            def _(dve):
                with dve.Fori(0, LOOPS) as it:
                    dve_loop(dve, it)
                with dve.Fori(TILES - LAG, TILES) as j:
                    add_x(dve, nc.vector, j + (-1))
                    mix(dve, nc.vector, j)
                add_x(dve, nc.vector, TILES - 1)
            @block.scalar
            def _(act):
                with act.Fori(0, LAG) as it:
                    act_loop(act, it, None)
                with act.Fori(0, TILES - LAG) as j:
                    act_loop(act, j + LAG, j)
                with act.Fori(TILES - LAG, TILES) as j:
                    take_turned(act, j, 0)
                    take_turned(act, j, 1)
                    take_out(act, j)
                for i in range(2):
                    act.wait_ge(y_out[i], START + LOOPS * 64)
                    act.wait_ge(sg_out[i], START + LOOPS * 16)


def proj_phase(nc, I, X1, QK, V, X2, WDC):
    NP = 2 * NK
    STEPS = NQ + NP
    with ExitStack() as ctx:
        sb = lambda n, s, d=f32: ctx.enter_context(nc.sbuf_tensor("d_" + n, s, d))
        pb = lambda n, s, d=f32: ctx.enter_context(nc.psum_tensor("d_" + n, s, d))
        sems = []
        def sem(n):
            sems.append(ctx.enter_context(nc.semaphore("d_" + n)))
            return sems[-1]
        mats = "qkvwu"
        w_u = sb("w_u", [P, NK, MODEL])
        w_hi = {j: sb(f"w_{j}_hi", [P, NK, MODEL], f32r) for j in "qkv"}; w_lo = {j: sb(f"w_{j}_lo", [P, NK, MODEL], f32r) for j in "qkv"}
        ident = sb("ident", [P, P])
        v_rows = sb("v_rows", [P, BATCH, MODEL]); u_row = sb("u_row", [P, MODEL]); s1_row = sb("s1_row", [P, MODEL])
        qk = sb("qk", [P, 2 * NK * BATCH]); qk_col = sb("qk_col", [P, NK * BATCH]); idle = sb("idle", [P, 1])
        pt = pb("pt", [P, MODEL]); pv = pb("pv", [P, MODEL]); pvt = pb("pvt", [P, MODEL]); psk = pb("psk", [P, MODEL])
        pqk = [pb(f"pqk{i}", [P, SEQ]) for i in range(2)]
        consts = sem("consts"); styles = sem("styles"); act_setup = sem("act_setup"); sums = sem("sums"); dve_setup = sem("dve_setup"); rows_in = sem("rows_in"); row_in = sem("row_in")
        x_in = [sem(f"x_in{i}") for i in range(NQ)]
        s_xs = sem("s_xs"); s_st = sem("s_st"); s_mv = sem("s_mv"); s_ve = sem("s_ve"); s_sd = sem("s_sd"); s_nm = sem("s_nm"); s_xl = sem("s_xl")
        s_tp = sem("s_tp"); s_xt = sem("s_xt"); s_lt = sem("s_lt"); s_pv = sem("s_pv"); s_v = sem("s_v"); s_vt = sem("s_vt"); s_vc = sem("s_vc"); s_sk = sem("s_sk"); s_x2 = sem("s_x2"); s_wu = sem("s_wu")
        s_qk = sem("s_qk"); s_qf = sem("s_qf"); s_hi = sem("s_hi"); s_lo = sem("s_lo")
        o_v = [sem(f"o_v{i}") for i in range(2)]; o_x2 = [sem(f"o_x2{i}") for i in range(2)]; o_qk = [sem(f"o_qk{i}") for i in range(2)]
        x1 = sb("x1", [P, NQ, MODEL]); xl = sb("xl", [P, NQ, MODEL])
        stats = sb("stats", [P, NQ, 6]); mv = sb("mv", [P, NQ, 2]); var_eps = sb("var_eps", [P, NQ]); std = sb("std", [P, NQ]); rstd = sb("rstd", [P, NQ]); nmr = sb("nmr", [P, NQ])
        def load_rows(sp, n):
            sp.dma_start(s1_row[:], I["t_emb"][bass.ds(n, 1), 0:MODEL].to_broadcast([P, MODEL])).then_inc(row_in, 16)
            sp.dma_start(u_row[:], WDC[2, bass.ds(n, 1), :].to_broadcast([P, MODEL])).then_inc(row_in, 16)
        wu_b = sb("wu_b", [P, NK, MODEL])

        def load_x1(sp, n, q):
            sp.dma_start(x1[:, q, :], X1.rearrange("(q b) t c -> b q t c", b=BATCH)[bass.ds(n, 1)].rearrange("o q t c -> (o q) t c")[q]).then_inc(x_in[q], 16)
        def scale_x1(pool, n, q, first):
            pool.wait_ge(x_in[q], START + n * 16 + 16)
            if not first:
                pool.wait_ge(s_tp, START + n * NQ - NQ + q + 1)
            if q == 0:
                pool.wait_ge(row_in, START + n * 32 + (16 if first else 32))
            nc.gpsimd.tensor_tensor(out=xl[:, q, :], in0=x1[:, q, :], in1=s1_row[:], op=ALU.mult).then_inc(s_xs, 1)
        def scale_u(pool, n, first):
            if first:
                pool.wait_ge(row_in, START + 32)
            else:
                pool.wait_ge(s_sk, START + n * NQ)
            nc.gpsimd.tensor_tensor(out=wu_b[:], in0=w_u[:], in1=u_row[:].rearrange("p (o n) -> p o n", o=1).to_broadcast([P, NK, MODEL]), op=ALU.mult).then_inc(s_wu, 1)
        def two_stats(dve, n, q):
            for i in (q, q + 1):
                dve.wait_ge(s_xs, START + n * NQ + i + 1)
                nc.vector.bn_stats(out=stats[:, i, :], in_=xl[:, i, :]).then_inc(s_st, 1)
            dve.wait_ge(s_st, START + n * NQ + q + 2)
            nc.vector.memset(idle[:], 0.0)
            for i in (q, q + 1):
                nc.vector.bn_aggr(out=mv[:, i, :], in_=stats[:, i, :]).then_inc(s_mv, 1)
        def add_eps(dve, n):
            dve.wait_ge(s_mv, START + n * NQ + NQ)
            nc.vector.tensor_scalar(out=var_eps[:], in0=mv[:, :, 1], scalar1=1e-5, scalar2=None, op0=ALU.add).then_inc(s_ve, 1)
        def invert_std(dve, n):
            dve.wait_ge(s_sd, START + n + 1)
            nc.vector.reciprocal(out=rstd[:], in_=std[:]).then_inc(s_nm, 1)
            dve.wait_ge(s_nm, START + n * 2 + 1)
            nc.vector.scalar_tensor_tensor(out=nmr[:], in0=mv[:, :, 0], scalar=-1.0, in1=rstd[:], op0=ALU.mult, op1=ALU.mult).then_inc(s_nm, 1)
        def root(act, n):
            act.wait_ge(s_ve, START + n + 1)
            nc.scalar.activation(std[:], var_eps[:], ACT.Sqrt).then_inc(s_sd, 1)
        def normalise(act, n, q):
            act.wait_ge(s_nm, START + n * 2 + 2)
            nc.scalar.activation(xl[:, q, :], xl[:, q, :], ACT.Identity, bias=nmr[:, q:q + 1], scale=rstd[:, q:q + 1]).then_inc(s_xl, 1)

        with ExitStack() as setup:
            tb = lambda n, s: setup.enter_context(nc.sbuf_tensor("d_" + n, s, f32))
            w = {j: tb("w_" + j, [P, NK, MODEL]) for j in "qkvw"} | {"u": w_u}
            w2 = [tb(f"w2_{i}", [P, NK, MODEL]) for i in range(2)]
            s_col = tb("s_col", [P, 2 * NK, BATCH]); ssq = tb("ssq", [P, 2 * NK, BATCH])
            rows = tb("rows", [BATCH, 3, MODEL]); s2_rows = tb("s2_rows", [BATCH, MODEL])
            split = sem("split")
            with nc.Block() as block:
                @block.sync
                def _(sp):
                    start_counts(sp, sems)
                    for b in range(BATCH):
                        sp.dma_start(s_col[:, :, b], I["t_emb"][b].rearrange("(m p) -> p m", p=P), allow_slow_non_contiguous=True).then_inc(styles, 16)
                    sp.dma_start(s2_rows[:], I["t_emb"][:, MODEL:2 * MODEL]).then_inc(styles, 16)
                    sp.dma_start(ident[:], I["ident"]).then_inc(styles, 16)
                    sp.dma_start(s1_row[:], I["t_emb"][0:1, 0:MODEL].to_broadcast([P, MODEL])).then_inc(row_in, 16)
                    for n, j in enumerate(mats):
                        if n:
                            sp.wait_ge(consts, START + 16 * n)
                        sp.dma_start(w[j][:], I[j + "_t"].rearrange("(k p) n -> p k n", p=P)).then_inc(consts, 16)
                        for q in ((0, 1), (2, 3), (4, 5), (6, 7), ())[n]:
                            load_x1(sp, 0, q)
                    sp.wait_ge(dve_setup, START + 8)
                    sp.dma_start(WDC.rearrange("j b n -> b j n"), rows[:]).then_inc(rows_in, 16)
                    sp.wait_ge(rows_in, START + 16)
                    sp.dma_start(u_row[:], WDC[2, 0:1, :].to_broadcast([P, MODEL])).then_inc(row_in, 16)
                    for b in range(BATCH):
                        sp.dma_start(v_rows[:, b, :], WDC[0, b:b + 1, :].to_broadcast([P, MODEL])).then_inc(rows_in, 16)
                    sp.wait_ge(rows_in, START + 16 + 16 * BATCH)
                @block.gpsimd
                def _(pool):
                    for q in range(NQ):
                        scale_x1(pool, 0, q, True)
                    scale_u(pool, 0, True)
                @block.scalar
                def _(act):
                    act.wait_ge(styles, START + 16 * (BATCH + 2))
                    nc.scalar.activation(ssq[:], s_col[:], ACT.Square).then_inc(act_setup, 1)
                    for n, j in enumerate(mats):
                        act.wait_ge(consts, START + 16 * (n + 1))
                        if n >= 2:
                            act.wait_ge(sums, START + n - 1)
                        nc.scalar.activation(w2[n % 2][:], w[j][:], ACT.Square).then_inc(act_setup, 1)
                    act.wait_ge(dve_setup, START + 4)
                    nc.scalar.activation(rows[:], rows[:], ACT.Sqrt).then_inc(act_setup, 1)
                    nc.scalar.activation(qk[:], qk[:], ACT.Sqrt).then_inc(act_setup, 1)
                    root(act, 0)
                    for q in range(NQ):
                        normalise(act, 0, q)
                @block.tensor
                def _(pe):
                    for n, j in enumerate(mats):
                        pe.wait_ge(act_setup, START + n + 2)
                        if n < 2:
                            for ot in range(NK):
                                for k in range(NK):
                                    c = (n * NK + ot) * BATCH
                                    mm = nc.tensor.matmul(pt[:, c:c + BATCH], w2[n % 2][:, k, ot * P:(ot + 1) * P], ssq[:, k, :], start=(k == 0), stop=(k == NK - 1))
                        else:
                            for k in range(NK):
                                mm = nc.tensor.matmul((pv, pvt, psk)[n - 2][0:BATCH, :], ssq[:, (0 if n == 2 else NK) + k, :], w2[n % 2][:, k, :], start=(k == 0), stop=(k == NK - 1))
                        mm.then_inc(sums, 1)
                @block.vector
                def _(dve):
                    for n, j in enumerate("qkv"):
                        dve.wait_ge(consts, START + 16 * (n + 1))
                        nc.vector.tensor_copy(out=w_hi[j][:], in_=w[j][:]).then_inc(split, 1)
                        dve.wait_ge(split, START + n + 1)
                        nc.vector.tensor_tensor(out=w_lo[j][:], in0=w[j][:], in1=w_hi[j][:].bitcast(f32), op=ALU.subtract)
                    dve.wait_ge(sums, START + 2)
                    nc.vector.tensor_scalar(out=qk[:], in0=pt[:, 0:2 * NK * BATCH], scalar1=1e-8, scalar2=None, op0=ALU.add).then_inc(dve_setup, 1)
                    for n in range(3):
                        dve.wait_ge(sums, START + 3 + n)
                        nc.vector.tensor_scalar(out=rows[:, n, :], in0=(pv, pvt, psk)[n][0:BATCH, :], scalar1=1e-8, scalar2=None, op0=ALU.add).then_inc(dve_setup, 1)
                    for q in range(0, NQ, 2):
                        two_stats(dve, 0, q)
                    add_eps(dve, 0)
                    dve.wait_ge(act_setup, START + 8)
                    nc.vector.reciprocal(out=qk[:], in_=qk[:]).then_inc(dve_setup, 1)
                    nc.vector.reciprocal(out=rows[:], in_=rows[:]).then_inc(dve_setup, 1)
                    dve.wait_ge(dve_setup, START + 6)
                    nc.vector.scalar_tensor_tensor(out=qk_col[:], in0=qk[:, 0:NK * BATCH], scalar=float(np.float32(HD) ** np.float32(-0.5)), in1=qk[:, NK * BATCH:], op0=ALU.mult, op1=ALU.mult).then_inc(dve_setup, 1)
                    nc.vector.tensor_tensor(out=rows[:, 0, :], in0=rows[:, 0, :], in1=s2_rows[:], op=ALU.mult).then_inc(dve_setup, 1)
                    invert_std(dve, 0)

        xl_hi = sb("xl_hi", [P, NK, SEQ], f32r); xl_lo = sb("xl_lo", [P, NK, SEQ], f32r)
        v = sb("v", [P, 2, MODEL]); v_t = sb("v_t", [P, NK, P]); x2 = sb("x2", [P, 2, MODEL]);
        qf = sb("qf", [P, 2, SEQ]); hi = sb("hi", [P, 2, SEQ], f32r); lo = sb("lo", [P, 2, SEQ], f32r)

        def batches(e, body):
            with e.Fori(0, BATCH - 1) as b:
                body(b, True)
            body(BATCH - 1, False)

        with nc.Block() as block:
            @block.sync
            def _(sp):
                def body(b, ahead):
                    if ahead:
                        sp.wait_ge(s_wu, START + b + 1)
                        load_rows(sp, b + 1)
                    for s in range(STEPS + 1):
                        q = s - 2
                        if 0 <= q < NQ:
                            sp.wait_ge(s_v, START + b * NQ + q + 1)
                            sp.dma_start(V.rearrange("(b g) t c -> b t g c", b=BATCH)[bass.ds(b, 1)].rearrange("o t g c -> (o t) g c")[q * P:(q + 1) * P], v[:, q % 2, :].rearrange("p (g c) -> p g c", c=P)).then_inc(o_v[q % 2], 16)
                        q = s - 4
                        if 0 <= q < NQ:
                            sp.wait_ge(s_x2, START + b * NQ + q + 1)
                            sp.dma_start(X2[bass.ds(b, 1)].rearrange("o t c -> (o t) c")[q * P:(q + 1) * P, :], x2[:, q % 2, :]).then_inc(o_x2[q % 2], 16)
                            if ahead:
                                load_x1(sp, b + 1, q)
                        e = s - NQ - 1
                        if e >= 0:
                            ot, j = e // 2, e % 2
                            for part, t, s_t in ((0, hi, s_hi), (1, lo, s_lo)):
                                sp.wait_ge(s_t, START + b * NP + e + 1)
                                dst = QK[2 * j + part].rearrange("b (t p) s -> b t p s", p=P)[bass.ds(b, 1)].rearrange("o t p s -> (o t) p s")[ot]
                                sp.dma_start(dst, t[:, e % 2, :].bitcast(f32)).then_inc(o_qk[e % 2], 16)
                batches(sp, body)
                for i in range(2):
                    sp.wait_ge(o_v[i], START + 64 * BATCH)
                    sp.wait_ge(o_x2[i], START + 64 * BATCH)
                    sp.wait_ge(o_qk[i], START + 128 * BATCH)
            @block.gpsimd
            def _(pool):
                with pool.Fori(0, BATCH - 1) as b:
                    for q in range(NQ):
                        scale_x1(pool, b + 1, q, False)
                    scale_u(pool, b + 1, False)
            @block.tensor
            def _(pe):
                def body(b, ahead):
                    for s in range(STEPS):
                        q = s
                        if q < NQ:
                            pe.wait_ge(s_xl, START + b * NQ + q + 1)
                            pe.wait_ge(s_lt, START + b * NQ + q)
                            for k in range(NK):
                                mm = nc.tensor.transpose(pt[:, k * P:(k + 1) * P], xl[:, q, k * P:(k + 1) * P], ident[:])
                            mm.then_inc(s_tp, 1)
                        q = s - 1
                        if 0 <= q < NQ:
                            pe.wait_ge(s_lt, START + b * NQ + q + 1)
                            pe.wait_ge(s_v, START + b * NQ + q)
                            for k in range(NK):
                                for part, (rows_part, w_part) in enumerate(((xl_hi, w_hi), (xl_hi, w_lo), (xl_lo, w_hi))):
                                    mm = nc.tensor.matmul(pv[:], rows_part[:, k, q * P:(q + 1) * P], w_part["v"][:, k, :], start=(k == 0 and part == 0), stop=(k == NK - 1 and part == 2))
                            mm.then_inc(s_pv, 1)
                        q = s - 2
                        if 0 <= q < NQ:
                            pe.wait_ge(s_v, START + b * NQ + q + 1)
                            pe.wait_ge(s_vc, START + b * NQ + q)
                            for k in range(NK):
                                mm = nc.tensor.transpose(pvt[:, k * P:(k + 1) * P], v[:, q % 2, k * P:(k + 1) * P], ident[:])
                            mm.then_inc(s_vt, 1)
                        q = s - 3
                        if 0 <= q < NQ:
                            pe.wait_ge(s_vc, START + b * NQ + q + 1)
                            pe.wait_ge(s_x2, START + b * NQ + q)
                            if q == 0:
                                pe.wait_ge(s_wu, START + b + 1)
                            for k in range(NK):
                                mm = nc.tensor.matmul(psk[:], v_t[:, k, :], wu_b[:, k, :], start=(k == 0), stop=(k == NK - 1))
                            mm.then_inc(s_sk, 1)
                        e = s - NQ
                        if e >= 0:
                            ot, j = e // 2, e % 2
                            pe.wait_ge(s_qf, START + b * NP + max(e - 1, 0))
                            for h in range(NH):
                                for k in range(NK):
                                    for part, (w_part, rows_part) in enumerate(((w_hi, xl_hi), (w_hi, xl_lo), (w_lo, xl_hi))):
                                        mm = nc.tensor.matmul(pqk[e % 2][:, h * 512:h * 512 + 512], w_part["qk"[j]][:, k, ot * P:(ot + 1) * P], rows_part[:, k, h * 512:h * 512 + 512], start=(k == 0 and part == 0), stop=(k == NK - 1 and part == 2))
                            mm.then_inc(s_qk, 1)
                batches(pe, body)
            @block.scalar
            def _(act):
                def body(b, ahead):
                    for s in range(STEPS):
                        q = s
                        if q < NQ:
                            act.wait_ge(s_tp, START + b * NQ + q + 1)
                            if q == 0:
                                act.wait_ge(s_qk, START + b * NP)
                            nc.scalar.copy(xl_hi[:, :, q * P:(q + 1) * P], pt[:].rearrange("p (k t) -> p k t", k=NK)).then_inc(s_xt, 1)
                        q = s - 2
                        if 0 <= q < NQ:
                            act.wait_ge(s_vt, START + b * NQ + q + 1)
                            act.wait_ge(s_sk, START + b * NQ + q)
                            nc.scalar.copy(v_t[:], pvt[:].rearrange("p (k t) -> p k t", k=NK)).then_inc(s_vc, 1)
                        e = s - NQ
                        if e >= 0:
                            ot, j = e // 2, e % 2
                            act.wait_ge(s_qk, START + b * NP + e + 1)
                            act.wait_ge(s_lo, START + b * NP + max(e - 1, 0))
                            if j == 0:
                                scale = qk_col[:].rearrange("p (t b) -> p t b", b=BATCH)[:, ot, bass.ds(b, 1)]
                                nc.scalar.activation(qf[:, e % 2, :], pqk[e % 2][:], ACT.Identity, scale=scale, bias=0.0).then_inc(s_qf, 1)
                            else:
                                nc.scalar.copy(qf[:, e % 2, :], pqk[e % 2][:]).then_inc(s_qf, 1)
                        if ahead and e == 4:
                            root(act, b + 1)
                        if ahead and e in (5, 6):
                            for i in range(NQ // 2):
                                normalise(act, b + 1, (e - 5) * (NQ // 2) + i)
                batches(act, body)
            @block.vector
            def _(dve):
                def body(b, ahead):
                    for s in range(STEPS):
                        q = s
                        if q < NQ:
                            dve.wait_ge(s_xt, START + b * NQ + q + 1)
                            nc.vector.tensor_tensor(out=xl_lo[:, :, q * P:(q + 1) * P], in0=pt[:].rearrange("p (k t) -> p k t", k=NK), in1=xl_hi[:, :, q * P:(q + 1) * P].bitcast(f32), op=ALU.subtract).then_inc(s_lt, 1)
                        q = s - 1
                        if 0 <= q < NQ:
                            dve.wait_ge(s_pv, START + b * NQ + q + 1)
                            dve.wait_ge(o_v[q % 2], START + b * 64 + 16 * (q // 2))
                            dve.wait_ge(s_vt, START + b * NQ + max(q - 1, 0))
                            nc.vector.tensor_tensor(out=v[:, q % 2, :], in0=v_rows[:].rearrange("p b n -> p (b n)")[:, bass.ds(b * MODEL, MODEL)], in1=pv[:], op=ALU.mult).then_inc(s_v, 1)
                        q = s - 3
                        if 0 <= q < NQ:
                            dve.wait_ge(s_sk, START + b * NQ + q + 1)
                            dve.wait_ge(o_x2[q % 2], START + b * 64 + 16 * (q // 2))
                            nc.vector.tensor_tensor(out=x2[:, q % 2, :], in0=x1[:, q, :], in1=psk[:], op=ALU.add).then_inc(s_x2, 1)
                        e = s - NQ
                        if e >= 0:
                            dve.wait_ge(s_qf, START + b * NP + e + 1)
                            dve.wait_ge(o_qk[e % 2], START + b * 128 + 32 * (e // 2))
                            nc.vector.tensor_copy(out=hi[:, e % 2, :], in_=qf[:, e % 2, :]).then_inc(s_hi, 1)
                            dve.wait_ge(s_hi, START + b * NP + e + 1)
                            nc.vector.tensor_tensor(out=lo[:, e % 2, :], in0=qf[:, e % 2, :], in1=hi[:, e % 2, :].bitcast(f32), op=ALU.subtract).then_inc(s_lo, 1)
                        if ahead and 0 <= e < NQ // 2:
                            two_stats(dve, b + 1, 2 * e)
                        if ahead and e == 4:
                            add_eps(dve, b + 1)
                            invert_std(dve, b + 1)
                batches(dve, body)


def attention_phase(nc, I, QK, V, OT):
    GROUP = P // HD
    NGROUPS = BATCH * HEADS // GROUP
    KROWS = 3 * HD
    STACK = KROWS + 1
    ROWS = GROUP * NQ
    UNITS = ROWS * NH
    STEPS = NH * NQ
    HALFQ = SEQ // NH
    PIECES = 4
    RING = 3
    PAIRS = STEPS // 2
    LATER = 4
    DEN_STEP = {LATER - 2: 1, NQ + LATER - 2: 0}
    INVERT = {4: (1, 0), 6: (1, 1), 7: (1, 2), 8: (1, 3), 11: (0, 0), 12: (0, 1), 13: (0, 2), 14: (0, 3)}
    TURN_STEP = STEPS - 2
    PER_STEP = [(5, 4)[s % 2] for s in range(TURN_STEP)]
    PER_STEP += [UNITS - sum(PER_STEP), 0]
    assert 0 <= PER_STEP[TURN_STEP] <= 2
    with ExitStack() as ctx:
        sb = lambda n, s, d=f32: ctx.enter_context(nc.sbuf_tensor("e_" + n, s, d))
        pb = lambda n, s, d=f32: ctx.enter_context(nc.psum_tensor("e_" + n, s, d))
        sems = []
        def sem(n):
            sems.append(ctx.enter_context(nc.semaphore("e_" + n)))
            return sems[-1]
        qs = [sb(f"qs{i}", [STACK, GROUP, SEQ], f32r) for i in range(RING)]
        ks = [sb(f"ks{i}", [STACK, GROUP, SEQ], f32r) for i in range(RING)]
        v = [sb(f"v{i}", [P, NQ, P]) for i in range(RING)]
        ident = sb("ident", [P, P]); ones = sb("ones", [P, HD])
        half_max = sb("half_max", [P, ROWS, NH]); row_max = sb("row_max", [P, ROWS])
        neg_row = [sb(f"neg_row{i}", [ROWS, P], f32r) for i in range(RING)]
        probs = sb("probs", [P, 4, GROUP, HALFQ]); pair_sum = sb("pair_sum", [P, 2, GROUP, HALFQ])
        den = sb("den", [P, NH, HALFQ]); rden = sb("rden", [P, NH, HALFQ]); raw = sb("raw", [P, NH, HALFQ]); o = sb("o", [P, NH, HALFQ])
        p_max = [pb(f"p_max{i}", [P, 512]) for i in range(2)]; p_exp = [pb(f"p_exp{i}", [P, 2, HALFQ]) for i in range(2)]
        p_o = pb("p_o", [P, HALFQ]); p_d = pb("p_d", [P, HALFQ])
        consts = sem("consts"); cleared = sem("cleared")
        stacks_in = [sem(f"stacks_in{i}") for i in range(RING)]; max_in = [sem(f"max_in{i}") for i in range(RING)]
        unit_scores = sem("unit_scores"); unit_max = sem("unit_max"); max_turned = sem("max_turned"); max_row = sem("max_row"); max_whole = sem("max_whole")
        scores = sem("scores"); exps = sem("exps"); products = sem("products"); paired = sem("paired"); key_sums = sem("key_sums")
        den_taken = sem("den_taken"); raw_taken = sem("raw_taken")
        rden_ready = [sem(f"rden_ready{i}") for i in range(NH)]; o_ready = [sem(f"o_ready{i}") for i in range(NH)]
        o_out = [sem(f"o_out{i}") for i in range(NH)]
        LOADS = 7 * 16


        def load(sp, n, i):
            for stack, order in ((qs[i], (0, 0, 1)), (ks[i], (2, 3, 2))):
                for row, part in enumerate(order):
                    src = QK[part].rearrange("b (g h p) s -> (b g) p h s", h=GROUP, p=HD)[bass.ds(n, 1)].rearrange("o p h s -> (o p) h s")
                    sp.dma_start(stack[row * HD:(row + 1) * HD].bitcast(f32), src).then_inc(stacks_in[i], 16)
            sp.dma_start(v[i][:], V[bass.ds(n, 1)].rearrange("o (q p) c -> p (o q) c", p=P)).then_inc(stacks_in[i], 16)

        def send_max(sp, n, i):
            sp.wait_ge(max_row, START + n + 1)
            sp.dma_start(qs[i][KROWS:STACK].rearrange("o h (q c) -> o (h q) c", c=P).bitcast(f32), neg_row[i][:].bitcast(f32)).then_inc(max_in[i], 16)

        def max_unit(pe, n, i, turn, u):
            row, half = divmod(u, NH)
            h, q = divmod(row, NQ)
            if u == 0:
                pe.wait_ge(stacks_in[i], START + turn * LOADS + LOADS)
            if u == 1:
                pe.wait_ge(max_row, START + n)
            pe.wait_ge(unit_max, START + n * UNITS + max(u - 1, 0))
            nc.tensor.matmul(p_max[u % 2][:], qs[i][0:KROWS, h, q * P:(q + 1) * P], ks[i][0:KROWS, h, half * 512:(half + 1) * 512], start=True, stop=True).then_inc(unit_scores, 1)

        def turn_max(pe, n):
            pe.wait_ge(max_whole, START + n + 1)
            nc.tensor.transpose(p_max[1][0:ROWS, 0:P], row_max[:], ident[:]).then_inc(max_turned, 1)

        def scores_pair(pe, n, i, s, pair):
            half, kt = divmod(s, NQ)
            pe.wait_ge(exps, START + n * (2 * STEPS) + (2 * s - 1 + pair))
            for j in range(2):
                h = 2 * pair + j
                mm = nc.tensor.matmul(p_exp[pair][:, j, :], ks[i][:, h, kt * P:(kt + 1) * P], qs[i][:, h, half * HALFQ:(half + 1) * HALFQ], start=True, stop=True)
            mm.then_inc(scores, 1)

        def products_o(pe, n, i, s):
            kt = s % NQ
            pe.wait_ge(exps, START + n * (2 * STEPS) + 2 * (s + 1))
            if kt == 0:
                pe.wait_ge(raw_taken, START + n * NH + s // NQ + 1)
            vi = v[i if s >= 0 else (i - 1) % RING]
            for h in range(GROUP):
                mm = nc.tensor.matmul(p_o[HD * h:HD * (h + 1), :], vi[:, kt, HD * h:HD * (h + 1)], probs[:, s % 4, h, :], start=(kt == 0), stop=(kt == NQ - 1), skip_group_check=True)
            mm.then_inc(products, 1)

        def sum_keys(pe, n, s):
            t = s // 2 - LATER // 2
            pe.wait_ge(paired, START + n * PAIRS + t + 1)
            if t % (NQ // 2) == 0:
                pe.wait_ge(den_taken, START + n * NH + t // (NQ // 2) + 1)
            for h in range(GROUP):
                mm = nc.tensor.matmul(p_d[HD * h:HD * (h + 1), :], ones[:], pair_sum[:, t % 2, h, :], start=(t % (NQ // 2) == 0), stop=(t % (NQ // 2) == NQ // 2 - 1), skip_group_check=True)
            mm.then_inc(key_sums, 1)

        def pe_group(pe, n, i, turn, ahead):
            pe.wait_ge(max_in[i], START + turn * 16 + 16)
            i1, turn1 = (i + 1) % RING, turn + (i + 1) // RING
            units = iter(range(UNITS if ahead else 0))
            def some(count):
                for _, u in zip(range(count), units):
                    max_unit(pe, n + 1, i1, turn1, u)
            for s in range(STEPS):
                left = PER_STEP[s]
                scores_pair(pe, n, i, s, 0)
                some(min(left, 1))
                scores_pair(pe, n, i, s, 1)
                some(min(left - 1, 1))
                products_o(pe, n, i, s - 1)
                some(min(left - 2, 2))
                if ahead and s == TURN_STEP:
                    turn_max(pe, n + 1)
                if s % 2 == 0:
                    sum_keys(pe, n, s)
                some(min(left - 4, 1))

        def take_raw(act, n, half):
            act.wait_ge(products, START + n * STEPS + (NQ + 1 if half == 0 else 1))
            act.wait_ge(o_ready[half], START + n - half)
            nc.scalar.copy(raw[:, half], p_o[:]).then_inc(raw_taken, 1)

        def act_group(act, n):
            for s in range(STEPS):
                for pair in range(2):
                    act.wait_ge(scores, START + n * (2 * STEPS) + 2 * s + pair + 1)
                    if pair == 0:
                        act.wait_ge(products, START + n * STEPS + max(s - 2, -1))
                        act.wait_ge(paired, START + n * PAIRS + s // 2 - 1)
                    nc.scalar.activation(probs[:, s % 4, 2 * pair:2 * pair + 2, :], p_exp[pair][:], ACT.Exp).then_inc(exps, 1)
                if s == 0:
                    take_raw(act, n, 1)
                if s == NQ:
                    take_raw(act, n, 0)

        def dve_unit(dve, n, u):
            dve.wait_ge(unit_scores, START + n * UNITS + u + 1)
            if u == 0:
                dve.wait_ge(max_whole, START + n)
            nc.vector.tensor_reduce(out=half_max[:].rearrange("p r h -> p (r h)")[:, u:u + 1], in_=p_max[u % 2][:], axis=mybir.AxisListType.X, op=ALU.max).then_inc(unit_max, 1)

        def dve_row(dve, n, i, turn):
            dve.wait_ge(unit_max, START + n * UNITS + UNITS)
            dve.wait_ge(max_turned, START + n)
            nc.vector.tensor_reduce(out=row_max[:], in_=half_max[:], axis=mybir.AxisListType.X, op=ALU.max).then_inc(max_whole, 1)
            dve.wait_ge(max_turned, START + n + 1)
            dve.wait_ge(max_in[i], START + turn * 16)
            nc.vector.tensor_scalar(out=neg_row[i][:], in0=p_max[1][0:ROWS, 0:P], scalar1=-1.0, scalar2=None, op0=ALU.mult).then_inc(max_row, 1)

        def take_den(dve, n, half):
            dve.wait_ge(key_sums, START + n * PAIRS + (LATER // 2 + NQ // 2 if half == 0 else LATER // 2))
            dve.wait_ge(rden_ready[half], START + n)
            nc.vector.tensor_copy(out=den[:, half], in_=p_d[:]).then_inc(den_taken, 1)

        def invert(dve, n, half, piece):
            w = HALFQ // PIECES
            if piece == 0:
                dve.wait_ge(den_taken, START + n * NH + (2 if half == 0 else 1))
                dve.wait_ge(o_ready[half], START + n - half)
            r = nc.vector.reciprocal(out=rden[:, half, piece * w:(piece + 1) * w], in_=den[:, half, piece * w:(piece + 1) * w])
            if piece == PIECES - 1:
                r.then_inc(rden_ready[half], 1)

        def dve_group(dve, n, i, turn, ahead):
            i1, turn1 = (i + 1) % RING, turn + (i + 1) // RING
            units = iter(range(UNITS if ahead else 0))
            for s in range(STEPS):
                for k, u in zip(range(PER_STEP[s]), units):
                    if k == 2 and s in INVERT:
                        invert(dve, n, *INVERT[s])
                    dve_unit(dve, n + 1, u)
                if s in INVERT and (not ahead or PER_STEP[s] <= 2):
                    invert(dve, n, *INVERT[s])
                if s in DEN_STEP:
                    take_den(dve, n, DEN_STEP[s])
                if ahead and s == TURN_STEP:
                    dve_row(dve, n + 1, i1, turn1)

        def add_pair(pool, n, t):
            pool.wait_ge(exps, START + n * (2 * STEPS) + 4 * t + 4)
            pool.wait_ge(key_sums, START + n * PAIRS + t + 1)
            nc.gpsimd.tensor_tensor(out=pair_sum[:, t % 2], in0=probs[:, (2 * t) % 4], in1=probs[:, (2 * t + 1) % 4], op=ALU.add).then_inc(paired, 1)

        def divide(pool, n, half):
            pool.wait_ge(rden_ready[half], START + n + 1 + half)
            pool.wait_ge(raw_taken, START + n * NH + half + 2)
            pool.wait_ge(o_out[half], START + n * 16)
            nc.gpsimd.tensor_tensor(out=o[:, half, :], in0=raw[:, half], in1=rden[:, half], op=ALU.mult).then_inc(o_ready[half], 1)

        def store(sp, n, half):
            sp.wait_ge(o_ready[half], START + n + 1)
            sp.dma_start(OT[bass.ds(n, 1)].rearrange("o p s -> (o p) s")[:, half * HALFQ:(half + 1) * HALFQ], o[:, half, :]).then_inc(o_out[half], 16)

        def pool_group(pool, n, before):
            for t in range(PAIRS):
                add_pair(pool, n, t)
                if t == PAIRS // 2 and before is not None:
                    divide(pool, before, 1)
            divide(pool, n, 0)

        with nc.Block() as block:
            @block.sync
            def _(sp):
                start_counts(sp, sems)
                sp.dma_start(ident[:], I["ident"]).then_inc(consts, 16)
                for i in range(2):
                    load(sp, i, i)
                send_max(sp, 0, 0)
                sp.wait_ge(max_in[0], START + 16)
            @block.vector
            def _(dve):
                nc.vector.memset(ones[:], 1.0)
                nc.vector.memset(probs[:, 3], 0.0)
                nc.vector.memset(pair_sum[:], 0.0)
                nc.vector.memset(v[RING - 1][:, NQ - 1, :], 0.0)
                for i in range(RING):
                    nc.vector.memset(ks[i][KROWS:STACK].bitcast(f32), 1.0)
                nc.vector.memset(den[:, 1], 1.0).then_inc(cleared, 1)
                for u in range(UNITS):
                    dve_unit(dve, 0, u)
                dve_row(dve, 0, 0, 0)
            @block.tensor
            def _(pe):
                pe.wait_ge(consts, START + 16)
                for u in range(UNITS):
                    max_unit(pe, 0, 0, 0, u)
                turn_max(pe, 0)
                pe.wait_ge(cleared, START + 1)
                for bank in (p_o, p_d):
                    nc.tensor.matmul(bank[:], probs[:, 3, 0, 0:P], probs[:, 3, 0, :], start=True, stop=True)

        LOOPS = (NGROUPS - 2) // RING
        def groups(e, body, last=0):
            with e.Fori(0, LOOPS) as it:
                for i in range(RING):
                    body(it * RING + i, i, it, True)
            for n in range(LOOPS * RING, NGROUPS):
                body(n, n % RING, n // RING, n < NGROUPS - 1)

        with nc.Block() as block:
            @block.sync
            def _(sp):
                def body(n, i, turn, ahead, before, more):
                    if more:
                        sp.wait_ge(products, START + n * STEPS + 1)
                        load(sp, n + 2, (i + 2) % RING)
                    if before is not None:
                        store(sp, before, 1)
                    if ahead:
                        send_max(sp, n + 1, (i + 1) % RING)
                    store(sp, n, 0)
                for n in range(RING):
                    body(n, n, 0, True, n - 1 if n else None, True)
                with sp.Fori(1, LOOPS) as it:
                    for i in range(RING):
                        body(it * RING + i, i, it, True, it * RING + (i - 1), True)
                for n in range(LOOPS * RING, NGROUPS):
                    body(n, n % RING, n // RING, n < NGROUPS - 1, n - 1, n + 2 < NGROUPS)
                store(sp, NGROUPS - 1, 1)
                for half in range(NH):
                    sp.wait_ge(o_out[half], START + 16 * NGROUPS)
            @block.tensor
            def _(pe):
                groups(pe, lambda n, i, turn, ahead: pe_group(pe, n, i, turn, ahead))
                products_o(pe, NGROUPS, NGROUPS % RING, -1)
                for s in range(0, LATER, 2):
                    sum_keys(pe, NGROUPS, s)
            @block.scalar
            def _(act):
                with act.Fori(0, NGROUPS) as n:
                    act_group(act, n)
                take_raw(act, NGROUPS, 1)
            @block.vector
            def _(dve):
                groups(dve, lambda n, i, turn, ahead: dve_group(dve, n, i, turn, ahead))
                take_den(dve, NGROUPS, 1)
                for piece in range(PIECES):
                    invert(dve, NGROUPS, 1, piece)
            @block.gpsimd
            def _(pool):
                pool_group(pool, 0, None)
                with pool.Fori(1, NGROUPS) as n:
                    pool_group(pool, n, n + (-1))
                divide(pool, NGROUPS - 1, 1)

def out_phase(nc, I, OT, X2, WDC, out):
    with ExitStack() as ctx:
        sb = lambda n, s, d=f32: ctx.enter_context(nc.sbuf_tensor("f_" + n, s, d))
        sems = []
        def sem(n):
            sems.append(ctx.enter_context(nc.semaphore("f_" + n)))
            return sems[-1]
        w = sb("w", [P, NK, MODEL]); wdc = sb("wdc", [P, BATCH, MODEL]); wb = sb("wb", [P, BATCH, NK, MODEL])
        ot = [sb(f"ot{i}", [P, NK, SEQ]) for i in range(3)]; x2 = sb("x2", [P, NQ, MODEL]); o = sb("o", [P, 4, MODEL])
        po = [ctx.enter_context(nc.psum_tensor(f"f_po{i}", [P, MODEL], f32)) for i in range(4)]
        consts = sem("consts"); coefs_in = sem("coefs_in"); b_in = [sem(f"b_in{i}") for i in range(3)]; x_in = [sem(f"x_in{i}") for i in range(NQ)]
        scaled_pool = sem("scaled_pool"); scaled_dve = sem("scaled_dve"); products = sem("products"); added = sem("added"); o_out = [sem(f"o_out{i}") for i in range(4)]
        TILES = BATCH * NQ

        def load_batch(sp, b):
            sp.dma_start(ot[b % 3][:], OT.rearrange("(b g) p s -> b p g s", b=BATCH)[b]).then_inc(b_in[b % 3], 16)
        def load_x2(sp, t):
            sp.dma_start(x2[:, t % NQ, :], X2[t // NQ, t % NQ * P:(t % NQ + 1) * P, :]).then_inc(x_in[t % NQ], 16)
        def scale_w(e, engine, b, k, done):
            engine.tensor_tensor(out=wb[:, b, k, :], in0=w[:, k, :], in1=wdc[:, b, :], op=ALU.mult).then_inc(done, 1)

        with nc.Block() as block:
            @block.sync
            def _(sp):
                start_counts(sp, sems)
                sp.dma_start(w[:], I["w_t"].rearrange("(k p) n -> p k n", p=P)).then_inc(consts, 16)
                for b in range(BATCH):
                    sp.dma_start(wdc[:, b, :], WDC[1, b:b + 1, :].to_broadcast([P, MODEL])).then_inc(coefs_in, 16)
                load_batch(sp, 0)
                for t in range(NQ):
                    load_x2(sp, t)
                for b in range(1, 3):
                    load_batch(sp, b)
                for t in range(TILES):
                    if t == NQ:
                        sp.wait_ge(products, START + NQ)
                        load_batch(sp, 3)
                    sp.wait_ge(added, START + t + 1)
                    sp.dma_start(out[t // NQ, t % NQ * P:(t % NQ + 1) * P, :], o[:, t % 4, :]).then_inc(o_out[t % 4], 16)
                    if t + NQ < TILES:
                        load_x2(sp, t + NQ)
                for i in range(4):
                    sp.wait_ge(o_out[i], START + 16 * TILES // 4)
            @block.gpsimd
            def _(pool):
                pool.wait_ge(consts, START + 16)
                pool.wait_ge(coefs_in, START + 16 * BATCH)
                for b in range(BATCH):
                    for k in (range(2, NK) if b == 0 else range(NK)):
                        scale_w(pool, nc.gpsimd, b, k, scaled_pool)
            @block.tensor
            def _(pe):
                for t in range(TILES):
                    b, q = divmod(t, NQ)
                    if q == 0:
                        pe.wait_ge(b_in[b % 3], START + 16 * (b // 3 + 1))
                    if t >= 4:
                        pe.wait_ge(added, START + t - 3)
                    for k in range(NK):
                        if q == 0:
                            if b == 0 and k < 2:
                                pe.wait_ge(scaled_dve, START + k + 1)
                            else:
                                pe.wait_ge(scaled_pool, START + b * NK + k - 1)
                        mm = nc.tensor.matmul(po[t % 4][:], ot[b % 3][:, k, q * P:(q + 1) * P], wb[:, b, k, :], start=(k == 0), stop=(k == NK - 1))
                    mm.then_inc(products, 1)
            @block.vector
            def _(dve):
                dve.wait_ge(consts, START + 16)
                dve.wait_ge(coefs_in, START + 16 * BATCH)
                for k in range(2):
                    scale_w(dve, nc.vector, 0, k, scaled_dve)
                for t in range(TILES):
                    dve.wait_ge(products, START + t + 1)
                    dve.wait_ge(x_in[t % NQ], START + 16 * (t // NQ + 1))
                    if t >= 4:
                        dve.wait_ge(o_out[t % 4], START + 16 * (t // 4))
                    nc.vector.tensor_tensor(out=o[:, t % 4, :], in0=x2[:, t % NQ, :], in1=po[t % 4][:], op=ALU.add).then_inc(added, 1)


def build(nc, I, out):
    def scratch(name, shape, dtype=f32):
        return nc.dram_tensor(name, shape, dtype, kind="Internal").ap()

    Xp = scratch("xn_parts", [3 * 2 * BATCH, SEQ * HALF], bf16)
    Xn = scratch("xn_full", [BATCH, SEQ, INNER])
    Bp = scratch("b_parts", [3, BATCH, SEQ, STATES], bf16)
    Ad = scratch("decays", [BATCH * STATES, SEQ])
    Cm = scratch("c_rows", [BATCH * STATES, SEQ])
    Y = scratch("scan_out", [SEQ, 2 * BATCH, HALF])
    SG = scratch("silu_gate", [NQ * BATCH, P, INNER])
    X1 = scratch("x1_tiles", [NQ * BATCH, P, MODEL])
    QK = scratch("qk_parts", [4, BATCH, MODEL, SEQ])
    V = scratch("v_groups", [BATCH * HEADS * HD // P, SEQ, P])
    X2 = scratch("x2_full", [BATCH, SEQ, MODEL])
    WDC = scratch("coefs", [3, BATCH, MODEL])
    OT = scratch("attended", [BATCH * HEADS * HD // P, P, SEQ])
    pre_semaphores = pre_phase(nc, I, Xp, Xn, Bp, Ad, Cm)
    scan_phase(nc, I, Xp, Xn, Bp, Ad, Cm, Y, SG, X1, pre_semaphores)
    proj_phase(nc, I, X1, QK, V, X2, WDC)
    attention_phase(nc, I, QK, V, OT)
    out_phase(nc, I, OT, X2, WDC, out)


def kernel(**inputs):
    import concourse.bacc as bacc
    from concourse.bass_utils import run_bass_kernel_spmd

    turned = lambda name: np.ascontiguousarray(np.asarray(inputs[name]).T)
    plain = lambda name: np.ascontiguousarray(inputs[name])
    mask_b = np.zeros((6 * 2 * BATCH, P), np.float32)
    for k in range(mask_b.shape[0]):
        r = k % (2 * BATCH)
        mask_b[k, r * STATES:(r + 1) * STATES] = 1
    mask_c = np.zeros((P, 16, 32), np.float32)
    for p in range(P):
        for t in range(16):
            mask_c[p, t, (t % 4) * 8 + p // STATES] = 1
    arrays = {
        "x": plain("x"), "x_t": np.ascontiguousarray(np.asarray(inputs["x"]).transpose(0, 2, 1)), "x_tiles": np.ascontiguousarray(np.asarray(inputs["x"]).reshape(BATCH, NQ, P, NK, P).transpose(1, 0, 4, 3, 2)).reshape(NQ * BATCH, P, NK, P),
        "t_emb": plain("cond_2048"),
        "w_in_t": turned("L0_cond_W_in"), "w_conv": plain("L0_cond_W_conv"), "b_conv": plain("L0_cond_b_conv"),
        "ln_g": plain("L0_cond_ln_g"), "ln_b": plain("L0_cond_ln_b"), "w_xproj_t": turned("L0_cond_W_xproj"),
        "w_dt_t": np.ascontiguousarray(np.pad(turned("L0_cond_W_dt"), ((0, 0), (0, 64 - STATES)))),
        "b_dt": plain("L0_cond_b_dt"), "a_log": plain("L0_cond_A_log"), "D": plain("L0_cond_D"), "w_out_t": turned("L0_cond_W_out"),
        "ident": np.eye(P, dtype=np.float32), "mask_b": mask_b, "mask_c": mask_c,
    }
    for j in "qkvwu":
        arrays[j + "_t"] = turned(f"L1_cond_{j}_weight")
    nc = bacc.Bacc("TRN2", target_bir_lowering=False, num_devices=1)
    I = {n: nc.dram_tensor(f"in_{n}_dram", a.shape, mybir.dt.from_np(a.dtype), kind="ExternalInput").ap() for n, a in arrays.items()}
    out = nc.dram_tensor("out_dram", (BATCH, SEQ, MODEL), f32, kind="ExternalOutput").ap()
    build(nc, I, out)
    r = run_bass_kernel_spmd(nc, [{f"in_{n}_dram": a for n, a in arrays.items()}], core_ids=[0])
    return r.results[0]["out_dram"]
```

```python
from contextlib import ExitStack

import numpy as np

import concourse.bass as bass
from concourse import mybir

f32 = mybir.dt.float32
f32r = mybir.dt.float32r
bf16 = mybir.dt.bfloat16
ALU = mybir.AluOpType
ACT = mybir.ActivationFunctionType

P = 128
BATCH, SEQ, MODEL, INNER, STATES, TAPS = 4, 1024, 512, 1024, 16, 4
HEADS = 16
HD = MODEL // HEADS
NM, NQ, NK, NH = INNER // P, SEQ // P, MODEL // P, SEQ // 512
HALF = INNER // 2

START = 2


def start_counts(engine, semaphores):
    for s in semaphores:
        engine.sem_inc(s, START)


def pre_phase(nc, I, Xp, Xn, Bp, Ad, Cm):
    ALL = 3 * STATES
    with ExitStack() as ctx:
        sb = lambda n, s, d=f32: ctx.enter_context(nc.sbuf_tensor("a_" + n, s, d))
        pb = lambda n, s, d=f32: ctx.enter_context(nc.psum_tensor("a_" + n, s, d))
        sems = []
        def sem(n):
            sems.append(nc.alloc_semaphore(name="a_" + n))
            return sems[-1]
        w_in = sb("w_in", [P, NK, INNER]); x_t = sb("x_t", [P, NK, SEQ])
        temb = sb("temb", [P, NM]); w_conv = sb("w_conv", [P, NM, TAPS]); b_conv = sb("b_conv", [P, NM])
        ln_g = sb("ln_g", [P, INNER]); ln_b = sb("ln_b", [P, INNER])
        w_xp = sb("w_xp", [P, NM, ALL]); w_dt = sb("w_dt", [ALL, 64])
        b_dt = sb("b_dt", [STATES, 1]); a_log = sb("a_log", [STATES, 1]); neg_a = sb("neg_a", [STATES, 1])
        ident = sb("ident", [P, P]); idle = sb("idle", [P, NQ])
        padded = sb("padded", [P, 2, TAPS - 1 + SEQ]); acc = sb("acc", [P, 2, SEQ]); xc_t = sb("xc_t", [P, NM, SEQ])
        stats = sb("stats", [P, NQ, 2, 6]); mv = sb("mv", [P, NQ, 2]); var_eps = sb("var_eps", [P, NQ]); std = sb("std", [P, NQ])
        inv_std = sb("inv_std", [P, NQ]); shift = sb("shift", [P, NQ])
        xn = sb("xn", [P, NQ, INNER])
        part1 = sb("part1", [P, 2, INNER], bf16); rest = sb("rest", [P, 2, INNER]); part2 = sb("part2", [P, 2, INNER], bf16); part3 = sb("part3", [P, 2, INNER], bf16)
        square = sb("square", [P, INNER]); sumsq = sb("sumsq", [P, NQ])
        xn_t = sb("xn_t", [P, 2, NM, P]); xproj = sb("xproj", [P, NQ, P])
        sum_capped = sb("sum_capped", [P, NQ]); root = sb("root", [P, NQ]); at_least_one = sb("at_least_one", [P, NQ]); norm_capped = sb("norm_capped", [P, NQ])
        b_whole = sb("b_whole", [P, NQ, STATES]); b_part1 = sb("b_part1", [P, NQ, STATES], bf16); b_rest = sb("b_rest", [P, NQ, STATES]); b_part2 = sb("b_part2", [P, NQ, STATES], bf16); b_part3 = sb("b_part3", [P, NQ, STATES], bf16)
        proj_t = sb("proj_t", [ALL, SEQ]); dt_tanh = sb("dt_tanh", [STATES, SEQ]); decays = sb("decays", [STATES, SEQ])
        p_rows = [pb(f"p_rows{i}", [P, 1024]) for i in range(2)]
        p_turn = pb("p_turn", [P, 1024]); p_xproj = pb("p_xproj", [P, 512])
        consts = sem("consts"); late_consts = sem("late_consts"); a_ready = sem("a_ready"); batch_in = sem("batch_in"); projected = sem("projected"); evicted = sem("evicted"); last_tap = sem("last_tap"); taps_added = sem("taps_added"); silu_ready = sem("silu_ready")
        turned = sem("turned"); turned_copied = sem("turned_copied"); stats_ready = sem("stats_ready"); moments_ready = sem("moments_ready"); var_ready = sem("var_ready"); std_ready = sem("std_ready"); shift_ready = sem("shift_ready"); centred = sem("centred"); scaled = sem("scaled"); xn_ready = sem("xn_ready")
        part1_ready = sem("part1_ready"); squares_summed = sem("squares_summed"); rest_ready = sem("rest_ready"); part2_ready = sem("part2_ready"); part3_ready = sem("part3_ready"); xn_turned = sem("xn_turned"); xn_t_ready = sem("xn_t_ready"); xproj_ready = sem("xproj_ready"); xproj_copied = sem("xproj_copied")
        xn_out = [sem(f"xn_out{i}") for i in range(2)]; part1_out = [sem(f"part1_out{i}") for i in range(2)]
        part2_out = [sem(f"part2_out{i}") for i in range(2)]; part3_out = [sem(f"part3_out{i}") for i in range(2)]
        states_turned = sem("states_turned"); states_copied = sem("states_copied"); dt_ready = sem("dt_ready"); tanh_ready = sem("tanh_ready"); decays_ready = sem("decays_ready"); root_ready = sem("root_ready"); norm_steps = sem("norm_steps"); b_parts_ready = sem("b_parts_ready"); states_out = sem("states_out")

        def load_batch(sp, n):
            sp.dma_start(x_t[:], I["x_t"][bass.ds(n, 1)].rearrange("o (k p) t -> p (o k) t", p=P)).then_inc(batch_in, 16)
            sp.dma_start(temb[:], I["t_emb"][bass.ds(n, 1)].rearrange("o (m p) -> p (o m)", p=P), allow_slow_non_contiguous=True).then_inc(batch_in, 16)

        with nc.Block() as block:
            @block.sync
            def _(sp):
                start_counts(sp, sems)
                load_batch(sp, 0)
                for dst, src in ((w_in[:], I["w_in_t"][:, 0:INNER].rearrange("(k p) n -> p k n", p=P)),
                                 (w_conv[:], I["w_conv"].rearrange("(m p) o j -> p m (o j)", p=P)),
                                 (b_conv[:], I["b_conv"].rearrange("(m p) -> p m", p=P)),
                                 (a_log[:], I["a_log"].rearrange("(p o) -> p o", o=1))):
                    sp.dma_start(dst, src, allow_slow_non_contiguous=True).then_inc(consts, 16)
                for dst, src in ((ident[:], I["ident"]),
                                 (ln_g[:], I["ln_g"].rearrange("(o n) -> o n", o=1).to_broadcast([P, INNER])),
                                 (ln_b[:], I["ln_b"].rearrange("(o n) -> o n", o=1).to_broadcast([P, INNER])),
                                 (w_xp[:], I["w_xproj_t"].rearrange("(m p) n -> p m n", p=P)),
                                 (w_dt[2 * STATES:ALL, :], I["w_dt_t"]), (b_dt[:], I["b_dt"].rearrange("(p o) -> p o", o=1))):
                    sp.dma_start(dst, src).then_inc(late_consts, 16)
                sp.wait_ge(consts, START + 64)
            @block.vector
            def _(dve):
                nc.vector.memset(padded[:, :, 0:TAPS - 1], 0.0)
                nc.vector.memset(xproj[:, :, ALL:P], 0.0)
                dve.wait_ge(tanh_ready, START + 1)
                nc.vector.tensor_scalar(out=neg_a[:], in0=neg_a[:], scalar1=-0.01, scalar2=None, op0=ALU.mult).then_inc(a_ready, 1)
            @block.scalar
            def _(act):
                act.wait_ge(consts, START + 64)
                nc.scalar.activation(neg_a[:], a_log[:], ACT.Tanh).then_inc(tanh_ready, 1)

        def sp_part(sp, n, p, more):
            if p is not None:
                xp_b = Xp.rearrange("(i h b) (t c) -> b i t h c", i=3, h=2, c=HALF)[bass.ds(p, 1)].rearrange("o i t h c -> i (o t) h c")
            for s in range(NQ + 1):
                q = s
                if p is not None and q < NQ:
                    sp.wait_ge(xn_ready, START + p * NQ + q + 1)
                    sp.dma_start(Xn[bass.ds(p, 1)].rearrange("o t c -> (o t) c")[q * P:(q + 1) * P, :], xn[:, q, :]).then_inc(xn_out[q % 2], 16)
                    sp.wait_ge(part1_ready, START + p * NQ + q + 1)
                    sp.dma_start(xp_b[0][q * P:(q + 1) * P], part1[:, q % 2, :].rearrange("p (h c) -> p h c", h=2)).then_inc(part1_out[q % 2], 16)
                if s == NQ and more:
                    sp.wait_ge(projected, START + n * NM + NM)
                    sp.wait_ge(evicted, START + n * NM + NM)
                    load_batch(sp, n + 1)
                q = s - 1
                if p is not None and q >= 0:
                    sp.wait_ge(part2_ready, START + p * NQ + q + 1)
                    sp.dma_start(xp_b[1][q * P:(q + 1) * P], part2[:, q % 2, :].rearrange("p (h c) -> p h c", h=2)).then_inc(part2_out[q % 2], 16)
                    sp.wait_ge(part3_ready, START + p * NQ + q + 1)
                    sp.dma_start(xp_b[2][q * P:(q + 1) * P], part3[:, q % 2, :].rearrange("p (h c) -> p h c", h=2)).then_inc(part3_out[q % 2], 16)
            if p is not None:
                sp.wait_ge(states_copied, START + p + 1)
                sp.dma_start(Cm[bass.ds(p * STATES, STATES), :], proj_t[STATES:2 * STATES, :]).then_inc(states_out, 16)
                bp = Bp[:, bass.ds(p, 1)].rearrange("i o (q t) d -> i t (o q) d", t=P)
                sp.wait_ge(b_parts_ready, START + p * 3 + 3)
                for j, t in enumerate((b_part1, b_part2, b_part3)):
                    sp.dma_start(bp[j], t[:]).then_inc(states_out, 16)
                sp.wait_ge(decays_ready, START + p + 1)
                sp.dma_start(Ad[bass.ds(p * STATES, STATES), :], decays[:]).then_inc(states_out, 16)

        def pe_part(pe, n, p):
            for s in range(NQ + 1):
                if n is not None and s < NM:
                    m = s
                    if m == 0:
                        pe.wait_ge(batch_in, START + n * 32 + 32)
                    if m < 2:
                        pe.wait_ge(turned_copied, START + n * NQ)
                    else:
                        pe.wait_ge(evicted, START + n * NM + m - 1)
                    for h in range(NH):
                        for k in range(NK):
                            mm = nc.tensor.matmul(p_rows[m % 2][:, h * 512:h * 512 + 512], w_in[:, k, m * P:(m + 1) * P], x_t[:, k, h * 512:h * 512 + 512], start=(k == 0), stop=(k == NK - 1))
                    mm.then_inc(projected, 1)
                q = s
                if p is not None and q < NQ:
                    pe.wait_ge(xn_ready, START + p * NQ + q + 1)
                    if q == 0:
                        pe.wait_ge(tanh_ready, START + p + 1)
                    else:
                        pe.wait_ge(xn_t_ready, START + p * NQ + q)
                    for m in range(NM):
                        mm = nc.tensor.transpose(p_turn[:, m * P:(m + 1) * P], xn[:, q, m * P:(m + 1) * P], ident[:])
                    mm.then_inc(xn_turned, 1)
                q = s - 1
                if p is not None and q >= 0:
                    pe.wait_ge(xn_t_ready, START + p * NQ + q + 1)
                    pe.wait_ge(xproj_copied, START + p * NQ + q)
                    for m in range(NM):
                        mm = nc.tensor.matmul(p_xproj[:, 0:ALL], xn_t[:, q % 2, m, :], w_xp[:, m, :], start=(m == 0), stop=(m == NM - 1))
                    mm.then_inc(xproj_ready, 1)
            if p is not None:
                pe.wait_ge(xproj_copied, START + p * NQ + NQ)
                for q in range(NQ):
                    mm = nc.tensor.transpose(p_turn[:, q * P:(q + 1) * P], xproj[:, q, :], ident[:])
                mm.then_inc(states_turned, 1)
            if n is not None:
                if p is None:
                    pe.wait_ge(late_consts, START + 96)
                for q in range(NQ):
                    if q >= 2:
                        pe.wait_ge(turned_copied, START + n * NQ + q - 1)
                    for m in range(NM):
                        if q == 0 and m in (0, NM - 1):
                            pe.wait_ge(silu_ready, START + n * NM + (NM if m else NM - 1))
                        mm = nc.tensor.transpose(p_rows[q % 2][:, m * P:(m + 1) * P], xc_t[:, m, q * P:(q + 1) * P], ident[:])
                    mm.then_inc(turned, 1)
            if p is not None:
                pe.wait_ge(states_copied, START + p + 1)
                for h in range(NH):
                    mm = nc.tensor.matmul(p_turn[0:64, h * 512:h * 512 + 512], w_dt[2 * STATES:ALL, :], proj_t[2 * STATES:ALL, h * 512:h * 512 + 512], start=True, stop=True)
                mm.then_inc(dt_ready, 1)

        def act_part(act, n, p):
            def centre(q):
                nc.scalar.activation(xn[:, q, :], xn[:, q, :], ACT.Identity, bias=shift[:, q:q + 1], scale=inv_std[:, q:q + 1]).then_inc(centred, 1)
            if p is not None:
                act.wait_ge(shift_ready, START + p * 2 + 2)
                centre(0)
            for s in range(NQ + 2):
                m = s - 1
                if n is not None and 0 <= m < NM:
                    act.wait_ge(taps_added, START + n * (3 * NM) + 3 * m + 3)
                    nc.scalar.activation(xc_t[:, m, :], acc[:, m % 2, :], ACT.Silu).then_inc(silu_ready, 1)
                q = s - 1
                if p is not None and 0 <= q < NQ:
                    act.wait_ge(rest_ready, START + p * NQ + q + 1)
                    act.wait_ge(part2_out[q % 2], START + p * 64 + 16 * (q // 2))
                    act.wait_ge(part3_ready, START + p * NQ + max(q - 1, 0))
                    nc.scalar.copy(part2[:, q % 2, :], rest[:, q % 2, :]).then_inc(part2_ready, 1)
                q = s - 2
                if p is not None and q >= 0:
                    act.wait_ge(xproj_ready, START + p * NQ + q + 1)
                    nc.scalar.copy(xproj[:, q, 0:ALL], p_xproj[:, 0:ALL]).then_inc(xproj_copied, 1)
                m = s
                if n is not None and m < NM:
                    act.wait_ge(projected, START + n * NM + m + 1)
                    if m >= 2:
                        act.wait_ge(taps_added, START + n * (3 * NM) + 3 * (m - 1))
                    nc.scalar.activation(padded[:, m % 2, TAPS - 1:], p_rows[m % 2][:], ACT.Identity, bias=temb[:, m:m + 1]).then_inc(evicted, 1)
                    act.wait_ge(evicted, START + n * NM + m + 1)
                    nc.scalar.activation(acc[:, m % 2, :], padded[:, m % 2, TAPS - 1:], ACT.Identity, bias=b_conv[:, m:m + 1], scale=w_conv[:, m, TAPS - 1:TAPS]).then_inc(last_tap, 1)
                q = s
                if p is not None and q < NQ:
                    if q + 1 < NQ:
                        centre(q + 1)
                    act.wait_ge(xn_ready, START + p * NQ + q + 1)
                    act.wait_ge(part1_out[q % 2], START + p * 64 + 16 * (q // 2))
                    nc.scalar.copy(part1[:, q % 2, :], xn[:, q, :]).then_inc(part1_ready, 1)
                    act.wait_ge(squares_summed, START + p * NQ + q)
                    nc.scalar.activation(square[:], xn[:, q, :], ACT.Square, accum_out=sumsq[:, q:q + 1]).then_inc(squares_summed, 1)
            if p is not None:
                act.wait_ge(states_turned, START + p + 1)
                act.wait_ge(states_out, START + p * 80)
                nc.scalar.copy(proj_t[:], p_turn[0:ALL, :]).then_inc(states_copied, 1)
            if n is not None:
                for q in range(NQ):
                    act.wait_ge(turned, START + n * NQ + q + 1)
                    if p is not None:
                        act.wait_ge(xn_out[q % 2], START + n * 64)
                        act.wait_ge(rest_ready, START + n * NQ)
                    nc.scalar.copy(xn[:, q, :], p_rows[q % 2][:]).then_inc(turned_copied, 1)
                act.wait_ge(var_ready, START + n + 1)
                nc.scalar.activation(std[:], var_eps[:], ACT.Sqrt).then_inc(std_ready, 1)
            if p is not None:
                act.wait_ge(norm_steps, START + p * 6 + 2)
                nc.scalar.activation(root[:], sum_capped[:], ACT.Sqrt).then_inc(root_ready, 1)
                act.wait_ge(dt_ready, START + p + 1)
                act.wait_ge(decays_ready, START + p)
                nc.scalar.activation(dt_tanh[:], p_turn[0:STATES, :], ACT.Tanh, bias=b_dt[:]).then_inc(tanh_ready, 1)

        def pool_part(pool, p):
            for s in range(NQ + 1):
                q = s
                if q < NQ:
                    pool.wait_ge(centred, START + p * NQ + q + 1)
                    nc.gpsimd.tensor_tensor(out=xn[:, q, :], in0=xn[:, q, :], in1=ln_g[:], op=ALU.mult).then_inc(scaled, 1)
                q = s - 1
                if q >= 0:
                    pool.wait_ge(part2_ready, START + p * NQ + q + 1)
                    pool.wait_ge(part3_out[q % 2], START + p * 64 + 16 * (q // 2))
                    nc.gpsimd.tensor_tensor(out=part3[:, q % 2, :], in0=rest[:, q % 2, :], in1=part2[:, q % 2, :], op=ALU.subtract).then_inc(part3_ready, 1)

        def dve_part(dve, n, p):
            for s in range(NQ):
                q = m = s
                if p is not None:
                    dve.wait_ge(scaled, START + p * NQ + q + 1)
                    nc.vector.tensor_tensor(out=xn[:, q, :], in0=xn[:, q, :], in1=ln_b[:], op=ALU.add).then_inc(xn_ready, 1)
                if n is not None:
                    dve.wait_ge(last_tap, START + n * NM + m + 1)
                    for j in range(TAPS - 1):
                        if j:
                            dve.wait_ge(taps_added, START + n * (3 * NM) + 3 * m + j)
                        nc.vector.scalar_tensor_tensor(out=acc[:, m % 2, :], in0=padded[:, m % 2, j:j + SEQ], scalar=w_conv[:, m, j:j + 1], in1=acc[:, m % 2, :],
                                                       op0=ALU.mult, op1=ALU.add).then_inc(taps_added, 1)
                if p is not None:
                    dve.wait_ge(part1_ready, START + p * NQ + q + 1)
                    dve.wait_ge(part3_ready, START + p * NQ + max(q - 1, 0))
                    nc.vector.tensor_tensor(out=rest[:, q % 2, :], in0=xn[:, q, :], in1=part1[:, q % 2, :], op=ALU.subtract).then_inc(rest_ready, 1)
                    dve.wait_ge(xn_turned, START + p * NQ + q + 1)
                    dve.wait_ge(xproj_ready, START + p * NQ + max(q - 1, 0))
                    nc.vector.tensor_copy(out=xn_t[:, q % 2], in_=p_turn[:].rearrange("p (m t) -> p m t", m=NM)).then_inc(xn_t_ready, 1)
            if p is not None:
                dve.wait_ge(squares_summed, START + p * NQ + NQ)
                nc.vector.tensor_scalar(out=sum_capped[:], in0=sumsq[:], scalar1=1.0, scalar2=None, op0=ALU.min).then_inc(norm_steps, 1)
                nc.vector.tensor_scalar(out=at_least_one[:], in0=sumsq[:], scalar1=1.0, scalar2=None, op0=ALU.is_ge).then_inc(norm_steps, 1)
            if n is not None:
                for s in range(NQ + 1):
                    q = s
                    if q < NQ:
                        dve.wait_ge(turned_copied, START + n * NQ + q + 1)
                        for h in range(2):
                            nc.vector.bn_stats(out=stats[:, q, h, :], in_=xn[:, q, h * 512:h * 512 + 512]).then_inc(stats_ready, 1)
                    q = s - 1
                    if q >= 0:
                        dve.wait_ge(stats_ready, START + n * (2 * NQ) + 2 * q + 2)
                        nc.vector.memset(idle[:, q:q + 1], 0.0)
                        nc.vector.bn_aggr(out=mv[:, q, :], in_=stats[:, q]).then_inc(moments_ready, 1)
                dve.wait_ge(moments_ready, START + n * NQ + NQ)
                nc.vector.tensor_scalar(out=var_eps[:], in0=mv[:, :, 1], scalar1=1e-5, scalar2=None, op0=ALU.add).then_inc(var_ready, 1)
                dve.wait_ge(std_ready, START + n + 1)
                nc.vector.reciprocal(out=inv_std[:], in_=std[:]).then_inc(shift_ready, 1)
                dve.wait_ge(shift_ready, START + n * 2 + 1)
                nc.vector.scalar_tensor_tensor(out=shift[:], in0=mv[:, :, 0], scalar=-1.0, in1=inv_std[:], op0=ALU.mult, op1=ALU.mult).then_inc(shift_ready, 1)
            if p is not None:
                dve.wait_ge(root_ready, START + p + 1)
                nc.vector.tensor_tensor(out=norm_capped[:], in0=root[:], in1=at_least_one[:], op=ALU.max).then_inc(norm_steps, 1)
                dve.wait_ge(norm_steps, START + p * 6 + 3)
                nc.vector.tensor_scalar(out=norm_capped[:], in0=norm_capped[:], scalar1=1.0, scalar2=None, op0=ALU.min).then_inc(norm_steps, 1)
                dve.wait_ge(norm_steps, START + p * 6 + 4)
                dve.wait_ge(xproj_copied, START + p * NQ + NQ)
                dve.wait_ge(states_out, START + p * 80)
                nc.vector.tensor_tensor(out=b_whole[:], in0=xproj[:, :, 0:STATES], in1=norm_capped[:].rearrange("p (q o) -> p q o", o=1).to_broadcast([P, NQ, STATES]), op=ALU.mult).then_inc(norm_steps, 1)
                dve.wait_ge(norm_steps, START + p * 6 + 5)
                nc.vector.tensor_copy(out=b_part1[:], in_=b_whole[:]).then_inc(b_parts_ready, 1)
                dve.wait_ge(b_parts_ready, START + p * 3 + 1)
                nc.vector.tensor_tensor(out=b_rest[:], in0=b_whole[:], in1=b_part1[:], op=ALU.subtract).then_inc(norm_steps, 1)
                dve.wait_ge(norm_steps, START + p * 6 + 6)
                nc.vector.tensor_copy(out=b_part2[:], in_=b_rest[:]).then_inc(b_parts_ready, 1)
                dve.wait_ge(b_parts_ready, START + p * 3 + 2)
                nc.vector.tensor_tensor(out=b_part3[:], in0=b_rest[:], in1=b_part2[:], op=ALU.subtract).then_inc(b_parts_ready, 1)
                dve.wait_ge(tanh_ready, START + p + 2)
                nc.vector.tensor_scalar(out=decays[:], in0=dt_tanh[:], scalar1=neg_a[:], scalar2=1.0, op0=ALU.mult, op1=ALU.add).then_inc(decays_ready, 1)

        def batches(e, part):
            part(e, 0, None)
            e.wait_ge(late_consts, START + 96)
            with e.Fori(1, BATCH) as n:
                part(e, n, n - 1)
            part(e, None, BATCH - 1)

        with nc.Block() as block:
            @block.sync
            def _(sp):
                sp_part(sp, 0, None, True)
                with sp.Fori(1, BATCH - 1) as n:
                    sp_part(sp, n, n - 1, True)
                sp_part(sp, BATCH - 1, BATCH - 2, False)
                sp_part(sp, None, BATCH - 1, False)
                sp.wait_ge(states_out, START + 80 * BATCH)
                for t in xn_out + part1_out + part2_out + part3_out:
                    sp.wait_ge(t, START + 64 * BATCH)
            @block.tensor
            def _(pe):
                batches(pe, pe_part)
            @block.scalar
            def _(act):
                batches(act, act_part)
            @block.gpsimd
            def _(pool):
                pool.wait_ge(late_consts, START + 96)
                with pool.Fori(0, BATCH) as p:
                    pool_part(pool, p)
            @block.vector
            def _(dve):
                batches(dve, dve_part)
        return sems


def scan_phase(nc, I, Xp, Xn, Bp, Ad, Cm, Y, SG, X1, used_before):
    T = 16
    STEPS = 2 * T
    LOOPS = SEQ // STEPS
    ROWS = 2 * BATCH
    K = 6 * ROWS
    RING = 4
    LAG = P // STEPS
    assert LOOPS == BATCH * NQ and LAG == BATCH
    GC = 256
    gate_pieces = [("gate", h, n, k) for h in range(2) for n in range(HALF // GC) for k in range(NK)]
    turn_pieces = [("turn", g, i) for g in range(2) for i in range(2)]
    out_pieces = [("out", n, m) for n in range(MODEL // GC) for m in range(NM)]
    PIECES = gate_pieces[:-2] + turn_pieces[:2] + gate_pieces[-2:] + turn_pieces[2:] + out_pieces
    AT = [[p for c, p in enumerate(PIECES) if c * STEPS // len(PIECES) == u] for u in range(STEPS)]
    AHEAD = STEPS
    with ExitStack() as ctx:
        sb = lambda n, s, d: ctx.enter_context(nc.sbuf_tensor("b_" + n, s, d))
        pb = lambda n, s, d: ctx.enter_context(nc.psum_tensor("b_" + n, s, d))
        sems = []
        def sem(n):
            sems.append(ctx.enter_context(nc.semaphore("b_" + n)))
            return sems[-1]
        bd_all = sb("bd_all", [K, SEQ * STATES], bf16)
        decay_all = sb("decay_all", [128, SEQ], f32)
        c_all = sb("c_all", [128, SEQ], f32)
        mask_b = sb("mask_b", [K, 128], f32)
        mask_c = sb("mask_c", [128, T, 32], f32)
        x_moving = sb("x_moving", [K, 2, T * HALF], bf16)
        b_weights = sb("b_weights", [K, 2, T, 128], bf16)
        c_weights = sb("c_weights", [128, 2, T, 32], f32)
        decay = sb("decay", [128, 2, T], f32)
        z = sb("z", [128, HALF], f32)
        h = sb("h", [128, RING, HALF], f32)
        y_stage = sb("y_stage", [128, 2, T // 4, 128], f32)
        zeros = sb("zeros", [K, HALF], bf16)
        w_gate = sb("w_gate", [128, NK, INNER], f32); x_tile = sb("x_tile", [128, NK, 128], f32); sg = sb("sg", [128, 2, HALF], f32)
        w_out = sb("w_out", [P, NM, MODEL], f32); d_row = sb("d_row", [P, INNER], f32); ident = sb("ident", [P, P], f32)
        xn = sb("xn", [P, INNER], f32); y = sb("y", [P, INNER], f32); sg_in = sb("sg_in", [P, INNER], f32); yg = sb("yg", [P, INNER], f32)
        yg_t = sb("yg_t", [P, NM, P], f32); x = sb("x", [P, MODEL], f32); o = sb("o", [P, MODEL], f32); x1 = sb("x1", [P, MODEL], f32)
        p_turn = pb("p_turn", [P, HALF], f32); p_out = pb("p_out", [P, MODEL], f32)
        gate = [pb(f"gate{i}", [128, HALF], f32) for i in range(2)]
        bx = [pb(f"bx{i}", [128, HALF], f32) for i in range(2)]
        y_psum = [pb(f"y_psum{i}", [128, 512], f32) for i in range(2)]
        tile_in = sem("tile_in"); gate_ready = sem("gate_ready"); gate_taken = sem("gate_taken"); sg_out = [sem(f"sg_out{i}") for i in range(2)]
        weights_in = sem("weights_in"); others_in = sem("others_in"); xn_in = sem("xn_in"); y_in = sem("y_in"); res_in = sem("res_in"); mixed = sem("mixed"); gated = sem("gated"); turned = sem("turned"); turned_taken = sem("turned_taken")
        out_ready = sem("out_ready"); out_taken = sem("out_taken"); x1_ready = sem("x1_ready"); x1_out = sem("x1_out")
        consts_in = sem("consts_in"); zeros_ready = sem("zeros_ready")
        x_in = [sem(f"x_in{i}") for i in range(2)]
        w_ready = [sem(f"w_ready{i}") for i in range(2)]
        bx_ready = sem("bx_ready")
        z_ready = sem("z_ready")
        h_ready = sem("h_ready")
        read = sem("read")
        y_free = sem("y_free")
        y_out = [sem(f"y_out{i}") for i in range(2)]

        with nc.Block() as block:
            @block.sync
            def _(sp):
                start_counts(sp, sems)
                sp.dma_start(mask_b[:], I["mask_b"]).then_inc(consts_in, 16)
                sp.dma_start(mask_c[:], I["mask_c"]).then_inc(consts_in, 16)
                for half in range(2):
                    sp.dma_start(c_all[64 * half:64 * half + 64, :], Cm).then_inc(consts_in, 16)
                    sp.dma_start(decay_all[64 * half:64 * half + 64, :], Ad).then_inc(consts_in, 16)
                row = 0
                for part, copies in ((0, 3), (1, 2), (2, 1)):
                    for _ in range(2 * copies):
                        sp.dma_start(bd_all[row:row + BATCH, :], Bp[part].rearrange("b t d -> b (t d)")).then_inc(consts_in, 16)
                        row += BATCH
                sp.wait_ge(consts_in, START + 18 * 16)
            @block.vector
            def _(dve):
                nc.vector.memset(zeros[:], 0.0).then_inc(zeros_ready, 1)
                nc.vector.memset(h[:, RING - 1, :], 0.0).then_inc(zeros_ready, 1)
                nc.vector.memset(c_weights[:, 1, T - 1, :], 0.0).then_inc(zeros_ready, 1)
            @block.tensor
            def _(pe):
                pe.wait_ge(zeros_ready, START + 3)
                nc.tensor.matmul(y_psum[0][:], zeros[:, 0:128], zeros[:], start=True, stop=True).then_inc(read, AHEAD)
                nc.tensor.matmul(y_psum[1][:], zeros[:, 0:128], zeros[:], start=True, stop=True).then_inc(y_free, 1)

        nc.clear_and_free_semaphores(used_before)
        def load_mixed(sp, j, tq, b):
            sp.wait_ge(gated, START + j)
            sp.dma_start(xn[:], Xn[b, bass.ds(tq * P, P), :]).then_inc(xn_in, 16)
            for half in range(2):
                sp.wait_ge(sg_out[half], START + j * 16 + 16)
            sp.dma_start(sg_in[:], SG[bass.ds(j, 1)].rearrange("o p c -> (o p) c")).then_inc(xn_in, 16)
        def load_y(sp, j, tq, b, it):
            for i in range(2):
                sp.wait_ge(y_out[i], START + it * 64)
            sp.dma_start(y[:], Y[bass.ds(tq * P, P)].rearrange("t (h b) c -> b t h c", h=2)[b]).then_inc(y_in, 16)
        def load_x(sp, j, tq, b):
            sp.wait_ge(x1_ready, START + j)
            sp.dma_start(x[:], I["x"][b, bass.ds(tq * P, P), :]).then_inc(res_in, 16)
        def store_x1(sp, j):
            sp.wait_ge(x1_ready, START + j + 1)
            sp.dma_start(X1[bass.ds(j, 1)].rearrange("o p c -> (o p) c"), x1[:]).then_inc(x1_out, 16)

        def mix(e, engine, j):
            e.wait_ge(xn_in, START + j * 32 + 32)
            engine.tensor_tensor(out=xn[:], in0=xn[:], in1=d_row[:], op=ALU.mult).then_inc(mixed, 1)
            e.wait_ge(mixed, START + j * 2 + 1)
            e.wait_ge(y_in, START + j * 16 + 16)
            engine.tensor_tensor(out=xn[:], in0=xn[:], in1=y[:], op=ALU.add).then_inc(mixed, 1)
            e.wait_ge(mixed, START + j * 2 + 2)
            e.wait_ge(turned, START + j * 2)
            engine.tensor_tensor(out=yg[:], in0=xn[:], in1=sg_in[:], op=ALU.mult).then_inc(gated, 1)
        def add_x(e, engine, j):
            e.wait_ge(out_taken, START + j + 1)
            e.wait_ge(res_in, START + j * 16 + 16)
            e.wait_ge(x1_out, START + j * 16)
            engine.tensor_tensor(out=x1[:], in0=x[:], in1=o[:], op=ALU.add).then_inc(x1_ready, 1)

        def piece_of(pe, it, j, piece):
            if piece[0] == "gate":
                _, half, n, k = piece
                if piece == gate_pieces[0]:
                    pe.wait_ge(weights_in, START + 16)
                    pe.wait_ge(tile_in, START + it * 16 + 16)
                    pe.wait_ge(gate_taken, START + it * 2)
                c = half * HALF + n * GC
                mm = nc.tensor.matmul(gate[half][:, n * GC:(n + 1) * GC], x_tile[:, k, :], w_gate[:, k, c:c + GC], start=(k == 0), stop=(k == NK - 1))
                if n == HALF // GC - 1 and k == NK - 1:
                    mm.then_inc(gate_ready, 1)
            elif j is None:
                return
            elif piece[0] == "turn":
                _, g, i = piece
                if (g, i) == (0, 0):
                    pe.wait_ge(gated, START + j + 1)
                if (g, i) == (1, 0):
                    pe.wait_ge(turned_taken, START + j * 2 + 1)
                for m in (2 * i, 2 * i + 1):
                    mm = nc.tensor.transpose(p_turn[:, m * P:(m + 1) * P], yg[:, (4 * g + m) * P:(4 * g + m + 1) * P], ident[:])
                if i == 1:
                    mm.then_inc(turned, 1)
            else:
                _, n, m = piece
                if n == 0 and m % 4 == 0:
                    pe.wait_ge(turned_taken, START + j * 2 + m // 4 + 1)
                if (n, m) == (0, 0):
                    pe.wait_ge(out_taken, START + j)
                mm = nc.tensor.matmul(p_out[:, n * GC:(n + 1) * GC], yg_t[:, m, :], w_out[:, m, n * GC:(n + 1) * GC], start=(m == 0), stop=(m == NM - 1))
                if piece == out_pieces[-1]:
                    mm.then_inc(out_ready, 1)

        def take_gate(act, it, half):
            act.wait_ge(gate_ready, START + it * 2 + half + 1)
            act.wait_ge(sg_out[half], START + it * 16)
            nc.scalar.activation(sg[:, half, :], gate[half][:], ACT.Silu).then_inc(gate_taken, 1)
            act.wait_ge(gate_taken, START + it * 2 + half + 1)
            act.dma_start(SG[bass.ds(it, 1)].rearrange("o p c -> (o p) c")[:, half * HALF:(half + 1) * HALF], sg[:, half, :]).then_inc(sg_out[half], 16)
        def take_turned(act, j, g):
            act.wait_ge(turned, START + j * 2 + g + 1)
            act.wait_ge(out_ready, START + j)
            nc.scalar.copy(yg_t[:, 4 * g:4 * g + 4, :], p_turn[:].rearrange("p (m t) -> p m t", m=4)).then_inc(turned_taken, 1)
        def take_out(act, j):
            act.wait_ge(out_ready, START + j + 1)
            act.wait_ge(x1_ready, START + j)
            nc.scalar.copy(o[:], p_out[:]).then_inc(out_taken, 1)

        def sp_loop(sp, it, j, tq=None, b=None, out=False, weights=False):
            for i in range(2):
                sp.wait_ge(read, START + it * STEPS + (AHEAD - 15 if i == 0 else AHEAD + 1))
                t0 = it * STEPS + i * T
                for row, parts in ((0, 3), (24, 2), (40, 1)):
                    src = Xp[0:parts * ROWS, bass.ds(t0 * HALF, T * HALF)]
                    sp.dma_start(x_moving[row:row + parts * ROWS, i, :], src).then_inc(x_in[i], 16)
                if i == 0:
                    sp.wait_ge(gate_ready, START + it * 2)
                    sp.dma_start(x_tile[:], I["x_tiles"][bass.ds(it, 1)].rearrange("o p k t -> (o p) k t")).then_inc(tile_in, 16)
                    if weights:
                        sp.dma_start(w_gate[:], I["w_in_t"][:, INNER:2 * INNER].rearrange("(k p) n -> p k n", p=P)).then_inc(weights_in, 16)
                        for dst, src in ((w_out[:], I["w_out_t"].rearrange("(m p) n -> p m n", p=P)), (ident[:], I["ident"]),
                                         (d_row[:], I["D"].rearrange("(o n) -> o n", o=1).to_broadcast([P, INNER]))):
                            sp.dma_start(dst, src).then_inc(others_in, 16)
                    if j is not None:
                        load_mixed(sp, j, tq, b)
            if j is not None:
                load_y(sp, j, tq, b, it)
                if out:
                    store_x1(sp, j + (-1))
                load_x(sp, j, tq, b)

        def pool_loop(pool, it, j, out=False):
            for i in range(2):
                t0 = it * STEPS + i * T
                pool.wait_ge(read, START + it * STEPS + (AHEAD - 15 if i == 0 else AHEAD + 1))
                bd = bd_all[:, bass.ds(t0 * STATES, T * STATES)].rearrange("k (t o d) -> k t o d", o=1, d=STATES).to_broadcast([K, T, 8, STATES])
                mb = mask_b[:].rearrange("k (o r d) -> k o r d", o=1, d=STATES).to_broadcast([K, T, 8, STATES])
                nc.gpsimd.tensor_tensor(out=b_weights[:, i].rearrange("k t (r d) -> k t r d", d=STATES), in0=bd, in1=mb, op=ALU.mult).then_inc(w_ready[i], 1)
                cc = c_all[:, bass.ds(t0, T)].rearrange("p (t o) -> p t o", o=1).to_broadcast([128, T, 32])
                nc.gpsimd.tensor_tensor(out=c_weights[:, i], in0=cc, in1=mask_c[:], op=ALU.mult).then_inc(w_ready[i], 1)
                nc.gpsimd.tensor_copy(out=decay[:, i], in_=decay_all[:, bass.ds(t0, T)]).then_inc(w_ready[i], 1)
            if out:
                add_x(pool, nc.gpsimd, j + (-1))
            if j is not None:
                mix(pool, nc.gpsimd, j)

        def readout(pe, it, u):
            i, tt = (u // T) % 2, u % T
            pe.wait_ge(h_ready, START + it * (2 * STEPS) + 2 * (u + 1))
            if u % 4 == 0:
                pe.wait_ge(y_free, START + it * (STEPS // 4) + u // 4)
            for j in range(4):
                m = nc.tensor.matmul(y_psum[(u // 4) % 2][32 * j:32 * j + 32, 0:128], c_weights[:, i, tt, :],
                                     h[:, u % RING, 128 * j:128 * j + 128], start=(u % 4 == 0), stop=(u % 4 == 3), skip_group_check=True)
            m.then_inc(read, 1)

        def pe_loop(pe, it, j):
            for u in range(STEPS):
                i, tt = u // T, u % T
                if tt == 0:
                    pe.wait_ge(x_in[i], START + it * 48 + 48)
                    pe.wait_ge(w_ready[i], START + it * 3 + 3)
                if u == 0 or u == 1:
                    pe.wait_ge(h_ready, START + it * (2 * STEPS) + 2 * max(u - 1, 0))
                else:
                    pe.wait_ge(z_ready, START + it * (2 * STEPS) + 2 * (u - 1))
                nc.tensor.matmul(bx[u % 2][:], b_weights[:, i, tt, :], x_moving[:, i, tt * HALF:(tt + 1) * HALF],
                                 start=True, stop=True).then_inc(bx_ready, 1)
                for piece in AT[u]:
                    piece_of(pe, it, j, piece)
                readout(pe, it, u - 1)

        def dve_loop(dve, it):
            HW = HALF // 2
            for u in range(STEPS):
                i, tt = u // T, u % T
                if tt == 0:
                    dve.wait_ge(w_ready[i], START + it * 3 + 3)
                dve.wait_ge(bx_ready, START + it * STEPS + (u + 1))
                for g in range(2):
                    c = slice(g * HW, (g + 1) * HW)
                    dve.wait_ge(h_ready, START + it * (2 * STEPS) + max(2 * u - 1 + g, 0))
                    nc.vector.scalar_tensor_tensor(out=z[:, c], in0=h[:, (u - 1) % RING, c], scalar=decay[:, i, tt:tt + 1], in1=bx[u % 2][:, c],
                                                   op0=ALU.mult, op1=ALU.add).then_inc(z_ready, 1)
                dve.wait_ge(read, START + it * STEPS + (AHEAD + u - 2))
                for g in range(2):
                    c = slice(g * HW, (g + 1) * HW)
                    dve.wait_ge(z_ready, START + it * (2 * STEPS) + (2 * u + 1 + g))
                    nc.vector.tensor_scalar(out=h[:, u % RING, c], in0=z[:, c], scalar1=-10.0, scalar2=10.0,
                                            op0=ALU.max, op1=ALU.min).then_inc(h_ready, 1)

        def act_loop(act, it, j):
            for q in range(STEPS // 4):
                i = (4 * q) // T
                act.wait_ge(read, START + it * STEPS + (AHEAD + 4 * q + 5))
                if (4 * q) % T == 0:
                    act.wait_ge(y_out[i], START + it * 64)
                nc.scalar.copy(y_stage[:, i, q % (T // 4), :], y_psum[q % 2][:, 0:128]).then_inc(y_free, 1)
                if (4 * q + 4) % T == 0:
                    act.wait_ge(y_free, START + it * (STEPS // 4) + (q + 2))
                    dst = Y[bass.ds(it * STEPS + i * T, T)].rearrange("(q s) r (j c) -> j (s r) q c", s=4, j=4)
                    for part in range(4):
                        act.dma_start(dst[part], y_stage[32 * part:32 * part + 32, i]).then_inc(y_out[i], 16)
                if q == 1:
                    take_gate(act, it, 0)
                if q == 2 and j is not None:
                    take_turned(act, j, 0)
                if q == 3 and j is not None:
                    take_turned(act, j, 1)
                if q == 4:
                    take_gate(act, it, 1)
                if q == 7 and j is not None:
                    take_out(act, j)

        TILES = BATCH * NQ
        with nc.Block() as block:
            @block.sync
            def _(sp):
                sp_loop(sp, 0, None, weights=True)
                with sp.Fori(1, LAG) as it:
                    sp_loop(sp, it, None)
                for b in range(BATCH):
                    sp_loop(sp, LAG + b, b, 0, b, b > 0)
                with sp.Fori(1, NQ - 1) as tq:
                    for b in range(BATCH):
                        j = tq * BATCH + b
                        sp_loop(sp, j + LAG, j, tq, b, True)
                first = TILES - LAG
                for b in range(BATCH + 1):
                    j = first + b
                    if b < BATCH:
                        load_mixed(sp, j, NQ - 1, b)
                        load_y(sp, j, NQ - 1, b, LOOPS)
                    if b:
                        store_x1(sp, j - 2)
                        load_x(sp, j - 1, NQ - 1, b - 1)
                store_x1(sp, TILES - 1)
                sp.wait_ge(x1_out, START + TILES * 16)
            @block.gpsimd
            def _(pool):
                with pool.Fori(0, LAG) as it:
                    pool_loop(pool, it, None)
                pool.wait_ge(others_in, START + 48)
                pool_loop(pool, LAG, 0)
                with pool.Fori(1, TILES - LAG) as j:
                    pool_loop(pool, j + LAG, j, True)
            @block.tensor
            def _(pe):
                with pe.Fori(0, LAG) as it:
                    pe_loop(pe, it, None)
                pe.wait_ge(others_in, START + 48)
                with pe.Fori(0, TILES - LAG) as j:
                    pe_loop(pe, j + LAG, j)
                readout(pe, LOOPS, -1)
                with pe.Fori(TILES - LAG, TILES) as j:
                    for piece in turn_pieces + out_pieces:
                        piece_of(pe, None, j, piece)
            @block.vector
            def _(dve):
                with dve.Fori(0, LOOPS) as it:
                    dve_loop(dve, it)
                with dve.Fori(TILES - LAG, TILES) as j:
                    mix(dve, nc.vector, j)
                    add_x(dve, nc.vector, j + (-1))
                add_x(dve, nc.vector, TILES - 1)
            @block.scalar
            def _(act):
                with act.Fori(0, LAG) as it:
                    act_loop(act, it, None)
                with act.Fori(0, TILES - LAG) as j:
                    act_loop(act, j + LAG, j)
                with act.Fori(TILES - LAG, TILES) as j:
                    take_turned(act, j, 0)
                    take_turned(act, j, 1)
                    take_out(act, j)
                for i in range(2):
                    act.wait_ge(y_out[i], START + LOOPS * 64)
                    act.wait_ge(sg_out[i], START + LOOPS * 16)


def proj_phase(nc, I, X1, QK, V, X2, WDC):
    NP = 2 * NK
    STEPS = NQ + NP
    with ExitStack() as ctx:
        sb = lambda n, s, d=f32: ctx.enter_context(nc.sbuf_tensor("d_" + n, s, d))
        pb = lambda n, s, d=f32: ctx.enter_context(nc.psum_tensor("d_" + n, s, d))
        sems = []
        def sem(n):
            sems.append(ctx.enter_context(nc.semaphore("d_" + n)))
            return sems[-1]
        mats = "qkvwu"
        w_u = sb("w_u", [P, NK, MODEL])
        w_hi = {j: sb(f"w_{j}_hi", [P, NK, MODEL], f32r) for j in "qkv"}; w_lo = {j: sb(f"w_{j}_lo", [P, NK, MODEL], f32r) for j in "qkv"}
        ident = sb("ident", [P, P])
        v_rows = sb("v_rows", [P, BATCH, MODEL]); u_row = sb("u_row", [P, MODEL]); s1_row = sb("s1_row", [P, MODEL])
        qk = sb("qk", [P, 2 * NK * BATCH]); qk_col = sb("qk_col", [P, NK * BATCH]); idle = sb("idle", [P, 1])
        p_turn = pb("p_turn", [P, MODEL]); p_v = pb("p_v", [P, MODEL]); p_v_turn = pb("p_v_turn", [P, MODEL]); p_skip = pb("p_skip", [P, MODEL])
        p_qk = [pb(f"p_qk{i}", [P, SEQ]) for i in range(2)]
        consts = sem("consts"); styles = sem("styles"); act_setup = sem("act_setup"); sums = sem("sums"); dve_setup = sem("dve_setup"); rows_in = sem("rows_in"); row_in = sem("row_in")
        x_in = [sem(f"x_in{i}") for i in range(NQ)]
        scaled = sem("scaled"); stats_ready = sem("stats_ready"); moments_ready = sem("moments_ready"); var_ready = sem("var_ready"); std_ready = sem("std_ready"); shift_ready = sem("shift_ready"); xl_ready = sem("xl_ready")
        xl_turned = sem("xl_turned"); high_ready = sem("high_ready"); low_ready = sem("low_ready"); v_products = sem("v_products"); v_ready = sem("v_ready"); v_turned = sem("v_turned"); v_t_ready = sem("v_t_ready"); skip_ready = sem("skip_ready"); x2_ready = sem("x2_ready"); u_scaled = sem("u_scaled")
        qk_products = sem("qk_products"); qk_copied = sem("qk_copied"); hi_ready = sem("hi_ready"); lo_ready = sem("lo_ready")
        v_out = [sem(f"v_out{i}") for i in range(2)]; x2_out = [sem(f"x2_out{i}") for i in range(2)]; qk_out = [sem(f"qk_out{i}") for i in range(2)]
        x1 = sb("x1", [P, NQ, MODEL]); xl = sb("xl", [P, NQ, MODEL])
        stats = sb("stats", [P, NQ, 6]); mv = sb("mv", [P, NQ, 2]); var_eps = sb("var_eps", [P, NQ]); std = sb("std", [P, NQ]); inv_std = sb("inv_std", [P, NQ]); shift = sb("shift", [P, NQ])
        def load_rows(sp, n):
            sp.dma_start(s1_row[:], I["t_emb"][bass.ds(n, 1), 0:MODEL].to_broadcast([P, MODEL])).then_inc(row_in, 16)
            sp.dma_start(u_row[:], WDC[2, bass.ds(n, 1), :].to_broadcast([P, MODEL])).then_inc(row_in, 16)
        rows = sb("rows", [BATCH, 3, MODEL]); wu_b = sb("wu_b", [P, NK, MODEL])

        def load_x1(sp, n, q):
            sp.dma_start(x1[:, q, :], X1.rearrange("(q b) t c -> b q t c", b=BATCH)[bass.ds(n, 1)].rearrange("o q t c -> (o q) t c")[q]).then_inc(x_in[q], 16)
        def scale_x1(pool, n, q, first):
            pool.wait_ge(x_in[q], START + n * 16 + 16)
            if not first:
                pool.wait_ge(xl_turned, START + n * NQ - NQ + q + 1)
            if q == 0:
                pool.wait_ge(row_in, START + n * 32 + (16 if first else 32))
            nc.gpsimd.tensor_tensor(out=xl[:, q, :], in0=x1[:, q, :], in1=s1_row[:], op=ALU.mult).then_inc(scaled, 1)
        def scale_u(pool, n, first):
            if first:
                pool.wait_ge(row_in, START + 32)
            else:
                pool.wait_ge(skip_ready, START + n * NQ)
            nc.gpsimd.tensor_tensor(out=wu_b[:], in0=w_u[:], in1=u_row[:].rearrange("p (o n) -> p o n", o=1).to_broadcast([P, NK, MODEL]), op=ALU.mult).then_inc(u_scaled, 1)
        def two_stats(dve, n, q):
            for i in (q, q + 1):
                dve.wait_ge(scaled, START + n * NQ + i + 1)
                nc.vector.bn_stats(out=stats[:, i, :], in_=xl[:, i, :]).then_inc(stats_ready, 1)
            dve.wait_ge(stats_ready, START + n * NQ + q + 2)
            nc.vector.memset(idle[:], 0.0)
            for i in (q, q + 1):
                nc.vector.bn_aggr(out=mv[:, i, :], in_=stats[:, i, :]).then_inc(moments_ready, 1)
        def add_eps(dve, n):
            dve.wait_ge(moments_ready, START + n * NQ + NQ)
            nc.vector.tensor_scalar(out=var_eps[:], in0=mv[:, :, 1], scalar1=1e-5, scalar2=None, op0=ALU.add).then_inc(var_ready, 1)
        def invert_std(dve, n):
            dve.wait_ge(std_ready, START + n + 1)
            nc.vector.reciprocal(out=inv_std[:], in_=std[:]).then_inc(shift_ready, 1)
            dve.wait_ge(shift_ready, START + n * 2 + 1)
            nc.vector.scalar_tensor_tensor(out=shift[:], in0=mv[:, :, 0], scalar=-1.0, in1=inv_std[:], op0=ALU.mult, op1=ALU.mult).then_inc(shift_ready, 1)
        def root(act, n):
            act.wait_ge(var_ready, START + n + 1)
            nc.scalar.activation(std[:], var_eps[:], ACT.Sqrt).then_inc(std_ready, 1)
        def normalise(act, n, q):
            act.wait_ge(shift_ready, START + n * 2 + 2)
            nc.scalar.activation(xl[:, q, :], xl[:, q, :], ACT.Identity, bias=shift[:, q:q + 1], scale=inv_std[:, q:q + 1]).then_inc(xl_ready, 1)

        with ExitStack() as setup:
            tb = lambda n, s: setup.enter_context(nc.sbuf_tensor("d_" + n, s, f32))
            w = {j: tb("w_" + j, [P, NK, MODEL]) for j in "qkvw"} | {"u": w_u}
            w2 = [tb(f"w2_{i}", [P, NK, MODEL]) for i in range(2)]
            s_col = tb("s_col", [P, 2 * NK, BATCH]); ssq = tb("ssq", [P, 2 * NK, BATCH])
            s2_rows = tb("s2_rows", [BATCH, MODEL])
            split = sem("split")
            with nc.Block() as block:
                @block.sync
                def _(sp):
                    start_counts(sp, sems)
                    for b in range(BATCH):
                        sp.dma_start(s_col[:, :, b], I["t_emb"][b].rearrange("(m p) -> p m", p=P), allow_slow_non_contiguous=True).then_inc(styles, 16)
                    sp.dma_start(s2_rows[:], I["t_emb"][:, MODEL:2 * MODEL]).then_inc(styles, 16)
                    sp.dma_start(ident[:], I["ident"]).then_inc(styles, 16)
                    sp.dma_start(s1_row[:], I["t_emb"][0:1, 0:MODEL].to_broadcast([P, MODEL])).then_inc(row_in, 16)
                    for n, j in enumerate(mats):
                        if n:
                            sp.wait_ge(consts, START + 16 * n)
                        sp.dma_start(w[j][:], I[j + "_t"].rearrange("(k p) n -> p k n", p=P)).then_inc(consts, 16)
                        for q in ((0, 1), (2, 3), (4, 5), (6, 7), ())[n]:
                            load_x1(sp, 0, q)
                @block.gpsimd
                def _(pool):
                    for q in range(NQ):
                        scale_x1(pool, 0, q, True)
                @block.scalar
                def _(act):
                    act.wait_ge(styles, START + 16 * (BATCH + 2))
                    nc.scalar.activation(ssq[:], s_col[:], ACT.Square).then_inc(act_setup, 1)
                    for n, j in enumerate(mats):
                        act.wait_ge(consts, START + 16 * (n + 1))
                        if n >= 2:
                            act.wait_ge(sums, START + n - 1)
                        nc.scalar.activation(w2[n % 2][:], w[j][:], ACT.Square).then_inc(act_setup, 1)
                    act.wait_ge(dve_setup, START + 4)
                    nc.scalar.activation(rows[:], rows[:], ACT.Sqrt).then_inc(act_setup, 1)
                    nc.scalar.activation(qk[:], qk[:], ACT.Sqrt).then_inc(act_setup, 1)
                    root(act, 0)
                    for q in range(NQ):
                        normalise(act, 0, q)
                @block.tensor
                def _(pe):
                    for n, j in enumerate(mats):
                        pe.wait_ge(act_setup, START + n + 2)
                        if n < 2:
                            for ot in range(NK):
                                for k in range(NK):
                                    c = (n * NK + ot) * BATCH
                                    mm = nc.tensor.matmul(p_turn[:, c:c + BATCH], w2[n % 2][:, k, ot * P:(ot + 1) * P], ssq[:, k, :], start=(k == 0), stop=(k == NK - 1))
                        else:
                            for k in range(NK):
                                mm = nc.tensor.matmul((p_v, p_v_turn, p_skip)[n - 2][0:BATCH, :], ssq[:, (0 if n == 2 else NK) + k, :], w2[n % 2][:, k, :], start=(k == 0), stop=(k == NK - 1))
                        mm.then_inc(sums, 1)
                @block.vector
                def _(dve):
                    for n, j in enumerate("qkv"):
                        dve.wait_ge(consts, START + 16 * (n + 1))
                        nc.vector.tensor_copy(out=w_hi[j][:], in_=w[j][:]).then_inc(split, 1)
                        dve.wait_ge(split, START + n + 1)
                        nc.vector.tensor_tensor(out=w_lo[j][:], in0=w[j][:], in1=w_hi[j][:].bitcast(f32), op=ALU.subtract)
                    dve.wait_ge(sums, START + 2)
                    nc.vector.tensor_scalar(out=qk[:], in0=p_turn[:, 0:2 * NK * BATCH], scalar1=1e-8, scalar2=None, op0=ALU.add).then_inc(dve_setup, 1)
                    for n in range(3):
                        dve.wait_ge(sums, START + 3 + n)
                        nc.vector.tensor_scalar(out=rows[:, n, :], in0=(p_v, p_v_turn, p_skip)[n][0:BATCH, :], scalar1=1e-8, scalar2=None, op0=ALU.add).then_inc(dve_setup, 1)
                    for q in range(0, NQ, 2):
                        two_stats(dve, 0, q)
                    add_eps(dve, 0)
                    dve.wait_ge(act_setup, START + 8)
                    nc.vector.reciprocal(out=qk[:], in_=qk[:]).then_inc(dve_setup, 1)
                    nc.vector.reciprocal(out=rows[:], in_=rows[:]).then_inc(dve_setup, 1)
                    dve.wait_ge(dve_setup, START + 6)
                    nc.vector.scalar_tensor_tensor(out=qk_col[:], in0=qk[:, 0:NK * BATCH], scalar=float(np.float32(HD) ** np.float32(-0.5)), in1=qk[:, NK * BATCH:], op0=ALU.mult, op1=ALU.mult).then_inc(dve_setup, 1)
                    nc.vector.tensor_tensor(out=rows[:, 0, :], in0=rows[:, 0, :], in1=s2_rows[:], op=ALU.mult).then_inc(dve_setup, 1)
                    invert_std(dve, 0)

        xl_hi = sb("xl_hi", [P, NK, SEQ], f32r); xl_lo = sb("xl_lo", [P, NK, SEQ], f32r)
        v = sb("v", [P, 2, MODEL]); v_t = sb("v_t", [P, NK, P]); x2 = sb("x2", [P, 2, MODEL]);
        whole = sb("whole", [P, 2, SEQ]); hi = sb("hi", [P, 2, SEQ], f32r); lo = sb("lo", [P, 2, SEQ], f32r)

        def batches(e, body):
            with e.Fori(0, BATCH - 1) as b:
                body(b, True)
            body(BATCH - 1, False)

        with nc.Block() as block:
            @block.sync
            def _(sp):
                sp.dma_start(WDC.rearrange("j b n -> b j n"), rows[:]).then_inc(rows_in, 16)
                sp.wait_ge(rows_in, START + 16)
                sp.dma_start(u_row[:], WDC[2, 0:1, :].to_broadcast([P, MODEL])).then_inc(row_in, 16)
                for b in range(BATCH):
                    sp.dma_start(v_rows[:, b, :], WDC[0, b:b + 1, :].to_broadcast([P, MODEL])).then_inc(rows_in, 16)
                def body(b, ahead):
                    if ahead:
                        sp.wait_ge(u_scaled, START + b + 1)
                        load_rows(sp, b + 1)
                    for s in range(STEPS + 1):
                        q = s - 2
                        if 0 <= q < NQ:
                            sp.wait_ge(v_ready, START + b * NQ + q + 1)
                            sp.dma_start(V.rearrange("(b g) t c -> b t g c", b=BATCH)[bass.ds(b, 1)].rearrange("o t g c -> (o t) g c")[q * P:(q + 1) * P], v[:, q % 2, :].rearrange("p (g c) -> p g c", c=P)).then_inc(v_out[q % 2], 16)
                        q = s - 4
                        if 0 <= q < NQ:
                            sp.wait_ge(x2_ready, START + b * NQ + q + 1)
                            sp.dma_start(X2[bass.ds(b, 1)].rearrange("o t c -> (o t) c")[q * P:(q + 1) * P, :], x2[:, q % 2, :]).then_inc(x2_out[q % 2], 16)
                            if ahead:
                                load_x1(sp, b + 1, q)
                        e = s - NQ - 1
                        if e >= 0:
                            ot, j = e // 2, e % 2
                            for part, t, s_t in ((0, hi, hi_ready), (1, lo, lo_ready)):
                                sp.wait_ge(s_t, START + b * NP + e + 1)
                                dst = QK[2 * j + part].rearrange("b (t p) s -> b t p s", p=P)[bass.ds(b, 1)].rearrange("o t p s -> (o t) p s")[ot]
                                sp.dma_start(dst, t[:, e % 2, :].bitcast(f32)).then_inc(qk_out[e % 2], 16)
                batches(sp, body)
                for i in range(2):
                    sp.wait_ge(v_out[i], START + 64 * BATCH)
                    sp.wait_ge(x2_out[i], START + 64 * BATCH)
                    sp.wait_ge(qk_out[i], START + 128 * BATCH)
            @block.gpsimd
            def _(pool):
                scale_u(pool, 0, True)
                with pool.Fori(0, BATCH - 1) as b:
                    for q in range(NQ):
                        scale_x1(pool, b + 1, q, False)
                    scale_u(pool, b + 1, False)
            @block.tensor
            def _(pe):
                def body(b, ahead):
                    for s in range(STEPS):
                        q = s
                        if q < NQ:
                            pe.wait_ge(xl_ready, START + b * NQ + q + 1)
                            pe.wait_ge(low_ready, START + b * NQ + q)
                            for k in range(NK):
                                mm = nc.tensor.transpose(p_turn[:, k * P:(k + 1) * P], xl[:, q, k * P:(k + 1) * P], ident[:])
                            mm.then_inc(xl_turned, 1)
                        q = s - 1
                        if 0 <= q < NQ:
                            pe.wait_ge(low_ready, START + b * NQ + q + 1)
                            pe.wait_ge(v_ready, START + b * NQ + q)
                            for k in range(NK):
                                for part, (rows_part, w_part) in enumerate(((xl_hi, w_hi), (xl_hi, w_lo), (xl_lo, w_hi))):
                                    mm = nc.tensor.matmul(p_v[:], rows_part[:, k, q * P:(q + 1) * P], w_part["v"][:, k, :], start=(k == 0 and part == 0), stop=(k == NK - 1 and part == 2))
                            mm.then_inc(v_products, 1)
                        q = s - 2
                        if 0 <= q < NQ:
                            pe.wait_ge(v_ready, START + b * NQ + q + 1)
                            pe.wait_ge(v_t_ready, START + b * NQ + q)
                            for k in range(NK):
                                mm = nc.tensor.transpose(p_v_turn[:, k * P:(k + 1) * P], v[:, q % 2, k * P:(k + 1) * P], ident[:])
                            mm.then_inc(v_turned, 1)
                        q = s - 3
                        if 0 <= q < NQ:
                            pe.wait_ge(v_t_ready, START + b * NQ + q + 1)
                            pe.wait_ge(x2_ready, START + b * NQ + q)
                            if q == 0:
                                pe.wait_ge(u_scaled, START + b + 1)
                            for k in range(NK):
                                mm = nc.tensor.matmul(p_skip[:], v_t[:, k, :], wu_b[:, k, :], start=(k == 0), stop=(k == NK - 1))
                            mm.then_inc(skip_ready, 1)
                        e = s - NQ
                        if e >= 0:
                            ot, j = e // 2, e % 2
                            pe.wait_ge(qk_copied, START + b * NP + max(e - 1, 0))
                            for h in range(NH):
                                for k in range(NK):
                                    for part, (w_part, rows_part) in enumerate(((w_hi, xl_hi), (w_hi, xl_lo), (w_lo, xl_hi))):
                                        mm = nc.tensor.matmul(p_qk[e % 2][:, h * 512:h * 512 + 512], w_part["qk"[j]][:, k, ot * P:(ot + 1) * P], rows_part[:, k, h * 512:h * 512 + 512], start=(k == 0 and part == 0), stop=(k == NK - 1 and part == 2))
                            mm.then_inc(qk_products, 1)
                batches(pe, body)
            @block.scalar
            def _(act):
                def body(b, ahead):
                    for s in range(STEPS):
                        q = s
                        if q < NQ:
                            act.wait_ge(xl_turned, START + b * NQ + q + 1)
                            if q == 0:
                                act.wait_ge(qk_products, START + b * NP)
                            nc.scalar.copy(xl_hi[:, :, q * P:(q + 1) * P], p_turn[:].rearrange("p (k t) -> p k t", k=NK)).then_inc(high_ready, 1)
                        q = s - 2
                        if 0 <= q < NQ:
                            act.wait_ge(v_turned, START + b * NQ + q + 1)
                            act.wait_ge(skip_ready, START + b * NQ + q)
                            nc.scalar.copy(v_t[:], p_v_turn[:].rearrange("p (k t) -> p k t", k=NK)).then_inc(v_t_ready, 1)
                        e = s - NQ
                        if e >= 0:
                            ot, j = e // 2, e % 2
                            act.wait_ge(qk_products, START + b * NP + e + 1)
                            act.wait_ge(lo_ready, START + b * NP + max(e - 1, 0))
                            if j == 0:
                                scale = qk_col[:].rearrange("p (t b) -> p t b", b=BATCH)[:, ot, bass.ds(b, 1)]
                                nc.scalar.activation(whole[:, e % 2, :], p_qk[e % 2][:], ACT.Identity, scale=scale, bias=0.0).then_inc(qk_copied, 1)
                            else:
                                nc.scalar.copy(whole[:, e % 2, :], p_qk[e % 2][:]).then_inc(qk_copied, 1)
                        if ahead and e == 4:
                            root(act, b + 1)
                        if ahead and e in (5, 6):
                            for i in range(NQ // 2):
                                normalise(act, b + 1, (e - 5) * (NQ // 2) + i)
                batches(act, body)
            @block.vector
            def _(dve):
                def body(b, ahead):
                    for s in range(STEPS):
                        q = s
                        if q < NQ:
                            dve.wait_ge(high_ready, START + b * NQ + q + 1)
                            nc.vector.tensor_tensor(out=xl_lo[:, :, q * P:(q + 1) * P], in0=p_turn[:].rearrange("p (k t) -> p k t", k=NK), in1=xl_hi[:, :, q * P:(q + 1) * P].bitcast(f32), op=ALU.subtract).then_inc(low_ready, 1)
                        q = s - 1
                        if q == 0:
                            dve.wait_ge(rows_in, START + 16 + 16 * BATCH)
                        if 0 <= q < NQ:
                            dve.wait_ge(v_products, START + b * NQ + q + 1)
                            dve.wait_ge(v_out[q % 2], START + b * 64 + 16 * (q // 2))
                            dve.wait_ge(v_turned, START + b * NQ + max(q - 1, 0))
                            nc.vector.tensor_tensor(out=v[:, q % 2, :], in0=v_rows[:].rearrange("p b n -> p (b n)")[:, bass.ds(b * MODEL, MODEL)], in1=p_v[:], op=ALU.mult).then_inc(v_ready, 1)
                        q = s - 3
                        if 0 <= q < NQ:
                            dve.wait_ge(skip_ready, START + b * NQ + q + 1)
                            dve.wait_ge(x2_out[q % 2], START + b * 64 + 16 * (q // 2))
                            nc.vector.tensor_tensor(out=x2[:, q % 2, :], in0=x1[:, q, :], in1=p_skip[:], op=ALU.add).then_inc(x2_ready, 1)
                        e = s - NQ
                        if e >= 0:
                            dve.wait_ge(qk_copied, START + b * NP + e + 1)
                            dve.wait_ge(qk_out[e % 2], START + b * 128 + 32 * (e // 2))
                            nc.vector.tensor_copy(out=hi[:, e % 2, :], in_=whole[:, e % 2, :]).then_inc(hi_ready, 1)
                            dve.wait_ge(hi_ready, START + b * NP + e + 1)
                            nc.vector.tensor_tensor(out=lo[:, e % 2, :], in0=whole[:, e % 2, :], in1=hi[:, e % 2, :].bitcast(f32), op=ALU.subtract).then_inc(lo_ready, 1)
                        if ahead and 0 <= e < NQ // 2:
                            two_stats(dve, b + 1, 2 * e)
                        if ahead and e == 4:
                            add_eps(dve, b + 1)
                            invert_std(dve, b + 1)
                batches(dve, body)


def attention_phase(nc, I, QK, V, OT):
    GROUP = P // HD
    NGROUPS = BATCH * HEADS // GROUP
    KROWS = 3 * HD
    STACK = KROWS + 1
    ROWS = GROUP * NQ
    UNITS = ROWS * NH
    STEPS = NH * NQ
    HALFQ = SEQ // NH
    PIECES = 4
    RING = 3
    PAIRS = STEPS // 2
    LATER = 4
    DEN_STEP = {LATER - 2: 1, NQ + LATER - 2: 0}
    INVERT = {4: (1, 0), 6: (1, 1), 8: (1, 2), 10: (1, 3), 12: (0, 0), 13: (0, 1), 14: (0, 2), 15: (0, 3)}
    TURN_STEP = STEPS - 2
    PER_STEP = [(5, 4)[s % 2] for s in range(TURN_STEP)]
    PER_STEP += [UNITS - sum(PER_STEP), 0]
    assert 0 <= PER_STEP[TURN_STEP] <= 2
    with ExitStack() as ctx:
        sb = lambda n, s, d=f32: ctx.enter_context(nc.sbuf_tensor("e_" + n, s, d))
        pb = lambda n, s, d=f32: ctx.enter_context(nc.psum_tensor("e_" + n, s, d))
        sems = []
        def sem(n):
            sems.append(ctx.enter_context(nc.semaphore("e_" + n)))
            return sems[-1]
        qs = [sb(f"qs{i}", [STACK, GROUP, SEQ], f32r) for i in range(RING)]
        ks = [sb(f"ks{i}", [STACK, GROUP, SEQ], f32r) for i in range(RING)]
        v = [sb(f"v{i}", [P, NQ, P]) for i in range(RING)]
        ident = sb("ident", [P, P]); ones = sb("ones", [P, HD])
        half_max = sb("half_max", [P, ROWS, NH]); row_max = sb("row_max", [P, ROWS])
        neg_row = [sb(f"neg_row{i}", [ROWS, P], f32r) for i in range(RING)]
        probs = sb("probs", [P, 4, GROUP, HALFQ]); pair_sum = sb("pair_sum", [P, 2, GROUP, HALFQ])
        den = sb("den", [P, NH, HALFQ]); rden = sb("rden", [P, NH, HALFQ]); raw = sb("raw", [P, NH, HALFQ]); o = sb("o", [P, NH, HALFQ])
        p_max = [pb(f"p_max{i}", [P, 512]) for i in range(2)]; p_exp = [pb(f"p_exp{i}", [P, 2, HALFQ]) for i in range(2)]
        p_o = pb("p_o", [P, HALFQ]); p_d = pb("p_d", [P, HALFQ])
        consts = sem("consts"); cleared = sem("cleared")
        stacks_in = [sem(f"stacks_in{i}") for i in range(RING)]; max_in = [sem(f"max_in{i}") for i in range(RING)]
        unit_scores = sem("unit_scores"); unit_max = sem("unit_max"); max_turned = sem("max_turned"); max_row = sem("max_row"); max_whole = sem("max_whole")
        scores = sem("scores"); exps = sem("exps"); products = sem("products"); paired = sem("paired"); key_sums = sem("key_sums")
        den_taken = sem("den_taken"); raw_taken = sem("raw_taken")
        rden_ready = [sem(f"rden_ready{i}") for i in range(NH)]; o_ready = [sem(f"o_ready{i}") for i in range(NH)]
        o_out = [sem(f"o_out{i}") for i in range(NH)]
        LOADS = 7 * 16


        def load(sp, n, i):
            for stack, order in ((qs[i], (0, 0, 1)), (ks[i], (2, 3, 2))):
                for row, part in enumerate(order):
                    src = QK[part].rearrange("b (g h p) s -> (b g) p h s", h=GROUP, p=HD)[bass.ds(n, 1)].rearrange("o p h s -> (o p) h s")
                    sp.dma_start(stack[row * HD:(row + 1) * HD].bitcast(f32), src).then_inc(stacks_in[i], 16)
            sp.dma_start(v[i][:], V[bass.ds(n, 1)].rearrange("o (q p) c -> p (o q) c", p=P)).then_inc(stacks_in[i], 16)

        def send_max(sp, n, i):
            sp.wait_ge(max_row, START + n + 1)
            sp.dma_start(qs[i][KROWS:STACK].rearrange("o h (q c) -> o (h q) c", c=P).bitcast(f32), neg_row[i][:].bitcast(f32)).then_inc(max_in[i], 16)

        def max_unit(pe, n, i, turn, u):
            row, half = divmod(u, NH)
            h, q = divmod(row, NQ)
            if u == 0:
                pe.wait_ge(stacks_in[i], START + turn * LOADS + LOADS)
            if u == 1:
                pe.wait_ge(max_row, START + n)
            pe.wait_ge(unit_max, START + n * UNITS + max(u - 1, 0))
            nc.tensor.matmul(p_max[u % 2][:], qs[i][0:KROWS, h, q * P:(q + 1) * P], ks[i][0:KROWS, h, half * 512:(half + 1) * 512], start=True, stop=True).then_inc(unit_scores, 1)

        def turn_max(pe, n):
            pe.wait_ge(max_whole, START + n + 1)
            nc.tensor.transpose(p_max[1][0:ROWS, 0:P], row_max[:], ident[:]).then_inc(max_turned, 1)

        def scores_pair(pe, n, i, s, pair):
            half, kt = divmod(s, NQ)
            pe.wait_ge(exps, START + n * (2 * STEPS) + (2 * s - 1 + pair))
            for j in range(2):
                h = 2 * pair + j
                mm = nc.tensor.matmul(p_exp[pair][:, j, :], ks[i][:, h, kt * P:(kt + 1) * P], qs[i][:, h, half * HALFQ:(half + 1) * HALFQ], start=True, stop=True)
            mm.then_inc(scores, 1)

        def products_o(pe, n, i, s):
            kt = s % NQ
            pe.wait_ge(exps, START + n * (2 * STEPS) + 2 * (s + 1))
            if kt == 0:
                pe.wait_ge(raw_taken, START + n * NH + s // NQ + 1)
            vi = v[i if s >= 0 else (i - 1) % RING]
            for h in range(GROUP):
                mm = nc.tensor.matmul(p_o[HD * h:HD * (h + 1), :], vi[:, kt, HD * h:HD * (h + 1)], probs[:, s % 4, h, :], start=(kt == 0), stop=(kt == NQ - 1), skip_group_check=True)
            mm.then_inc(products, 1)

        def sum_keys(pe, n, s):
            t = s // 2 - LATER // 2
            pe.wait_ge(paired, START + n * PAIRS + t + 1)
            if t % (NQ // 2) == 0:
                pe.wait_ge(den_taken, START + n * NH + t // (NQ // 2) + 1)
            for h in range(GROUP):
                mm = nc.tensor.matmul(p_d[HD * h:HD * (h + 1), :], ones[:], pair_sum[:, t % 2, h, :], start=(t % (NQ // 2) == 0), stop=(t % (NQ // 2) == NQ // 2 - 1), skip_group_check=True)
            mm.then_inc(key_sums, 1)

        def pe_group(pe, n, i, turn, ahead):
            pe.wait_ge(max_in[i], START + turn * 16 + 16)
            i1, turn1 = (i + 1) % RING, turn + (i + 1) // RING
            units = iter(range(UNITS if ahead else 0))
            def some(count):
                for _, u in zip(range(count), units):
                    max_unit(pe, n + 1, i1, turn1, u)
            for s in range(STEPS):
                left = PER_STEP[s]
                scores_pair(pe, n, i, s, 0)
                some(min(left, 1))
                scores_pair(pe, n, i, s, 1)
                some(min(left - 1, 1))
                products_o(pe, n, i, s - 1)
                some(min(left - 2, 2))
                if ahead and s == TURN_STEP:
                    turn_max(pe, n + 1)
                if s % 2 == 0:
                    sum_keys(pe, n, s)
                some(min(left - 4, 1))

        def take_raw(act, n, half):
            act.wait_ge(products, START + n * STEPS + (NQ + 1 if half == 0 else 1))
            act.wait_ge(o_ready[half], START + n - half)
            nc.scalar.copy(raw[:, half], p_o[:]).then_inc(raw_taken, 1)

        def take_den(act, n, half):
            act.wait_ge(key_sums, START + n * PAIRS + (LATER // 2 + NQ // 2 if half == 0 else LATER // 2))
            act.wait_ge(rden_ready[half], START + n)
            nc.scalar.copy(den[:, half], p_d[:]).then_inc(den_taken, 1)

        def act_group(act, n):
            for s in range(STEPS):
                for pair in range(2):
                    act.wait_ge(scores, START + n * (2 * STEPS) + 2 * s + pair + 1)
                    if pair == 0:
                        act.wait_ge(products, START + n * STEPS + max(s - 2, -1))
                        act.wait_ge(paired, START + n * PAIRS + s // 2 - 1)
                    nc.scalar.activation(probs[:, s % 4, 2 * pair:2 * pair + 2, :], p_exp[pair][:], ACT.Exp).then_inc(exps, 1)
                if s == 0:
                    take_raw(act, n, 1)
                if s == NQ:
                    take_raw(act, n, 0)
                if s - 1 in DEN_STEP:
                    take_den(act, n, DEN_STEP[s - 1])

        def dve_unit(dve, n, u):
            dve.wait_ge(unit_scores, START + n * UNITS + u + 1)
            if u == 0:
                dve.wait_ge(max_whole, START + n)
            nc.vector.tensor_reduce(out=half_max[:].rearrange("p r h -> p (r h)")[:, u:u + 1], in_=p_max[u % 2][:], axis=mybir.AxisListType.X, op=ALU.max).then_inc(unit_max, 1)

        def dve_row(dve, n, i, turn):
            dve.wait_ge(unit_max, START + n * UNITS + UNITS)
            dve.wait_ge(max_turned, START + n)
            nc.vector.tensor_reduce(out=row_max[:], in_=half_max[:], axis=mybir.AxisListType.X, op=ALU.max).then_inc(max_whole, 1)
            dve.wait_ge(max_turned, START + n + 1)
            dve.wait_ge(max_in[i], START + turn * 16)
            nc.vector.tensor_scalar(out=neg_row[i][:], in0=p_max[1][0:ROWS, 0:P], scalar1=-1.0, scalar2=None, op0=ALU.mult).then_inc(max_row, 1)

        def invert(dve, n, half, piece):
            w = HALFQ // PIECES
            if piece == 0:
                dve.wait_ge(den_taken, START + n * NH + (2 if half == 0 else 1))
                dve.wait_ge(o_ready[half], START + n - half)
            r = nc.vector.reciprocal(out=rden[:, half, piece * w:(piece + 1) * w], in_=den[:, half, piece * w:(piece + 1) * w])
            if piece == PIECES - 1:
                r.then_inc(rden_ready[half], 1)

        def dve_group(dve, n, i, turn, ahead):
            i1, turn1 = (i + 1) % RING, turn + (i + 1) // RING
            units = iter(range(UNITS if ahead else 0))
            for s in range(STEPS):
                for k, u in zip(range(PER_STEP[s]), units):
                    if k == 2 and s in INVERT:
                        invert(dve, n, *INVERT[s])
                    dve_unit(dve, n + 1, u)
                if s in INVERT and (not ahead or PER_STEP[s] <= 2):
                    invert(dve, n, *INVERT[s])
                if ahead and s == TURN_STEP:
                    dve_row(dve, n + 1, i1, turn1)

        def add_pair(pool, n, t):
            pool.wait_ge(exps, START + n * (2 * STEPS) + 4 * t + 4)
            pool.wait_ge(key_sums, START + n * PAIRS + t + 1)
            nc.gpsimd.tensor_tensor(out=pair_sum[:, t % 2], in0=probs[:, (2 * t) % 4], in1=probs[:, (2 * t + 1) % 4], op=ALU.add).then_inc(paired, 1)

        def divide(pool, n, half):
            pool.wait_ge(rden_ready[half], START + n + 1 + half)
            pool.wait_ge(raw_taken, START + n * NH + half + 2)
            pool.wait_ge(o_out[half], START + n * 16)
            nc.gpsimd.tensor_tensor(out=o[:, half, :], in0=raw[:, half], in1=rden[:, half], op=ALU.mult).then_inc(o_ready[half], 1)

        def store(sp, n, half):
            sp.wait_ge(o_ready[half], START + n + 1)
            sp.dma_start(OT[bass.ds(n, 1)].rearrange("o p s -> (o p) s")[:, half * HALFQ:(half + 1) * HALFQ], o[:, half, :]).then_inc(o_out[half], 16)

        def pool_group(pool, n, before):
            for t in range(PAIRS):
                add_pair(pool, n, t)
                if t == PAIRS // 2 and before is not None:
                    divide(pool, before, 1)
            divide(pool, n, 0)

        with nc.Block() as block:
            @block.sync
            def _(sp):
                start_counts(sp, sems)
                sp.dma_start(ident[:], I["ident"]).then_inc(consts, 16)
                for i in range(2):
                    load(sp, i, i)
                send_max(sp, 0, 0)
                sp.wait_ge(max_in[0], START + 16)
            @block.vector
            def _(dve):
                nc.vector.memset(ones[:], 1.0)
                nc.vector.memset(probs[:, 3], 0.0)
                nc.vector.memset(pair_sum[:], 0.0)
                nc.vector.memset(v[RING - 1][:, NQ - 1, :], 0.0)
                for i in range(RING):
                    nc.vector.memset(ks[i][KROWS:STACK].bitcast(f32), 1.0)
                nc.vector.memset(den[:, 1], 1.0).then_inc(cleared, 1)
                for u in range(UNITS):
                    dve_unit(dve, 0, u)
                dve_row(dve, 0, 0, 0)
            @block.tensor
            def _(pe):
                pe.wait_ge(consts, START + 16)
                for u in range(UNITS):
                    max_unit(pe, 0, 0, 0, u)
                turn_max(pe, 0)
                pe.wait_ge(cleared, START + 1)
                for bank in (p_o, p_d):
                    nc.tensor.matmul(bank[:], probs[:, 3, 0, 0:P], probs[:, 3, 0, :], start=True, stop=True)

        LOOPS = (NGROUPS - 2) // RING
        def groups(e, body, last=0):
            with e.Fori(0, LOOPS) as it:
                for i in range(RING):
                    body(it * RING + i, i, it, True)
            for n in range(LOOPS * RING, NGROUPS):
                body(n, n % RING, n // RING, n < NGROUPS - 1)

        with nc.Block() as block:
            @block.sync
            def _(sp):
                def body(n, i, turn, ahead, before, more):
                    if more:
                        sp.wait_ge(products, START + n * STEPS + 1)
                        load(sp, n + 2, (i + 2) % RING)
                    if before is not None:
                        store(sp, before, 1)
                    if ahead:
                        send_max(sp, n + 1, (i + 1) % RING)
                    store(sp, n, 0)
                for n in range(RING):
                    body(n, n, 0, True, n - 1 if n else None, True)
                with sp.Fori(1, LOOPS) as it:
                    for i in range(RING):
                        body(it * RING + i, i, it, True, it * RING + (i - 1), True)
                for n in range(LOOPS * RING, NGROUPS):
                    body(n, n % RING, n // RING, n < NGROUPS - 1, n - 1, n + 2 < NGROUPS)
                store(sp, NGROUPS - 1, 1)
                for half in range(NH):
                    sp.wait_ge(o_out[half], START + 16 * NGROUPS)
            @block.tensor
            def _(pe):
                groups(pe, lambda n, i, turn, ahead: pe_group(pe, n, i, turn, ahead))
                products_o(pe, NGROUPS, NGROUPS % RING, -1)
                for s in range(0, LATER, 2):
                    sum_keys(pe, NGROUPS, s)
            @block.scalar
            def _(act):
                with act.Fori(0, NGROUPS) as n:
                    act_group(act, n)
                take_raw(act, NGROUPS, 1)
                take_den(act, NGROUPS, 1)
            @block.vector
            def _(dve):
                groups(dve, lambda n, i, turn, ahead: dve_group(dve, n, i, turn, ahead))
                for piece in range(PIECES):
                    invert(dve, NGROUPS, 1, piece)
            @block.gpsimd
            def _(pool):
                pool_group(pool, 0, None)
                with pool.Fori(1, NGROUPS) as n:
                    pool_group(pool, n, n + (-1))
                divide(pool, NGROUPS - 1, 1)

def out_phase(nc, I, OT, X2, WDC, out):
    with ExitStack() as ctx:
        sb = lambda n, s, d=f32: ctx.enter_context(nc.sbuf_tensor("f_" + n, s, d))
        sems = []
        def sem(n):
            sems.append(ctx.enter_context(nc.semaphore("f_" + n)))
            return sems[-1]
        w = sb("w", [P, NK, MODEL]); wdc = sb("wdc", [P, BATCH, MODEL]); wb = sb("wb", [P, BATCH, NK, MODEL])
        ot = [sb(f"ot{i}", [P, NK, SEQ]) for i in range(3)]; x2 = sb("x2", [P, NQ, MODEL]); o = sb("o", [P, 4, MODEL])
        po = [ctx.enter_context(nc.psum_tensor(f"f_po{i}", [P, MODEL], f32)) for i in range(4)]
        consts = sem("consts"); coefs_in = sem("coefs_in"); b_in = [sem(f"b_in{i}") for i in range(3)]; x_in = [sem(f"x_in{i}") for i in range(NQ)]
        scaled_pool = sem("scaled_pool"); scaled_dve = sem("scaled_dve"); products = sem("products"); added = sem("added"); o_out = [sem(f"o_out{i}") for i in range(4)]
        TILES = BATCH * NQ

        def load_batch(sp, b):
            sp.dma_start(ot[b % 3][:], OT.rearrange("(b g) p s -> b p g s", b=BATCH)[b]).then_inc(b_in[b % 3], 16)
        def load_x2(sp, t):
            sp.dma_start(x2[:, t % NQ, :], X2[t // NQ, t % NQ * P:(t % NQ + 1) * P, :]).then_inc(x_in[t % NQ], 16)
        def scale_w(e, engine, b, k, done):
            engine.tensor_tensor(out=wb[:, b, k, :], in0=w[:, k, :], in1=wdc[:, b, :], op=ALU.mult).then_inc(done, 1)

        with nc.Block() as block:
            @block.sync
            def _(sp):
                start_counts(sp, sems)
                sp.dma_start(w[:], I["w_t"].rearrange("(k p) n -> p k n", p=P)).then_inc(consts, 16)
                for b in range(BATCH):
                    sp.dma_start(wdc[:, b, :], WDC[1, b:b + 1, :].to_broadcast([P, MODEL])).then_inc(coefs_in, 16)
                load_batch(sp, 0)
                for t in range(NQ):
                    load_x2(sp, t)
                for b in range(1, 3):
                    load_batch(sp, b)
                for t in range(TILES):
                    if t == NQ:
                        sp.wait_ge(products, START + NQ)
                        load_batch(sp, 3)
                    sp.wait_ge(added, START + t + 1)
                    sp.dma_start(out[t // NQ, t % NQ * P:(t % NQ + 1) * P, :], o[:, t % 4, :]).then_inc(o_out[t % 4], 16)
                    if t + NQ < TILES:
                        load_x2(sp, t + NQ)
                for i in range(4):
                    sp.wait_ge(o_out[i], START + 16 * TILES // 4)
            @block.gpsimd
            def _(pool):
                pool.wait_ge(consts, START + 16)
                pool.wait_ge(coefs_in, START + 16 * BATCH)
                for b in range(BATCH):
                    for k in (range(2, NK) if b == 0 else range(NK)):
                        scale_w(pool, nc.gpsimd, b, k, scaled_pool)
            @block.tensor
            def _(pe):
                for t in range(TILES):
                    b, q = divmod(t, NQ)
                    if q == 0:
                        pe.wait_ge(b_in[b % 3], START + 16 * (b // 3 + 1))
                    if t >= 4:
                        pe.wait_ge(added, START + t - 3)
                    for k in range(NK):
                        if q == 0:
                            if b == 0 and k < 2:
                                pe.wait_ge(scaled_dve, START + k + 1)
                            else:
                                pe.wait_ge(scaled_pool, START + b * NK + k - 1)
                        mm = nc.tensor.matmul(po[t % 4][:], ot[b % 3][:, k, q * P:(q + 1) * P], wb[:, b, k, :], start=(k == 0), stop=(k == NK - 1))
                    mm.then_inc(products, 1)
            @block.vector
            def _(dve):
                dve.wait_ge(consts, START + 16)
                dve.wait_ge(coefs_in, START + 16 * BATCH)
                for k in range(2):
                    scale_w(dve, nc.vector, 0, k, scaled_dve)
                for t in range(TILES):
                    dve.wait_ge(products, START + t + 1)
                    dve.wait_ge(x_in[t % NQ], START + 16 * (t // NQ + 1))
                    if t >= 4:
                        dve.wait_ge(o_out[t % 4], START + 16 * (t // 4))
                    nc.vector.tensor_tensor(out=o[:, t % 4, :], in0=x2[:, t % NQ, :], in1=po[t % 4][:], op=ALU.add).then_inc(added, 1)


def build(nc, I, out):
    def scratch(name, shape, dtype=f32):
        return nc.dram_tensor(name, shape, dtype, kind="Internal").ap()

    Xp = scratch("xn_parts", [3 * 2 * BATCH, SEQ * HALF], bf16)
    Xn = scratch("xn_full", [BATCH, SEQ, INNER])
    Bp = scratch("b_parts", [3, BATCH, SEQ, STATES], bf16)
    Ad = scratch("decays", [BATCH * STATES, SEQ])
    Cm = scratch("c_rows", [BATCH * STATES, SEQ])
    Y = scratch("scan_out", [SEQ, 2 * BATCH, HALF])
    SG = scratch("silu_gate", [NQ * BATCH, P, INNER])
    X1 = scratch("x1_tiles", [NQ * BATCH, P, MODEL])
    QK = scratch("qk_parts", [4, BATCH, MODEL, SEQ])
    V = scratch("v_groups", [BATCH * HEADS * HD // P, SEQ, P])
    X2 = scratch("x2_full", [BATCH, SEQ, MODEL])
    WDC = scratch("coefs", [3, BATCH, MODEL])
    OT = scratch("attended", [BATCH * HEADS * HD // P, P, SEQ])
    pre_semaphores = pre_phase(nc, I, Xp, Xn, Bp, Ad, Cm)
    scan_phase(nc, I, Xp, Xn, Bp, Ad, Cm, Y, SG, X1, pre_semaphores)
    proj_phase(nc, I, X1, QK, V, X2, WDC)
    attention_phase(nc, I, QK, V, OT)
    out_phase(nc, I, OT, X2, WDC, out)


def kernel(**inputs):
    import concourse.bacc as bacc
    from concourse.bass_utils import run_bass_kernel_spmd

    turned = lambda name: np.ascontiguousarray(np.asarray(inputs[name]).T)
    plain = lambda name: np.ascontiguousarray(inputs[name])
    mask_b = np.zeros((6 * 2 * BATCH, P), np.float32)
    for k in range(mask_b.shape[0]):
        r = k % (2 * BATCH)
        mask_b[k, r * STATES:(r + 1) * STATES] = 1
    mask_c = np.zeros((P, 16, 32), np.float32)
    for p in range(P):
        for t in range(16):
            mask_c[p, t, (t % 4) * 8 + p // STATES] = 1
    arrays = {
        "x": plain("x"), "x_t": np.ascontiguousarray(np.asarray(inputs["x"]).transpose(0, 2, 1)), "x_tiles": np.ascontiguousarray(np.asarray(inputs["x"]).reshape(BATCH, NQ, P, NK, P).transpose(1, 0, 4, 3, 2)).reshape(NQ * BATCH, P, NK, P),
        "t_emb": plain("cond_2048"),
        "w_in_t": turned("L0_cond_W_in"), "w_conv": plain("L0_cond_W_conv"), "b_conv": plain("L0_cond_b_conv"),
        "ln_g": plain("L0_cond_ln_g"), "ln_b": plain("L0_cond_ln_b"), "w_xproj_t": turned("L0_cond_W_xproj"),
        "w_dt_t": np.ascontiguousarray(np.pad(turned("L0_cond_W_dt"), ((0, 0), (0, 64 - STATES)))),
        "b_dt": plain("L0_cond_b_dt"), "a_log": plain("L0_cond_A_log"), "D": plain("L0_cond_D"), "w_out_t": turned("L0_cond_W_out"),
        "ident": np.eye(P, dtype=np.float32), "mask_b": mask_b, "mask_c": mask_c,
    }
    for j in "qkvwu":
        arrays[j + "_t"] = turned(f"L1_cond_{j}_weight")
    nc = bacc.Bacc("TRN2", target_bir_lowering=False, num_devices=1)
    I = {n: nc.dram_tensor(f"in_{n}_dram", a.shape, mybir.dt.from_np(a.dtype), kind="ExternalInput").ap() for n, a in arrays.items()}
    out = nc.dram_tensor("out_dram", (BATCH, SEQ, MODEL), f32, kind="ExternalOutput").ap()
    build(nc, I, out)
    r = run_bass_kernel_spmd(nc, [{f"in_{n}_dram": a for n, a in arrays.items()}], core_ids=[0])
    return r.results[0]["out_dram"]
```
